# Optimizing a Trainium2 kernel written in Bass

```python
import numpy as np
import jax
import jax.numpy as jnp

def _softmax(x, axis=-1):
    return jax.nn.softmax(x, axis=axis)

def _gelu(x):
    return jax.nn.gelu(x, approximate=True)

def _silu(x):
    return jax.nn.silu(x)

def _sigmoid(x):
    return jax.nn.sigmoid(x)

def _layernorm(x, axis=-1, eps=1e-05):
    m = jnp.mean(x, axis=axis, keepdims=True)
    v = jnp.var(x, axis=axis, keepdims=True)
    return (x - m) / jnp.sqrt(v + eps)

def _scatter_add(tgt, idx, src, axis=0):
    return tgt.at[idx].add(src)

def _segment_sum(src, seg, n):
    return jax.ops.segment_sum(src, seg, n)
kernel_name = 'mk_metaformer_d2_conv_nhwc256_r2_0e1d6f'

def setup_inputs(seed: int=0):
    np.random.seed(seed)
    _w = jnp.asarray

    def _rec_inputs():
        import jax
        import jax.numpy as jnp
        _gk = jax.random.key(seed)
        x = -0.0002928 + 1 * jax.random.normal(jax.random.fold_in(_gk, 1), (4, 32, 32, 128), jnp.float32)
        return x
    x = _rec_inputs()

    def _L0_conv_setup():
        import jax, jax.numpy as jnp
        import numpy as np
        import math
        B, H, W, CIN = (4, 32, 32, 128)
        G, C, K = (8, 32, 9)
        MAX_SCALE = 6.0

        def _dcn_sample(v, deform, weights):
            b_, h_, w_, g_, c_ = v.shape
            ww = jnp.arange(w_, dtype=v.dtype)[None, None, :, None, None]
            hh = jnp.arange(h_, dtype=v.dtype)[None, :, None, None, None]
            px = ww + deform[..., 0]
            py = hh + deform[..., 1]
            x0 = jnp.floor(px)
            y0 = jnp.floor(py)
            wx1 = px - x0
            wx0 = 1.0 - wx1
            wy1 = py - y0
            wy0 = 1.0 - wy1
            bidx = jnp.arange(b_)[:, None, None, None, None]
            gidx = jnp.arange(g_)[None, None, None, :, None]

            def gather(yi, xi):
                valid = ((yi >= 0) & (yi < h_) & (xi >= 0) & (xi < w_)).astype(v.dtype)
                yc = jnp.clip(yi, 0, h_ - 1).astype(jnp.int32)
                xc = jnp.clip(xi, 0, w_ - 1).astype(jnp.int32)
                return v[bidx, yc, xc, gidx] * valid[..., None]
            samp = gather(y0, x0) * (wy0 * wx0)[..., None] + gather(y0, x0 + 1) * (wy0 * wx1)[..., None] + gather(y0 + 1, x0) * (wy1 * wx0)[..., None] + gather(y0 + 1, x0 + 1) * (wy1 * wx1)[..., None]
            return jnp.einsum('bhwgkc,bhwgk->bhwgc', samp, weights)
        key = jax.random.key(seed)
        ks = jax.random.split(key, 10)
        s = 0.02
        x = jax.random.normal(ks[0], (B, H, W, CIN), dtype=jnp.float32)
        v_w = jax.random.normal(ks[1], (CIN, G * C), dtype=jnp.float32) * s
        v_b = jax.random.normal(ks[2], (G * C,), dtype=jnp.float32) * s
        qd_w = jax.random.normal(ks[3], (CIN, G * K * 2), dtype=jnp.float32) * s
        qd_b = jax.random.normal(ks[4], (G * K * 2,), dtype=jnp.float32) * s
        qs_w = jax.random.normal(ks[5], (CIN, G * K), dtype=jnp.float32) * s
        qw_w = jax.random.normal(ks[6], (CIN, G * K), dtype=jnp.float32) * s
        qw_b = jax.random.normal(ks[7], (G * K,), dtype=jnp.float32) * s
        out_w = jax.random.normal(ks[8], (G * C, CIN), dtype=jnp.float32) * s
        out_b = jax.random.normal(ks[9], (CIN,), dtype=jnp.float32) * s
        n = int(math.isqrt(K))
        d = np.linspace(-1.0, 1.0, n, dtype=np.float32)
        gx, gy = np.meshgrid(d, d, indexing='xy')
        prior = jnp.asarray(np.stack([gx, gy], axis=-1).reshape(1, 1, 1, 1, K, 2))
        sc = np.array([(i + 1) / G - 0.0001 for i in range(G)], dtype=np.float32)
        dscale = jnp.asarray(np.log(sc / (1.0 - sc)).reshape(1, 1, 1, G, 1, 1))
        return dict(x=x, v_w=v_w, v_b=v_b, qd_w=qd_w, qd_b=qd_b, qs_w=qs_w, qw_w=qw_w, qw_b=qw_b, out_w=out_w, out_b=out_b, prior=prior, dscale=dscale)
    _L0_conv_all = _L0_conv_setup()
    _L0_conv_in = {k: v for k, v in _L0_conv_all.items() if k in ('v_w', 'v_b', 'qd_w', 'qd_b', 'qs_w', 'qw_w', 'qw_b', 'out_w', 'out_b', 'prior', 'dscale')}
    del _L0_conv_all

    def _L0_ffn_setup():
        import math
        import jax, jax.numpy as jnp
        import numpy as np
        CAPACITY_FACTOR = 1.25
        key = jax.random.key(seed)
        ks = jax.random.split(key, 5)
        B, L, D, F, E = (8, 4096, 128, 512, 8)
        h = jax.random.normal(ks[0], (B, L, D), dtype=jnp.float32)
        gate_w = jax.random.normal(ks[1], (D, E), dtype=jnp.float32) * 0.02
        gate_b = jnp.zeros((E,), dtype=jnp.float32)
        w1 = jax.random.normal(ks[2], (E, D, F), dtype=jnp.float32) * (1.0 / math.sqrt(D))
        b1 = jnp.zeros((E, F), dtype=jnp.float32)
        w2 = jax.random.normal(ks[3], (E, F, D), dtype=jnp.float32) * (1.0 / math.sqrt(F))
        b2 = jnp.zeros((E, D), dtype=jnp.float32)
        return {'h': h, 'gate_w': gate_w, 'gate_b': gate_b, 'w1': w1, 'b1': b1, 'w2': w2, 'b2': b2}
    _L0_ffn_all = _L0_ffn_setup()
    _L0_ffn_in = {k: v for k, v in _L0_ffn_all.items() if k in ('gate_w', 'gate_b', 'w1', 'b1', 'w2', 'b2')}
    del _L0_ffn_all

    def _L1_conv_setup():
        import jax, jax.numpy as jnp
        import numpy as np
        DIM = 128
        NUM_HEADS = 8
        HEAD_DIM = DIM // NUM_HEADS
        K = 7
        key = jax.random.key(seed)
        ks = jax.random.split(key, 6)
        B, H, W, C = (2, 56, 56, DIM)
        x = jax.random.normal(ks[0], (B, H, W, C), dtype=jnp.float32)
        s = 1.0 / np.sqrt(C)
        Wqkv = jax.random.normal(ks[1], (C, 3 * C), dtype=jnp.float32) * s
        bqkv = jnp.zeros((3 * C,), dtype=jnp.float32)
        rpb = jnp.clip(jax.random.normal(ks[2], (NUM_HEADS, 2 * K - 1, 2 * K - 1), dtype=jnp.float32) * 0.02, -2.0, 2.0)
        Wproj = jax.random.normal(ks[3], (C, C), dtype=jnp.float32) * s
        bproj = jnp.zeros((C,), dtype=jnp.float32)
        return {'x': x, 'Wqkv': Wqkv, 'bqkv': bqkv, 'rpb': rpb, 'Wproj': Wproj, 'bproj': bproj}
    _L1_conv_all = _L1_conv_setup()
    _L1_conv_in = {k: v for k, v in _L1_conv_all.items() if k in ('Wqkv', 'bqkv', 'rpb', 'Wproj', 'bproj')}
    del _L1_conv_all

    def _L1_ffn_setup():
        import math
        import jax, jax.numpy as jnp
        import numpy as np
        CAPACITY_FACTOR = 1.25
        key = jax.random.key(seed)
        ks = jax.random.split(key, 5)
        B, L, D, F, E = (8, 4096, 128, 512, 8)
        h = jax.random.normal(ks[0], (B, L, D), dtype=jnp.float32)
        gate_w = jax.random.normal(ks[1], (D, E), dtype=jnp.float32) * 0.02
        gate_b = jnp.zeros((E,), dtype=jnp.float32)
        w1 = jax.random.normal(ks[2], (E, D, F), dtype=jnp.float32) * (1.0 / math.sqrt(D))
        b1 = jnp.zeros((E, F), dtype=jnp.float32)
        w2 = jax.random.normal(ks[3], (E, F, D), dtype=jnp.float32) * (1.0 / math.sqrt(F))
        b2 = jnp.zeros((E, D), dtype=jnp.float32)
        return {'h': h, 'gate_w': gate_w, 'gate_b': gate_b, 'w1': w1, 'b1': b1, 'w2': w2, 'b2': b2}
    _L1_ffn_all = _L1_ffn_setup()
    _L1_ffn_in = {k: v for k, v in _L1_ffn_all.items() if k in ('gate_w', 'gate_b', 'w1', 'b1', 'w2', 'b2')}
    del _L1_ffn_all
    return {'x': x, 'L0_conv_v_w': _L0_conv_in['v_w'], 'L0_conv_v_b': _L0_conv_in['v_b'], 'L0_conv_qd_w': _L0_conv_in['qd_w'], 'L0_conv_qd_b': _L0_conv_in['qd_b'], 'L0_conv_qs_w': _L0_conv_in['qs_w'], 'L0_conv_qw_w': _L0_conv_in['qw_w'], 'L0_conv_qw_b': _L0_conv_in['qw_b'], 'L0_conv_out_w': _L0_conv_in['out_w'], 'L0_conv_out_b': _L0_conv_in['out_b'], 'L0_conv_prior': _L0_conv_in['prior'], 'L0_conv_dscale': _L0_conv_in['dscale'], 'L0_ffn_gate_w': _L0_ffn_in['gate_w'], 'L0_ffn_gate_b': _L0_ffn_in['gate_b'], 'L0_ffn_w1': _L0_ffn_in['w1'], 'L0_ffn_b1': _L0_ffn_in['b1'], 'L0_ffn_w2': _L0_ffn_in['w2'], 'L0_ffn_b2': _L0_ffn_in['b2'], 'L1_conv_Wqkv': _L1_conv_in['Wqkv'], 'L1_conv_bqkv': _L1_conv_in['bqkv'], 'L1_conv_rpb': _L1_conv_in['rpb'], 'L1_conv_Wproj': _L1_conv_in['Wproj'], 'L1_conv_bproj': _L1_conv_in['bproj'], 'L1_ffn_gate_w': _L1_ffn_in['gate_w'], 'L1_ffn_gate_b': _L1_ffn_in['gate_b'], 'L1_ffn_w1': _L1_ffn_in['w1'], 'L1_ffn_b1': _L1_ffn_in['b1'], 'L1_ffn_w2': _L1_ffn_in['w2'], 'L1_ffn_b2': _L1_ffn_in['b2']}

def reference(x, L0_conv_v_w, L0_conv_v_b, L0_conv_qd_w, L0_conv_qd_b, L0_conv_qs_w, L0_conv_qw_w, L0_conv_qw_b, L0_conv_out_w, L0_conv_out_b, L0_conv_prior, L0_conv_dscale, L0_ffn_gate_w, L0_ffn_gate_b, L0_ffn_w1, L0_ffn_b1, L0_ffn_w2, L0_ffn_b2, L1_conv_Wqkv, L1_conv_bqkv, L1_conv_rpb, L1_conv_Wproj, L1_conv_bproj, L1_ffn_gate_w, L1_ffn_gate_b, L1_ffn_w1, L1_ffn_b1, L1_ffn_w2, L1_ffn_b2):
    import jax
    import jax.numpy as jnp

    def _L0_conv_ref(x, v_w, v_b, qd_w, qd_b, qs_w, qw_w, qw_b, out_w, out_b, prior, dscale):
        import jax, jax.numpy as jnp
        import numpy as np
        import math
        B, H, W, CIN = (4, 32, 32, 128)
        G, C, K = (8, 32, 9)
        MAX_SCALE = 6.0

        def _dcn_sample(v, deform, weights):
            b_, h_, w_, g_, c_ = v.shape
            ww = jnp.arange(w_, dtype=v.dtype)[None, None, :, None, None]
            hh = jnp.arange(h_, dtype=v.dtype)[None, :, None, None, None]
            px = ww + deform[..., 0]
            py = hh + deform[..., 1]
            x0 = jnp.floor(px)
            y0 = jnp.floor(py)
            wx1 = px - x0
            wx0 = 1.0 - wx1
            wy1 = py - y0
            wy0 = 1.0 - wy1
            bidx = jnp.arange(b_)[:, None, None, None, None]
            gidx = jnp.arange(g_)[None, None, None, :, None]

            def gather(yi, xi):
                valid = ((yi >= 0) & (yi < h_) & (xi >= 0) & (xi < w_)).astype(v.dtype)
                yc = jnp.clip(yi, 0, h_ - 1).astype(jnp.int32)
                xc = jnp.clip(xi, 0, w_ - 1).astype(jnp.int32)
                return v[bidx, yc, xc, gidx] * valid[..., None]
            samp = gather(y0, x0) * (wy0 * wx0)[..., None] + gather(y0, x0 + 1) * (wy0 * wx1)[..., None] + gather(y0 + 1, x0) * (wy1 * wx0)[..., None] + gather(y0 + 1, x0 + 1) * (wy1 * wx1)[..., None]
            return jnp.einsum('bhwgkc,bhwgk->bhwgc', samp, weights)
        b_, h_, w_, _ = x.shape
        v = (x @ v_w + v_b).reshape(b_, h_, w_, G, C)
        deform = (x @ qd_w + qd_b).reshape(b_, h_, w_, G, K, 2)
        scale = (x @ qs_w).reshape(b_, h_, w_, G, K, 1) + dscale
        deform = (deform + prior) * jax.nn.sigmoid(scale) * MAX_SCALE
        weights = (x @ qw_w + qw_b).reshape(b_, h_, w_, G, K)
        out = _dcn_sample(v, deform, weights)
        out = out.reshape(b_, h_, w_, G * C)
        return out @ out_w + out_b

    def _L0_ffn_ref(h, gate_w, gate_b, w1, b1, w2, b2):
        import math
        import jax, jax.numpy as jnp
        import numpy as np
        CAPACITY_FACTOR = 1.25
        B, L, D = h.shape
        E = gate_w.shape[1]
        T = B * L
        C = max(1, math.ceil(CAPACITY_FACTOR * T / E))
        x = h.reshape(T, D)
        logits = x @ gate_w + gate_b
        probs = jax.nn.softmax(logits, axis=-1)
        idx = jnp.argmax(probs, axis=-1)
        prb = jnp.take_along_axis(probs, idx[:, None], axis=1)[:, 0]
        one_hot = jax.nn.one_hot(idx, E, dtype=jnp.float32)
        pos = (jnp.cumsum(one_hot, axis=0) * one_hot).sum(-1).astype(jnp.int32) - 1
        kept = pos < C
        pos_safe = jnp.where(kept, pos, C)
        buf = jnp.zeros((E, C, D), dtype=h.dtype).at[idx, pos_safe].set(x, mode='drop')
        hmid = jax.nn.relu(jnp.einsum('ecd,edf->ecf', buf, w1) + b1[:, None, :])
        ybuf = jnp.einsum('ecf,efd->ecd', hmid, w2) + b2[:, None, :]
        pos_g = jnp.minimum(pos, C - 1)
        y_tok = ybuf[idx, pos_g] * (prb * kept)[:, None]
        y = y_tok.reshape(B, L, D)
        y = jnp.nan_to_num(y, nan=0.0, posinf=10000.0, neginf=-10000.0)
        return y

    def _L1_conv_ref(x, Wqkv, bqkv, rpb, Wproj, bproj):
        import jax, jax.numpy as jnp
        import numpy as np
        DIM = 128
        NUM_HEADS = 8
        HEAD_DIM = DIM // NUM_HEADS
        K = 7
        B, H, W, C = x.shape
        NH, D = (NUM_HEADS, HEAD_DIM)
        scale = D ** (-0.5)
        qkv = (x @ Wqkv + bqkv).reshape(B, H, W, 3, NH, D)
        qkv = qkv.transpose(3, 0, 4, 1, 2, 5)
        q, k, v = (qkv[0] * scale, qkv[1], qkv[2])
        start_h = jnp.clip(jnp.arange(H) - K // 2, 0, H - K)
        start_w = jnp.clip(jnp.arange(W) - K // 2, 0, W - K)
        idx_h = start_h[:, None] + jnp.arange(K)
        idx_w = start_w[:, None] + jnp.arange(K)
        k_nb = k[:, :, idx_h][:, :, :, :, idx_w]
        v_nb = v[:, :, idx_h][:, :, :, :, idx_w]
        attn = jnp.einsum('bnijd,bniajcd->bnijac', q, k_nb)
        rel_h = idx_h - jnp.arange(H)[:, None] + (K - 1)
        rel_w = idx_w - jnp.arange(W)[:, None] + (K - 1)
        bias = rpb[:, rel_h][:, :, :, rel_w]
        bias = bias.transpose(0, 1, 3, 2, 4)
        attn = attn + bias[None]
        attn = jax.nn.softmax(attn.reshape(B, NH, H, W, K * K), axis=-1)
        attn = attn.reshape(B, NH, H, W, K, K)
        out = jnp.einsum('bnijac,bniajcd->bnijd', attn, v_nb)
        out = out.transpose(0, 2, 3, 1, 4).reshape(B, H, W, C)
        return out @ Wproj + bproj

    def _L1_ffn_ref(h, gate_w, gate_b, w1, b1, w2, b2):
        import math
        import jax, jax.numpy as jnp
        import numpy as np
        CAPACITY_FACTOR = 1.25
        B, L, D = h.shape
        E = gate_w.shape[1]
        T = B * L
        C = max(1, math.ceil(CAPACITY_FACTOR * T / E))
        x = h.reshape(T, D)
        logits = x @ gate_w + gate_b
        probs = jax.nn.softmax(logits, axis=-1)
        idx = jnp.argmax(probs, axis=-1)
        prb = jnp.take_along_axis(probs, idx[:, None], axis=1)[:, 0]
        one_hot = jax.nn.one_hot(idx, E, dtype=jnp.float32)
        pos = (jnp.cumsum(one_hot, axis=0) * one_hot).sum(-1).astype(jnp.int32) - 1
        kept = pos < C
        pos_safe = jnp.where(kept, pos, C)
        buf = jnp.zeros((E, C, D), dtype=h.dtype).at[idx, pos_safe].set(x, mode='drop')
        hmid = jax.nn.relu(jnp.einsum('ecd,edf->ecf', buf, w1) + b1[:, None, :])
        ybuf = jnp.einsum('ecf,efd->ecd', hmid, w2) + b2[:, None, :]
        pos_g = jnp.minimum(pos, C - 1)
        y_tok = ybuf[idx, pos_g] * (prb * kept)[:, None]
        y = y_tok.reshape(B, L, D)
        y = jnp.nan_to_num(y, nan=0.0, posinf=10000.0, neginf=-10000.0)
        return y

    def _gn(v, G=32, eps=1e-05):
        B_, H_, W_, C_ = v.shape
        g = v.reshape(B_, H_, W_, G, C_ // G)
        m = jnp.mean(g, axis=(1, 2, 4), keepdims=True)
        s = jnp.var(g, axis=(1, 2, 4), keepdims=True)
        return ((g - m) / jnp.sqrt(s + eps)).reshape(v.shape)

    def _ln_c(v, eps=1e-06):
        m = jnp.mean(v, axis=-1, keepdims=True)
        s = jnp.var(v, axis=-1, keepdims=True)
        return (v - m) / jnp.sqrt(s + eps)

    def _ln_t(v, eps=1e-05):
        m = jnp.mean(v, axis=-1, keepdims=True)
        s = jnp.var(v, axis=-1, keepdims=True)
        return (v - m) / jnp.sqrt(s + eps)

    def _to_tokens(v):
        B_, H_, W_, C_ = v.shape
        return v.reshape(B_, H_ * W_, C_)

    def _from_tokens(t, like):
        return t.reshape(like.shape)
    x = x + _L0_conv_ref(_ln_c(x), L0_conv_v_w, L0_conv_v_b, L0_conv_qd_w, L0_conv_qd_b, L0_conv_qs_w, L0_conv_qw_w, L0_conv_qw_b, L0_conv_out_w, L0_conv_out_b, L0_conv_prior, L0_conv_dscale)
    t = _to_tokens(x)
    t = t + _L0_ffn_ref(_ln_t(t), L0_ffn_gate_w, L0_ffn_gate_b, L0_ffn_w1, L0_ffn_b1, L0_ffn_w2, L0_ffn_b2)
    x = _from_tokens(t, x)
    x = x + _L1_conv_ref(_ln_c(x), L1_conv_Wqkv, L1_conv_bqkv, L1_conv_rpb, L1_conv_Wproj, L1_conv_bproj)
    t = _to_tokens(x)
    t = t + _L1_ffn_ref(_ln_t(t), L1_ffn_gate_w, L1_ffn_gate_b, L1_ffn_w1, L1_ffn_b1, L1_ffn_w2, L1_ffn_b2)
    x = _from_tokens(t, x)
    return x

_drawn_inputs = setup_inputs


def setup_inputs(seed=0):
    import zlib

    import numpy as np

    out = dict(_drawn_inputs(seed))
    spreads = {'L0_ffn_gate_b': (0.0, 0.1),
     'L0_ffn_b1': (0.0, 0.435),
     'L0_ffn_b2': (0.0, 0.325),
     'L1_conv_bqkv': (0.0, 0.1),
     'L1_conv_bproj': (0.0, 0.1),
     'L1_ffn_gate_b': (0.0, 0.1),
     'L1_ffn_b1': (0.0, 0.695),
     'L1_ffn_b2': (0.0, 0.481)}
    factors = {'L0_conv_v_b': 5.794, 'L0_conv_qd_b': 3.908, 'L0_conv_qw_b': 5.908, 'L1_conv_rpb': 6.829}
    for name, (base, spread) in spreads.items():
        noise = np.random.default_rng([zlib.crc32(name.encode()), seed]).standard_normal(out[name].shape)
        drawn = base * np.exp(spread * noise) if base else spread * noise
        out[name] = jnp.asarray(drawn.astype(out[name].dtype))
    for name, factor in factors.items():
        out[name] = (out[name] * factor).astype(out[name].dtype)
    return out
```

```python
from contextlib import ExitStack

import numpy as np

import concourse.bass as bass
from concourse import mybir

ALU = mybir.AluOpType
ACT = mybir.ActivationFunctionType
AX = mybir.AxisListType
F32 = mybir.dt.float32
I32 = mybir.dt.int32
U32 = mybir.dt.uint32

P = 128
B, H, W, D = 4, 32, 32, 128
TILE_ROWS = P // W
TB = H // TILE_ROWS
NT = B * TB
G, C, K = 8, 32, 9
GK = G * K
CORNERS = 4
NQ = 4
QJ = GK // NQ
QG = G // NQ
PATCH = CORNERS * C
PADM = W + 1
PATCHES = H * W + PADM
MAX_SCALE = 6.0
CORNER_AT = [0, 1, W, W + 1]
VW, OFFW = G * C, GK * 4
E, F = 8, 512
FC = F // P
CAPACITY = -(-5 * B * H * W // (4 * E))
BIGGEST = float(np.finfo(np.float32).max)
NH, HD, WIN = 8, 16, 7
BLK = 4
NB = W // BLK
KW = BLK + WIN - 1
KK = KW * KW
HALO = WIN // 2
PH = H + 2 * HALO
RING = 2
QRING = 4
LEAD = 12
RRING = 16


PREPARE = ("stats", "norm", "turn", "values", "offsets", "places", "corners")


class Steps:

    def __init__(self, sem, names):
        self.sem, self.names, self.at = sem, names.split(), 0

    def begin(self, eng):
        eng.sem_inc(self.sem, 2 * len(self.names))

    def step(self, name):
        assert self.names[self.at] == name, (self.names[self.at], name)
        self.at = (self.at + 1) % len(self.names)
        return self.sem, 1

    def done(self, name, turn):
        return self.sem, turn * len(self.names) + (2 * len(self.names) + self.names.index(name) + 1)

    def all(self, turn):
        return self.done(self.names[-1], turn)


class Landed:

    def __init__(self, sem, dmas=1, ahead=1):
        self.sem, self.dmas, self.ahead = sem, dmas, ahead

    def begin(self, eng):
        eng.sem_inc(self.sem, 16 * self.dmas)

    def one(self):
        return self.sem, 16

    def through(self, turn):
        return self.sem, turn * (16 * self.dmas) + (1 + self.ahead) * 16 * self.dmas


def build(nc, x, v_w, v_b, qd_w, qd_b, qs_w, qw_w, qw_b, out_w, out_b, prior, dscale,
          moe_weights, Wqkv, bqkv, rpb, Wproj, bproj,
          c_ident, c_tri, c_pos, c_base, c_heads, c_dec, c_mask, out):
    ctx = ExitStack()
    with ctx:
        def sb(name, shape, dt=F32):
            return ctx.enter_context(nc.sbuf_tensor(name, shape, dt))

        def sem(name):
            return ctx.enter_context(nc.semaphore(name))

        def bank(name):
            return ctx.enter_context(nc.psum_tensor(name, [P, 512], F32))

        patches = nc.dram_tensor("patches", (B * G * PATCHES, PATCH), F32, kind="Internal").ap()
        weights = nc.dram_tensor("weights", (NT * P, GK * CORNERS), F32, kind="Internal").ap()
        vpad = nc.dram_tensor("vpad", (B * PH, PH, D), F32, kind="Internal").ap()

        X = sb("X", [P, NT, D])
        ident = sb("ident", [P, P])
        tri = sb("tri", [P, P])
        ones = sb("ones", [P, P])
        pos = sb("pos", [P, NT, 2])
        base = sb("base", [P, NT, G])
        heads = sb("heads", [P, NH])
        dec = sb("dec", [P, E])

        wv = sb("wv", [D, VW])
        wo = sb("wo", [D, OFFW])
        vb = sb("vb", [P, VW])
        ob = sb("ob", [P, OFFW])
        pr = sb("pr", [P, K * 2])
        ow = sb("ow", [P, 2, D])
        rows = sb("rows", [1, 2, D])
        w1 = [sb(f"w1_{n}", [D, E, F]) for n in range(2)]
        w2 = [sb(f"w2_{n}", [P, E * FC, D]) for n in range(2)]
        b1 = [sb(f"b1_{n}", [P, E * FC]) for n in range(2)]
        b2 = [sb(f"b2_{n}", [E, D]) for n in range(2)]
        gw = [sb(f"gw_{n}", [D, E]) for n in range(2)]
        gb = [sb(f"gb_{n}", [P, E]) for n in range(2)]
        taken = [sb(f"taken_{n}", [P, E]) for n in range(2)]
        wqkv = sb("wqkv", [D, 3 * D])
        bq = sb("bq", [P, 2])
        bv = sb("bv", [P, D])
        wp = sb("wp", [P, NH, D])
        bias = sb("bias", [P, 3, 3, KK])

        rank = sb("rank", [P, RRING, GK], U32)
        st_p, mv_p, sd_p, rs_p = sb("st_p", [P, 6]), sb("mv_p", [P, 2]), sb("sd_p", [P, 2]), sb("rs_p", [P, 1])
        got = sb("got", [P, NQ, QJ * PATCH])
        ranks = sb("ranks", [P, NQ, QJ], U32)
        wbuf = sb("wbuf", [P, GK * CORNERS])
        summed = sb("summed", [P, VW])
        summed_T = sb("summed_T", [P, 2, P])
        st_m, mv_m, sd_m, rs_m = sb("st_m", [P, 6]), sb("mv_m", [P, 2]), sb("sd_m", [P, 2]), sb("rs_m", [P, 1])
        st_q, mv_q, sd_q, rs_q = sb("st_q", [P, 6]), sb("mv_q", [P, 2]), sb("sd_q", [P, 2]), sb("rs_q", [P, 1])
        xn_q, xt_q = sb("xn_q", [P, D]), sb("xt_q", [D, P])
        xn_m = [sb(f"xn_m{n}", [P, D]) for n in range(2)]
        xt_m = [sb(f"xt_m{n}", [D, P]) for n in range(2)]
        route_b = [sb(f"route{n}", [P, 7, E]) for n in range(2)]
        small = [sb(f"small{n}", [P, 6]) for n in range(2)]
        gate_T = [sb(f"gate_T{n}", [E, P]) for n in range(2)]
        share = [sb(f"share{n}", [P, D]) for n in range(2)]
        hid = sb("hid", [P, 2, FC, P])
        acc = sb("acc", [P, D])
        fin = sb("fin", [P, 4, D])
        QT = sb("QT", [P, QRING, NB, BLK * BLK])
        KT = sb("KT", [P, RING * PH, PH])
        vt = sb("vt", [P, D])
        soft = sb("soft", [P, 4, NB])
        qbd = sb("qbd", [P, NB, NH, BLK * BLK])[:, :, :, :]
        PT = sb("PT", [P, NB, P])[:, :, :]
        OT = sb("OT", [P, NH, P])[:, :, :]
        vwin = sb("vwin", [P, NB, D])[:, :, :]
        prob = sb("prob", [P, NB, KK])[:, :, :]
        arena = sb("arena", [P, 2 * D + VW + OFFW + 23 * GK])
        cut = [0]

        def part(n):
            cut[0] += n
            return arena[:, cut[0] - n:cut[0]]

        xn_p, xt_p = part(D), part(P)
        vsb, osb = part(VW), part(OFFW)
        sg = part(GK)
        pp, fl, fr, fr0, tmp = (part(2 * GK) for _ in range(5))
        pint = part(2 * GK).bitcast(I32)
        wlin = part(4 * GK)
        wyw = part(2 * GK)
        wq = part(4 * GK)
        zeros = got[:, 0, 0:PATCHES]

        Z = [bank("Z0"), bank("Z1")]
        Y = [bank("Y0"), bank("Y1")]
        M = bank("M")
        N = [bank("N0"), bank("N1")]
        CV = bank("CV")
        RB = [CV, M]

        x_in = sem("x_in")
        const_in = sem("const_in")
        rpb_in = sem("rpb_in")
        zeros_out = sem("zeros_out")
        cleared = sem("cleared")
        zeros_set = sem("zeros_set")
        values_out = Landed(sem("values_out"), CORNERS)
        weights_out = Landed(sem("weights_out"))
        weights_in = Landed(sem("weights_in"))
        v_out = Landed(sem("v_out"), TILE_ROWS)
        v_in = Landed(sem("v_in"), KW)
        y_out = Landed(sem("y_out"))
        got_q = [Landed(sem(f"got_{q}"), QJ, ahead=0) for q in range(NQ)]
        setup = sem("setup")

        prep_v = Steps(sem("prep_v"), "stats aggr eps rstd xn vals offs e1 sig off pos clamp int flt "
                       "above floor frac frac0 a0 in0 w0 a1 in1 w1 wy wq flc lin rank")
        prep_s = Steps(sem("prep_s"), "std xT exp")
        prep_t = Steps(sem("prep_t"), "xT vals offs")
        gath_g = Steps(sem("gath_g"), "c0 c1 c2 c3")
        conv_v = Steps(sem("conv_v"), "m0 r0 m1 r1 m2 r2 m3 r3 add")
        conv_t = Steps(sem("conv_t"), "T proj")
        conv_s = Steps(sem("conv_s"), "T")
        route_v = [Steps(sem(f"route{n}_v"), "stats aggr eps rstd xn lg max neg eqd first hot rsum pos taken "
                         "kept gate") for n in range(2)]
        route_s = [Steps(sem(f"route{n}_s"), "std xT exp gT b2") for n in range(2)]
        route_t = [Steps(sem(f"route{n}_t"), "xT lg cum gT b2") for n in range(2)]
        exp_v = Steps(sem("exp_v"), "a0 a1 a2 a3 a4 a5 a6 a7 le fin clip fpart hi sign x1 x2")
        exp_s = Steps(sem("exp_s"), "h0 h1 h2 h3 h4 h5 h6 h7")
        exp_t = Steps(sem("exp_t"), "z0 z1 y0 z2 y1 z3 y2 z4 y3 z5 y4 z6 y5 z7 y6 y7")
        qkv_v = Steps(sem("qkv_v"), "stats aggr eps rstd xn q k v")
        qkv_s = Steps(sem("qkv_s"), "std xT")
        qkv_t = Steps(sem("qkv_t"), "xT qkv")
        att_v = Steps(sem("att_v"), "qbd s0 s1 max neg rsum norm o1 add")
        att_s = Steps(sem("att_s"), "exp p0 p1 o0")
        att_t = Steps(sem("att_t"), "s0 s1 p0 p1 o proj")

        passed = sem("passed")

        block = ctx.enter_context(nc.Block())

        def slots(eng, conv, route, experts, close, qkv, attend, prepare):

            def slot(i, u1, u0, u0_before, ends, qk, att, e1, cv=True, prep=True, apart=0):
                last = NT - 1
                after = last if isinstance(i, int) and i - 2 > last else i - 2

                def beside_second(e):
                    if e == 0:
                        if qk:
                            close(u0_before, 0, i - 2)
                        if e1:
                            route("gate", 1, i - 4)
                        if ends:
                            conv("turn", i - 1, i - 1 + LEAD if prep else last)
                    if e == 1:
                        if ends:
                            conv("project", i - 1)
                            route("stats", 0, i - 1)
                        if e1:
                            route("gate_T", 1, i - 4)
                    if e == 2:
                        if qk:
                            qkv("stats", i - 2, u0_before)
                        if ends:
                            route("norm", 0, i - 1)
                        if e1:
                            route("share", 1, i - 4)
                    if e == 3:
                        if ends:
                            route("turn", 0, i - 1, u0_before)
                        if qk:
                            qkv("norm", i - 2)
                        if prep:
                            prepare("stats", i + LEAD)
                    if e == 4:
                        if ends:
                            route("logits", 0, i - 1, u0_before)
                        if qk:
                            qkv("turn", i - 2)
                        if prep:
                            prepare("norm", i + LEAD)
                    if e == 5:
                        if ends:
                            route("gate", 0, i - 1)
                        if qk:
                            qkv("project", i - 2)
                    if e == 6:
                        if ends:
                            route("gate_T", 0, i - 1)
                        if cv:
                            conv(0, i)
                    if e == 7:
                        if ends:
                            route("share", 0, i - 1)

                def beside_first(e):
                    if e == 0:
                        if e1 and not apart:
                            close(u1, 1, i - 4)
                        if att:
                            attend("queries", i - 3, after)
                        if prep:
                            prepare("turn", i + LEAD, i - 1 if ends else None)
                    if e == 1:
                        if att:
                            attend("scores", i - 3)
                        if cv:
                            conv(1, i)
                        if prep:
                            prepare("values", i + LEAD)
                    if e == 2:
                        if att:
                            attend("weights", i - 3)
                        if prep:
                            prepare("offsets", i + LEAD)
                    if e == 3:
                        if att:
                            attend("turn", i - 3)
                        if cv:
                            conv(2, i)
                    if e == 4:
                        if att:
                            attend("values", i - 3)
                    if e == 5:
                        if att:
                            attend("project", i - 3)
                            route("stats", 1, i - 3)
                        if prep:
                            prepare("places", i + LEAD)
                    if e == 6:
                        if att:
                            route("norm", 1, i - 3)
                        if prep:
                            prepare("corners", i + LEAD)
                        if att:
                            route("turn", 1, i - 3, u1, after)
                    if e == 7:
                        if att:
                            route("logits", 1, i - 3, u1)
                        if cv:
                            conv(3, i)

                if apart:
                    def beside(e):
                        beside_second(e)
                        if e >= apart - 1:
                            beside_first(e - (apart - 1))

                    experts(u1, 1, i - 4, beside)
                    for e in range(E - (apart - 1), E):
                        beside_first(e)
                    close(u1, 1, i - 4)
                    return
                if e1:
                    experts(u1, 1, i - 4, beside_second)
                else:
                    for e in range(E):
                        beside_second(e)
                if ends:
                    experts(u0, 0, i - 1, beside_first)
                else:
                    for e in range(E):
                        beside_first(e)

            for i in range(4):
                slot(i, 1, i - 1, i - 2, ends=i > 0, qk=i > 1, att=i > 2, e1=False)
            with eng.Fori(4, NT - LEAD) as i:
                slot(i, i * 2 - 5, i * 2 - 4, i * 2 - 6, True, True, True, True)
            with eng.Fori(NT - LEAD, NT) as i:
                slot(i, i * 2 - 5, i * 2 - 4, i * 2 - 6, True, True, True, True, prep=False)
            u = 2 * NT - 5
            slot(NT, u, u + 1, u - 1, True, True, True, True, cv=False, prep=False)
            slot(NT + 1, u + 2, None, u + 1, False, True, True, True, cv=False, prep=False, apart=7)
            slot(NT + 2, u + 3, None, None, False, False, True, True, cv=False, prep=False, apart=1)
            slot(NT + 3, u + 4, None, None, False, False, False, True, cv=False, prep=False, apart=8)

        CONSTS = 0

        @block.sync
        def _(sp):
            nonlocal CONSTS
            for landed in (values_out, weights_out, weights_in, v_out, v_in, y_out):
                landed.begin(sp)
            sp.sem_inc(cleared, 16)
            xv = x.rearrange("b h w d -> (b h w) d").rearrange("(t p) d -> p t d", p=P)
            sp.dma_start(X[:, :, :], xv).then_inc(x_in, 16)
            loads = [
                (ident[:, :], c_ident), (wv[:, :], v_w),
                (wo[:, 0:2 * GK], qd_w), (wo[:, 2 * GK:3 * GK], qs_w), (wo[:, 3 * GK:], qw_w),
                (vb[:, :], v_b.partition_broadcast(P)),
                (ob[:, 0:2 * GK], qd_b.partition_broadcast(P)),
                (ob[:, 3 * GK:], qw_b.partition_broadcast(P)),
                (sg[:, 0:G], dscale.rearrange("a b c g e f -> (a b c g e f)").partition_broadcast(P)),
                (pr[:, :], prior.rearrange("a b c e k t -> (a b c e k t)").partition_broadcast(P)),
                (pos[:, :, :], c_pos), (base[:, :, :], c_base),
                (heads[:, :], c_heads), (dec[:, :], c_dec), (tri[:, :], c_tri),
                (ow[:, :, :], out_w.rearrange("(n p) d -> p n d", p=P)),
                (rows[:, 0, :], out_b.unsqueeze(0)), (rows[:, 1, :], bproj.unsqueeze(0)),
                (wqkv[:, :], Wqkv), (wp[:, 0, :], Wproj),
                (bq[:, :], bqkv[0:2 * D].rearrange("(n p) -> p n", p=P)),
                (bv[:, :], bqkv[2 * D:3 * D].partition_broadcast(P)),
                (bias[:, :, :, :], c_mask),
            ]
            for n, (gate_w, gate_b, m1, mb1, m2, mb2) in enumerate(moe_weights):
                loads += [
                    (gw[n][:, :], gate_w), (gb[n][:, :], gate_b.partition_broadcast(P)),
                    (w1[n][:, :, :], m1.rearrange("e d f -> d e f")),
                    (b1[n][:, :], mb1.rearrange("e (c p) -> p (e c)", p=P)),
                    (w2[n][:, :, :], m2.rearrange("e (c p) d -> p (e c) d", p=P)),
                    (b2[n][:, :], mb2),
                ]
            for dst, src in loads:
                sp.dma_start(dst, src, allow_slow_non_contiguous=True).then_inc(const_in, 16)
            CONSTS = 16 * len(loads)
            for qi in range(BLK):
                for qj in range(BLK):
                    q = qi * BLK + qj
                    sp.dma_start(prob[q:P:BLK * BLK, 0, :].rearrange("h (a c) -> h a c", a=KW),
                                 rpb[:, HALO - qi:HALO - qi + KW, HALO - qj:HALO - qj + KW])\
                        .then_inc(rpb_in, 16)
            sp.wait_ge(zeros_set, 1)
            pv = patches.rearrange("(n m) f -> n m f", m=PATCHES)
            for q, at in enumerate(CORNER_AT):
                for m0, m1 in ((0, PADM - at), (PATCHES - at, PATCHES)):
                    if m1 > m0:
                        sp.dma_start(pv[0:G, m0:m1, q * C:(q + 1) * C],
                                     zeros[0:G, 0:(m1 - m0) * C].rearrange("n (m c) -> n m c", c=C))\
                            .then_inc(zeros_out, 16)
            for b in range(1, B):
                sp.dma_start(patches[b * G * PATCHES:(b + 1) * G * PATCHES, :].rearrange("n f -> (n f)")
                             .rearrange("(p g m) -> p g m", g=G, m=PATCHES),
                             zeros.unsqueeze(1).to_broadcast([P, G, PATCHES])).then_inc(cleared, 16)
            halo = HALO * PH * D // (B * G)
            for b in range(B):
                for r0 in (b * PH, (b + 1) * PH - HALO):
                    sp.dma_start(vpad[r0:r0 + HALO, :, :].rearrange("r w d -> (r w d)")
                                 .rearrange("(p f) -> p f", f=halo), zeros[0:B * G, 0:halo]).then_inc(zeros_out, 16)
                for w0 in (0, PH - HALO):
                    sp.dma_start(vpad[b * PH + HALO:b * PH + HALO + H, w0:w0 + HALO, :]
                                 .rearrange("r w d -> r (w d)"), zeros[0:H, 0:HALO * D]).then_inc(zeros_out, 16)

            def store_values(t):
                sp.wait_ge(*prep_v.done("vals", t))
                sp.wait_ge(cleared, (t // TB + B - 1) // B * (16 * (B - 1)) + 16)
                b, m0 = t // TB, (t % TB) * P
                for q, at in enumerate(CORNER_AT):
                    dst = pv[bass.ds(b * G, G), bass.ds(m0 + (PADM - at), P), q * C:(q + 1) * C]
                    sp.dma_start(dst.rearrange("g m c -> m g c"),
                                 vsb.rearrange("p (g c) -> p g c", g=G)).then_inc(*values_out.one())

            def store_weights(t):
                sp.wait_ge(*prep_v.done("wq", t))
                sp.dma_start(weights[bass.ds(t * P, P), :], wq).then_inc(*weights_out.one())

            def load_weights(t):
                sp.wait_ge(*weights_out.through(t))
                sp.wait_ge(*conv_v.done("m3", t - 1))
                sp.dma_start(wbuf[:, :], weights[bass.ds(t * P, P), :]).then_inc(*weights_in.one())

            def store_v(t):
                sp.wait_ge(*qkv_v.done("v", t))
                r = (t // TB) * PH + (t % TB) * TILE_ROWS + HALO
                for a in range(TILE_ROWS):
                    sp.dma_start(vpad[bass.ds(r + a, 1), HALO:HALO + W, :].rearrange("o w d -> (o w) d"),
                                 vt[a * W:(a + 1) * W, :]).then_inc(*v_out.one())

            windows = bass.AP(tensor=vpad.tensor, offset=0, ap=[
                [PH * D, B * PH], [D, KW], [BLK * D, NB], [1, D]])

            def load_window(t, stored):
                sp.wait_ge(*v_out.through(stored))
                sp.wait_ge(*att_t.done("o", t - 1))
                r = (t // TB) * PH + (t % TB) * TILE_ROWS
                for a in range(KW):
                    sp.dma_start(vwin[a * KW:(a + 1) * KW, :, :],
                                 windows[bass.ds(r + a, 1), :, :, :].rearrange("o c j d -> (o c) j d"))\
                        .then_inc(*v_in.one())

            yv = out.rearrange("b h w d -> (b h w) d")

            def store_out(t, u):
                sp.wait_ge(*exp_v.all(u))
                sp.dma_start(yv[bass.ds(t * P, P), :], X[:, bass.ds(t, 1), :].rearrange("p o d -> p (o d)"))\
                    .then_inc(*y_out.one())

            with sp.Fori(0, LEAD) as t:
                store_values(t)
                store_weights(t)
            sp.wait_ge(zeros_out, 16 * (6 + 4 * B))
            load_weights(0)

            def slot(i, u1, qk, att, e1, cv=True, prep=True):
                if qk:
                    store_v(i - 2)
                if att:
                    load_window(i - 3, i - 2 if not isinstance(i, int) or i - 2 < NT else NT - 1)
                if e1:
                    store_out(i - 4, u1)
                if prep:
                    store_values(i + LEAD)
                    store_weights(i + LEAD)
                if cv:
                    load_weights(i + 1)

            for i in range(4):
                slot(i, None, i > 1, i > 2, False)
            with sp.Fori(4, NT - LEAD) as i:
                slot(i, i * 2 - 5, True, True, True)
            with sp.Fori(NT - LEAD, NT - 1) as i:
                slot(i, i * 2 - 5, True, True, True, prep=False)
            u = 2 * NT - 5
            slot(NT - 1, u - 2, True, True, True, cv=False, prep=False)
            slot(NT, u, True, True, True, cv=False, prep=False)
            store_v(NT - 1)
            load_window(NT - 2, NT - 1)
            store_out(NT - 3, u + 2)
            load_window(NT - 1, NT - 1)
            store_out(NT - 2, u + 3)
            store_out(NT - 1, u + 4)
            sp.wait_ge(*y_out.through(NT - 1))

        @block.gpsimd
        def _(pool):
            gath_g.begin(pool)
            pool.memset(zeros, 0.0).then_inc(zeros_set, 1)
            pool.wait_ge(zeros_out, 16 * (6 + 4 * B))
            pool.wait_ge(cleared, 16 * B)
            with pool.Fori(0, NT) as t:
                pool.wait_ge(*values_out.through((t // TB) * TB + (TB - 1)))
                pool.wait_ge(*prep_v.done("rank", t))
                for q in range(NQ):
                    pool.wait_ge(*conv_v.done(f"r{q}", t - 1))
                    pool.wait_ge(*gath_g.done(f"c{q}", t - 1))
                    rt = rank[:, bass.ds(t % RRING, 1), q * QJ:(q + 1) * QJ].rearrange("p o j -> p (o j)")
                    pool.tensor_copy(ranks[:, q, :], rt).then_inc(*gath_g.step(f"c{q}"))
                    pool.wait_ge(*gath_g.done(f"c{q}", t))
                    pool.sem_inc(passed, 1)
                    for j in range(QJ):
                        pool.indirect_dma_start(
                            out=got[:, q, j * PATCH:(j + 1) * PATCH], out_offset=None,
                            in_=patches, in_offset=bass.IndirectOffsetOnAxis(ap=ranks[:, q, j:j + 1], axis=0),
                        ).then_inc(*got_q[q].one())

        @block.vector
        def _(v):
            for s in (prep_v, conv_v, *route_v, exp_v, qkv_v, att_v):
                s.begin(v)
            v.memset(KT[:, :, :], 0.0).then_inc(setup, 1)
            v.memset(ones[:, :], 1.0).then_inc(setup, 1)
            for n in range(2):
                v.memset(taken[n][:, :], 0.0).then_inc(setup, 1)
            v.wait_ge(const_in, CONSTS)
            v.wait_ge(x_in, 16)
            v.tensor_tensor(ob[:, 0:2 * GK].rearrange("p (g k) -> p g k", g=G),
                            ob[:, 0:2 * GK].rearrange("p (g k) -> p g k", g=G),
                            pr[:, :].unsqueeze(1).to_broadcast([P, G, 2 * K]), ALU.add).then_inc(setup, 1)
            v.tensor_scalar(ob[:, 2 * GK:3 * GK].rearrange("p (g k) -> p g k", g=G),
                            sg[:, 0:G].unsqueeze(2).to_broadcast([P, G, K]), 1.0, None, ALU.mult)\
                .then_inc(setup, 1)
            for h in range(NH - 1, -1, -1):
                v.wait_ge(setup, 6 + (NH - 1 - h))
                v.tensor_scalar(wp[:, h, :], wp[:, 0, :], heads[:, h:h + 1], None, ALU.mult).then_inc(setup, 1)
            v.wait_ge(rpb_in, 16 * BLK * BLK)
            bt = bias[:, :, :, :].rearrange("p t j k -> p (t j) k")
            v.tensor_tensor(bt, bt, prob[:, 0:1, :].to_broadcast([P, 9, KK]), ALU.add).then_inc(setup, 1)
            v.wait_ge(setup, 7 + NH)

            def prepare(part, t, before=None):
                d = prep_v.done
                s = prep_v.step
                if part == "stats":
                    xt = X[:, bass.ds(t, 1), :].rearrange("p o d -> p (o d)")
                    v.wait_ge(*prep_v.all(t - 1))
                    v.sem_inc(passed, 1)
                    v.bn_stats(st_p[:, :], xt).then_inc(*s("stats"))
                    v.wait_ge(*d("stats", t))
                    v.sem_inc(passed, 1)
                    v.bn_aggr(mv_p[:, :], st_p[:, :]).then_inc(*s("aggr"))
                    v.wait_ge(*d("aggr", t))
                    v.tensor_scalar(sd_p[:, 0:1], mv_p[:, 1:2], 1e-6, None, ALU.add).then_inc(*s("eps"))
                if part == "norm":
                    xt = X[:, bass.ds(t, 1), :].rearrange("p o d -> p (o d)")
                    v.wait_ge(*prep_s.done("std", t))
                    v.reciprocal(rs_p[:, :], sd_p[:, 1:2]).then_inc(*s("rstd"))
                    v.wait_ge(*d("rstd", t))
                    v.tensor_scalar(xn_p, xt, mv_p[:, 0:1], rs_p[:, 0:1], ALU.subtract, ALU.mult).then_inc(*s("xn"))
                if part == "values":
                    v.wait_ge(*prep_t.done("vals", t))
                    v.wait_ge(*values_out.through(t - 1))
                    v.tensor_tensor(vsb, CV[:, P:P + VW], vb[:, :], ALU.add).then_inc(*s("vals"))
                if part == "offsets":
                    v.wait_ge(*prep_t.done("offs", t))
                    v.tensor_tensor(osb, CV[:, 0:OFFW], ob[:, :], ALU.add).then_inc(*s("offs"))
                if part == "places":
                    v.wait_ge(*prep_s.done("exp", t))
                    v.tensor_scalar(sg, sg, 1.0, None, ALU.add).then_inc(*s("e1"))
                    v.wait_ge(*d("e1", t))
                    v.reciprocal(sg, sg).then_inc(*s("sig"))
                    v.wait_ge(*d("sig", t))
                    v.scalar_tensor_tensor(out=pp.rearrange("p (a j) -> p j a", a=2),
                                           in0=osb[:, 0:2 * GK].rearrange("p (j a) -> p j a", a=2),
                                           scalar=MAX_SCALE, in1=sg.unsqueeze(2).to_broadcast([P, GK, 2]),
                                           op0=ALU.mult, op1=ALU.mult).then_inc(*s("off"))
                    v.wait_ge(*d("off", t))
                    pt = pos[:, bass.ds(t, 1), :].rearrange("p o a -> p (o a)")
                    p2 = pp.rearrange("p (a j) -> p a j", a=2)
                    v.tensor_tensor(p2, p2, pt.unsqueeze(2).to_broadcast([P, 2, GK]), ALU.add).then_inc(*s("pos"))
                    v.wait_ge(*d("pos", t))
                    v.tensor_scalar(pp, pp, -2.0, float(W + 1), ALU.max, ALU.min).then_inc(*s("clamp"))
                    v.wait_ge(*d("clamp", t))
                    v.tensor_copy(pint, pp).then_inc(*s("int"))
                    v.wait_ge(*d("int", t))
                    v.tensor_copy(fl, pint).then_inc(*s("flt"))
                    v.wait_ge(*d("flt", t))
                    v.tensor_tensor(tmp, fl, pp, ALU.is_gt).then_inc(*s("above"))
                    v.wait_ge(*d("above", t))
                    v.tensor_tensor(fl, fl, tmp, ALU.subtract).then_inc(*s("floor"))
                    v.wait_ge(*d("floor", t))
                    v.tensor_tensor(fr, pp, fl, ALU.subtract).then_inc(*s("frac"))
                    v.wait_ge(*d("frac", t))
                    v.tensor_scalar(fr0, fr, -1.0, 1.0, ALU.mult, ALU.add).then_inc(*s("frac0"))
                if part == "corners":
                    w0, w1_ = wlin[:, 0:2 * GK], wlin[:, 2 * GK:4 * GK]
                    v.tensor_scalar(tmp, fl, float(W - 1), None, ALU.is_le).then_inc(*s("a0"))
                    v.wait_ge(*d("a0", t))
                    v.scalar_tensor_tensor(out=tmp, in0=fl, scalar=0.0, in1=tmp, op0=ALU.is_ge, op1=ALU.mult)\
                        .then_inc(*s("in0"))
                    v.wait_ge(*d("in0", t))
                    v.tensor_tensor(w0, tmp, fr0, ALU.mult).then_inc(*s("w0"))
                    v.wait_ge(*d("w0", t))
                    v.tensor_scalar(tmp, fl, float(W - 2), None, ALU.is_le).then_inc(*s("a1"))
                    v.wait_ge(*d("a1", t))
                    v.scalar_tensor_tensor(out=tmp, in0=fl, scalar=-1.0, in1=tmp, op0=ALU.is_ge, op1=ALU.mult)\
                        .then_inc(*s("in1"))
                    v.wait_ge(*d("in1", t))
                    v.tensor_tensor(w1_, tmp, fr, ALU.mult).then_inc(*s("w1"))
                    v.wait_ge(*d("w1", t))
                    wl = wlin.rearrange("p (s a j) -> p s a j", s=2, a=2)
                    wy3 = wyw.rearrange("p (s j) -> p s j", s=2)
                    v.tensor_tensor(wy3, wl[:, :, 1, :], osb[:, 3 * GK:4 * GK].unsqueeze(1).to_broadcast([P, 2, GK]),
                                    ALU.mult).then_inc(*s("wy"))
                    v.wait_ge(*d("wy", t))
                    v.wait_ge(*weights_out.through(t - 1))
                    v.tensor_tensor(wq.rearrange("p (j y x) -> p j y x", y=2, x=2),
                                    wyw.rearrange("p (y j) -> p j y", y=2).unsqueeze(3).to_broadcast([P, GK, 2, 2]),
                                    wl[:, :, 0, :].rearrange("p x j -> p j x").unsqueeze(2).to_broadcast([P, GK, 2, 2]),
                                    ALU.mult).then_inc(*s("wq"))
                    v.tensor_scalar(tmp, fl, -1.0, float(W - 1), ALU.max, ALU.min).then_inc(*s("flc"))
                    v.wait_ge(*d("flc", t))
                    v.scalar_tensor_tensor(out=fr0[:, 0:GK], in0=tmp[:, GK:2 * GK], scalar=float(W),
                                           in1=tmp[:, 0:GK], op0=ALU.mult, op1=ALU.add).then_inc(*s("lin"))
                    v.wait_ge(*d("lin", t))
                    bs = base[:, bass.ds(t, 1), :].rearrange("p o g -> p (o g)")
                    rt = rank[:, bass.ds(t % RRING, 1), :].rearrange("p o j -> p (o j)")
                    v.tensor_tensor(rt.rearrange("p (g k) -> p g k", g=G),
                                    fr0[:, 0:GK].rearrange("p (g k) -> p g k", g=G),
                                    bs.unsqueeze(2).to_broadcast([P, G, K]), ALU.add).then_inc(*s("rank"))

            with v.Fori(0, LEAD) as t:
                for part in PREPARE:
                    prepare(part, t)

            def conv(part, t, prepared=None):
                d, s = conv_v.done, conv_v.step
                if isinstance(part, int):
                    q = part
                    if q == 0:
                        v.wait_ge(*weights_in.through(t))
                        v.wait_ge(*conv_t.done("T", t - 1))
                    g3 = got[:, q, :].rearrange("p (j c) -> p j c", c=C)
                    wj = wbuf[:, q * QJ * CORNERS:(q + 1) * QJ * CORNERS]
                    v.wait_ge(*got_q[q].through(t))
                    v.tensor_tensor(g3, g3, wj.unsqueeze(2).to_broadcast([P, QJ * CORNERS, C]), ALU.mult)\
                        .then_inc(*s(f"m{q}"))
                    v.wait_ge(*d(f"m{q}", t))
                    v.tensor_reduce(summed[:, q * QG * C:(q + 1) * QG * C].rearrange("p (g c) -> p g c", g=QG),
                                    got[:, q, :].rearrange("p (g j c) -> p g c j", g=QG, c=C), AX.X, ALU.add)\
                        .then_inc(*s(f"r{q}"))
                if part == "project":
                    xt = X[:, bass.ds(t, 1), :].rearrange("p o d -> p (o d)")
                    v.wait_ge(*conv_t.done("proj", t))
                    v.tensor_tensor(xt, CV[:, 256:384], xt, ALU.add).then_inc(*s("add"))

            def route(part, n, t, freed=None, after=None):
                d, s = route_v[n].done, route_v[n].step
                xt = X[:, bass.ds(t, 1), :].rearrange("p o d -> p (o d)")
                lg, eqd, hot, ps, kept, gate = (route_b[n][:, k, :] for k in range(6))
                if part == "stats":
                    v.wait_ge(*(conv_v, att_v)[n].all(t))
                    v.sem_inc(passed, 1)
                    v.bn_stats(st_m[:, :], xt).then_inc(*s("stats"))
                    v.wait_ge(*d("stats", t))
                    v.sem_inc(passed, 1)
                    v.bn_aggr(mv_m[:, :], st_m[:, :]).then_inc(*s("aggr"))
                    v.wait_ge(*d("aggr", t))
                    v.tensor_scalar(sd_m[:, 0:1], mv_m[:, 1:2], 1e-5, None, ALU.add).then_inc(*s("eps"))
                if part == "norm":
                    v.wait_ge(*route_s[n].done("std", t))
                    v.reciprocal(rs_m[:, :], sd_m[:, 1:2]).then_inc(*s("rstd"))
                    v.wait_ge(*d("rstd", t))
                    v.tensor_scalar(xn_m[n][:, :], xt, mv_m[:, 0:1], rs_m[:, 0:1], ALU.subtract, ALU.mult)\
                        .then_inc(*s("xn"))
                if part == "logits":
                    v.wait_ge(*route_t[n].done("lg", t))
                    v.tensor_tensor(lg, RB[n][:, 128:136], gb[n][:, :], ALU.add).then_inc(*s("lg"))
                    v.wait_ge(*d("lg", t))
                    v.tensor_reduce(small[n][:, 0:1], lg, AX.X, ALU.max).then_inc(*s("max"))
                    v.wait_ge(*d("max", t))
                    v.tensor_scalar(small[n][:, 1:2], small[n][:, 0:1], -1.0, None, ALU.mult).then_inc(*s("neg"))
                    v.scalar_tensor_tensor(out=eqd, in0=lg, scalar=small[n][:, 0:1], in1=dec[:, :],
                                           op0=ALU.is_equal, op1=ALU.mult).then_inc(*s("eqd"))
                    v.wait_ge(*d("eqd", t))
                    v.tensor_reduce(small[n][:, 2:3], eqd, AX.X, ALU.max).then_inc(*s("first"))
                    v.wait_ge(*d("first", t))
                    v.tensor_scalar(hot, eqd, small[n][:, 2:3], None, ALU.is_equal).then_inc(*s("hot"))
                if part == "gate":
                    v.wait_ge(*route_s[n].done("exp", t))
                    v.reciprocal(small[n][:, 4:5], small[n][:, 3:4]).then_inc(*s("rsum"))
                    v.wait_ge(*route_t[n].done("cum", t))
                    v.tensor_tensor(ps, RB[n][:, 136:144], taken[n][:, :], ALU.add).then_inc(*s("pos"))
                    v.wait_ge(*d("pos", t))
                    v.tensor_tensor(taken[n][:, :], RB[n][:, 144:152], taken[n][:, :], ALU.add)\
                        .then_inc(*s("taken"))
                    v.scalar_tensor_tensor(out=kept, in0=ps, scalar=float(CAPACITY), in1=hot,
                                           op0=ALU.is_le, op1=ALU.mult).then_inc(*s("kept"))
                    v.wait_ge(*d("kept", t))
                    v.tensor_scalar(gate, kept, small[n][:, 4:5], None, ALU.mult).then_inc(*s("gate"))

            def add_up(u, n, t, e0, e1):
                d, s = exp_v.done, exp_v.step
                gate = route_b[n][:, 5, :]
                v.wait_ge(*exp_t.done(f"y{e1 - 1}", u))
                for e in range(e0, e1):
                    so_far = acc
                    if e == 0:
                        v.wait_ge(*route_v[n].done("gate", t))
                        v.wait_ge(*route_s[n].done("b2", t))
                        v.wait_ge(*exp_v.all(u - 1))
                        so_far = share[n]
                    else:
                        v.wait_ge(*d(f"a{e - 1}", u))
                    v.scalar_tensor_tensor(out=acc[:, :], in0=Y[e // 4][:, (e % 4) * D:(e % 4 + 1) * D],
                                           scalar=gate[:, e:e + 1], in1=so_far[:, :],
                                           op0=ALU.mult, op1=ALU.add).then_inc(*s(f"a{e}"))

            def experts(u, n, t, beside):
                for e in range(E):
                    beside(e)
                    if e == 4:
                        add_up(u, n, t, 0, 4)

            def close(u, n, t):
                d, s = exp_v.done, exp_v.step
                xt = X[:, bass.ds(t, 1), :].rearrange("p o d -> p (o d)")
                add_up(u, n, t, 4, E)
                le, clip, hi = (fin[:, k, :] for k in range(3))
                v.wait_ge(*d(f"a{E - 1}", u))
                v.tensor_scalar(le, acc[:, :], BIGGEST, None, ALU.is_le).then_inc(*s("le"))
                v.wait_ge(*d("le", u))
                v.scalar_tensor_tensor(out=le, in0=acc[:, :], scalar=-BIGGEST, in1=le,
                                       op0=ALU.is_ge, op1=ALU.mult).then_inc(*s("fin"))
                v.tensor_scalar(clip, acc[:, :], -BIGGEST, BIGGEST, ALU.max, ALU.min).then_inc(*s("clip"))
                v.wait_ge(*d("clip", u))
                v.tensor_tensor(clip, clip, le, ALU.mult).then_inc(*s("fpart"))
                v.tensor_scalar(hi, acc[:, :], BIGGEST, None, ALU.is_gt).then_inc(*s("hi"))
                v.wait_ge(*d("hi", u))
                v.scalar_tensor_tensor(out=hi, in0=acc[:, :], scalar=-BIGGEST, in1=hi,
                                       op0=ALU.is_lt, op1=ALU.subtract).then_inc(*s("sign"))
                v.tensor_tensor(xt, xt, clip, ALU.add).then_inc(*s("x1"))
                v.wait_ge(*d("x1", u))
                v.scalar_tensor_tensor(out=xt, in0=hi, scalar=-1e4, in1=xt,
                                       op0=ALU.mult, op1=ALU.add).then_inc(*s("x2"))

            def qkv(part, t, u=None):
                d, s = qkv_v.done, qkv_v.step
                xt = X[:, bass.ds(t, 1), :].rearrange("p o d -> p (o d)")
                if part == "stats":
                    v.wait_ge(*exp_v.all(u))
                    v.sem_inc(passed, 1)
                    v.bn_stats(st_q[:, :], xt).then_inc(*s("stats"))
                    v.wait_ge(*d("stats", t))
                    v.sem_inc(passed, 1)
                    v.bn_aggr(mv_q[:, :], st_q[:, :]).then_inc(*s("aggr"))
                    v.wait_ge(*d("aggr", t))
                    v.tensor_scalar(sd_q[:, 0:1], mv_q[:, 1:2], 1e-6, None, ALU.add).then_inc(*s("eps"))
                if part == "norm":
                    v.wait_ge(*qkv_s.done("std", t))
                    v.reciprocal(rs_q[:, :], sd_q[:, 1:2]).then_inc(*s("rstd"))
                    v.wait_ge(*d("rstd", t))
                    v.tensor_scalar(xn_q[:, :], xt, mv_q[:, 0:1], rs_q[:, 0:1], ALU.subtract, ALU.mult)\
                        .then_inc(*s("xn"))
                if part == "project":
                    r = t % QRING
                    v.wait_ge(*qkv_t.done("qkv", t))
                    v.tensor_scalar(QT[:, bass.ds(r, 1), :, :].rearrange("p o j (a c) -> p (o a) j c", a=BLK),
                                    M[:, 128:256].rearrange("p (a j c) -> p a j c", a=BLK, j=NB),
                                    bq[:, 0:1], HD ** -0.5, ALU.add, ALU.mult).then_inc(*s("q"))
                    kr = (t // TB) % RING * PH + (t % TB) * TILE_ROWS + HALO
                    v.tensor_scalar(KT[:, bass.ds(kr, TILE_ROWS), HALO:HALO + W],
                                    M[:, 256:384].rearrange("p (a w) -> p a w", a=TILE_ROWS),
                                    bq[:, 1:2], None, ALU.add).then_inc(*s("k"))
                    v.wait_ge(*v_out.through(t - 1))
                    v.tensor_tensor(vt[:, :], M[:, 384:512], bv[:, :], ALU.add).then_inc(*s("v"))

            def attend(part, t, after=None):
                d, s = att_v.done, att_v.step
                if part == "queries":
                    v.wait_ge(*att_t.done("s1", t - 1))
                    v.tensor_tensor(qbd, QT[:, bass.ds(t % QRING, 1), :, :].rearrange("p o j q -> p (o j) q")
                                    .unsqueeze(2).to_broadcast([P, NB, NH, BLK * BLK]),
                                    heads[:, :].unsqueeze(1).unsqueeze(3).to_broadcast([P, NB, NH, BLK * BLK]),
                                    ALU.mult).then_inc(*s("qbd"))
                if part == "scores":
                    row = (t % TB + (TB - 1)) // TB + (t % TB + 1) // TB
                    bt = bias[:, bass.ds(row, 1), :, :].rearrange("p o j k -> p (o j) k")
                    for k, blocks in enumerate((((0, 1, 0), (1, 4, 1)), ((4, 7, 1), (7, 8, 2)))):
                        v.wait_ge(*att_t.done(f"s{k}", t))
                        for j0, j1, kind in blocks:
                            a, b = (j0 % 4) * P, (j0 % 4 + j1 - j0) * P
                            ins = v.tensor_tensor(
                                prob[:, j0:j1, :],
                                N[k][:, a:b].rearrange("p (j k) -> p j k", k=P)[:, :, 0:KK],
                                bt[:, kind:kind + 1, :].to_broadcast([P, j1 - j0, KK]), ALU.add)
                        ins.then_inc(*s(f"s{k}"))
                    v.wait_ge(*d("s1", t))
                    v.tensor_reduce(soft[:, 0, :], prob, AX.X, ALU.max).then_inc(*s("max"))
                    v.wait_ge(*d("max", t))
                    v.tensor_scalar(soft[:, 1, :], soft[:, 0, :], -1.0, None, ALU.mult).then_inc(*s("neg"))
                if part == "weights":
                    v.wait_ge(*att_s.done("exp", t))
                    v.reciprocal(soft[:, 3, :], soft[:, 2, :]).then_inc(*s("rsum"))
                    v.wait_ge(*d("rsum", t))
                    v.tensor_tensor(prob, prob, soft[:, 3, :].unsqueeze(2).to_broadcast([P, NB, KK]), ALU.mult)\
                        .then_inc(*s("norm"))
                if part == "values":
                    v.wait_ge(*att_t.done("o", t))
                    v.tensor_copy(OT[:, 4:8, :].rearrange("p h n -> p (h n)"), N[1][:, :]).then_inc(*s("o1"))
                if part == "project":
                    xt = X[:, bass.ds(t, 1), :].rearrange("p o d -> p (o d)")
                    v.wait_ge(*att_t.done("proj", t))
                    v.tensor_tensor(xt, N[0][:, 0:D], xt, ALU.add).then_inc(*s("add"))

            slots(v, conv, route, experts, close, qkv, attend, prepare)

        @block.scalar
        def _(a):
            for s in (prep_s, conv_s, *route_s, exp_s, qkv_s, att_s):
                s.begin(a)

            def prepare(part, t, before=None):
                s = prep_s.step
                if part == "stats":
                    a.wait_ge(*prep_v.done("eps", t))
                    a.activation(sd_p[:, 1:2], sd_p[:, 0:1], ACT.Sqrt).then_inc(*s("std"))
                if part == "turn":
                    a.wait_ge(*prep_t.done("xT", t))
                    a.activation(xt_p, CV[:, 0:P], ACT.Copy).then_inc(*s("xT"))
                if part == "offsets":
                    a.wait_ge(*prep_v.done("offs", t))
                    a.activation(sg, osb[:, 2 * GK:3 * GK], ACT.Exp, scale=-1.0).then_inc(*s("exp"))

            with a.Fori(0, LEAD) as t:
                for part in PREPARE:
                    prepare(part, t)

            def conv(part, t, prepared=None):
                if part == "turn":
                    a.wait_ge(*conv_t.done("T", t))
                    a.activation(summed_T[:, :, :].rearrange("p n q -> p (n q)"), CV[:, 0:256], ACT.Copy)\
                        .then_inc(*conv_s.step("T"))

            def route(part, n, t, freed=None, after=None):
                s = route_s[n].step
                if part == "stats":
                    a.wait_ge(*route_v[n].done("eps", t))
                    a.activation(sd_m[:, 1:2], sd_m[:, 0:1], ACT.Sqrt).then_inc(*s("std"))
                if part == "turn":
                    a.wait_ge(*route_t[n].done("xT", t))
                    a.wait_ge(*exp_t.done("z7", freed))
                    a.activation(xt_m[n][:, :], RB[n][:, 0:P], ACT.Copy).then_inc(*s("xT"))
                if part == "logits":
                    a.wait_ge(*route_v[n].done("neg", t))
                    a.activation(route_b[n][:, 6, :], route_b[n][:, 0, :], ACT.Exp, bias=small[n][:, 1:2],
                                 accum_out=small[n][:, 3:4]).then_inc(*s("exp"))
                if part == "gate_T":
                    a.wait_ge(*route_t[n].done("gT", t))
                    a.activation(gate_T[n][:, :], RB[n][0:E, 152:280], ACT.Copy).then_inc(*s("gT"))
                if part == "share":
                    a.wait_ge(*route_t[n].done("b2", t))
                    a.activation(share[n][:, :], RB[n][:, 280:408], ACT.Copy).then_inc(*s("b2"))

            def experts(u, n, t, beside):
                def relu(e):
                    a.wait_ge(*exp_t.done(f"z{e}", u))
                    a.wait_ge(*(exp_t.done(f"y{e - 2}", u) if e >= 2 else exp_t.done(f"y{e + 6}", u - 1)))
                    for c in range(FC):
                        ins = a.activation(hid[:, e % 2, c, :], Z[e % 2][:, c * P:(c + 1) * P], ACT.Relu,
                                           bias=b1[n][:, e * FC + c:e * FC + c + 1])
                    ins.then_inc(*exp_s.step(f"h{e}"))

                relu(0)
                for e in range(E):
                    if e + 1 < E:
                        relu(e + 1)
                    beside(e)

            def close(u, n, t):
                pass

            def qkv(part, t, u=None):
                s = qkv_s.step
                if part == "stats":
                    a.wait_ge(*qkv_v.done("eps", t))
                    a.activation(sd_q[:, 1:2], sd_q[:, 0:1], ACT.Sqrt).then_inc(*s("std"))
                if part == "turn":
                    a.wait_ge(*qkv_t.done("xT", t))
                    a.activation(xt_q[:, :], M[:, 0:P], ACT.Copy).then_inc(*s("xT"))

            def attend(part, t, after=None):
                s = att_s.step
                if part == "scores":
                    a.wait_ge(*att_v.done("neg", t))
                    for j in range(NB):
                        ins = a.activation(prob[:, j, :], prob[:, j, :], ACT.Exp, bias=soft[:, 1, j:j + 1],
                                           accum_out=soft[:, 2, j:j + 1])
                    ins.then_inc(*s("exp"))
                if part == "turn":
                    for k in range(2):
                        a.wait_ge(*att_t.done(f"p{k}", t))
                        a.activation(PT[0:KK, 4 * k:4 * k + 4, :].rearrange("p j q -> p (j q)"), N[k][0:KK, :],
                                     ACT.Copy).then_inc(*s(f"p{k}"))
                if part == "values":
                    a.wait_ge(*att_t.done("o", t))
                    a.activation(OT[:, 0:4, :].rearrange("p h n -> p (h n)"), N[0][:, :], ACT.Copy)\
                        .then_inc(*s("o0"))

            slots(a, conv, route, experts, close, qkv, attend, prepare)

        @block.tensor
        def _(pe):
            for s in (prep_t, conv_t, *route_t, exp_t, qkv_t, att_t):
                s.begin(pe)
            pe.wait_ge(setup, 7 + NH)

            def prepare(part, t, before=None):
                s = prep_t.step
                if part == "turn":
                    pe.wait_ge(*prep_v.done("xn", t))
                    pe.wait_ge(*prep_v.done("offs", t - 1))
                    if before is not None:
                        pe.wait_ge(*route_s[0].done("b2", before))
                    pe.transpose(CV[:, 0:P], xn_p, ident[:, :]).then_inc(*s("xT"))
                if part == "values":
                    pe.wait_ge(*prep_s.done("xT", t))
                    pe.matmul(CV[:, P:P + VW], xt_p, wv[:, :], start=True, stop=True).then_inc(*s("vals"))
                if part == "offsets":
                    pe.wait_ge(*prep_v.done("vals", t))
                    pe.matmul(CV[:, 0:OFFW], xt_p, wo[:, :], start=True, stop=True).then_inc(*s("offs"))

            with pe.Fori(0, LEAD) as t:
                for part in PREPARE:
                    prepare(part, t)

            def conv(part, t, prepared=None):
                s = conv_t.step
                if part == "turn":
                    pe.wait_ge(*conv_v.done("r3", t))
                    pe.wait_ge(*route_s[0].done("b2", t - 1))
                    pe.wait_ge(*prep_v.done("offs", prepared))
                    for n in range(2):
                        ins = pe.transpose(CV[:, n * P:(n + 1) * P], summed[:, n * P:(n + 1) * P], ident[:, :])
                    ins.then_inc(*s("T"))
                if part == "project":
                    pe.wait_ge(*conv_s.done("T", t))
                    pe.matmul(CV[:, 256:384], ones[0:1, :], rows[:, 0, :], start=True, stop=False)
                    pe.matmul(CV[:, 256:384], summed_T[:, 0, :], ow[:, 0, :], start=False, stop=False)
                    pe.matmul(CV[:, 256:384], summed_T[:, 1, :], ow[:, 1, :], start=False, stop=True)\
                        .then_inc(*s("proj"))

            def route(part, n, t, freed=None, after=None):
                s = route_t[n].step
                if part == "turn":
                    pe.wait_ge(*route_v[n].done("xn", t))
                    if n == 1:
                        pe.wait_ge(*route_s[n].done("b2", t - 1))
                        pe.wait_ge(*qkv_v.done("v", after))
                    pe.transpose(RB[n][:, 0:P], xn_m[n][:, :], ident[:, :]).then_inc(*s("xT"))
                if part == "logits":
                    pe.wait_ge(*route_s[n].done("xT", t))
                    pe.matmul(RB[n][:, 128:136], xt_m[n][:, :], gw[n][:, :], start=True, stop=True)\
                        .then_inc(*s("lg"))
                if part == "gate":
                    pe.wait_ge(*route_v[n].done("hot", t))
                    hot = route_b[n][:, 2, :]
                    pe.matmul(RB[n][:, 136:144], tri[:, :], hot, start=True, stop=True)
                    pe.matmul(RB[n][:, 144:152], ones[:, :], hot, start=True, stop=True).then_inc(*s("cum"))
                if part == "gate_T":
                    pe.wait_ge(*route_v[n].done("gate", t))
                    pe.matmul(RB[n][0:E, 152:280], route_b[n][:, 5, :], ident[:, :], start=True, stop=True)\
                        .then_inc(*s("gT"))
                if part == "share":
                    pe.wait_ge(*route_s[n].done("gT", t))
                    pe.matmul(RB[n][:, 280:408], gate_T[n][:, :], b2[n][:, :], start=True, stop=True)\
                        .then_inc(*s("b2"))

            def experts(u, n, t, beside):
                s = exp_t.step

                def up(e):
                    pe.wait_ge(*(exp_s.done(f"h{e - 2}", u) if e >= 2 else exp_s.done(f"h{e + 6}", u - 1)))
                    if e == 0:
                        pe.wait_ge(*route_s[n].done("xT", t))
                    for c in range(FC):
                        ins = pe.matmul(Z[e % 2][:, c * P:(c + 1) * P], w1[n][:, e, c * P:(c + 1) * P],
                                        xt_m[n][:, :], start=True, stop=True)
                    ins.then_inc(*s(f"z{e}"))

                def down(e):
                    pe.wait_ge(*exp_s.done(f"h{e}", u))
                    if e % 4 == 0:
                        pe.wait_ge(*exp_v.done(f"a{e + 3}", u - 1))
                    for c in range(FC):
                        ins = pe.matmul(Y[e // 4][:, (e % 4) * D:(e % 4 + 1) * D], hid[:, e % 2, c, :],
                                        w2[n][:, e * FC + c, :], start=(c == 0), stop=(c == FC - 1))
                    ins.then_inc(*s(f"y{e}"))

                up(0)
                for e in range(E):
                    if e + 1 < E:
                        up(e + 1)
                    down(e)
                    beside(e)

            def close(u, n, t):
                pass

            def qkv(part, t, u=None):
                s = qkv_t.step
                if part == "turn":
                    pe.wait_ge(*qkv_v.done("xn", t))
                    pe.wait_ge(*route_s[1].done("b2", t - 2))
                    pe.transpose(M[:, 0:P], xn_q[:, :], ident[:, :]).then_inc(*s("xT"))
                if part == "project":
                    pe.wait_ge(*qkv_s.done("xT", t))
                    for n in range(2):
                        pe.matmul(M[:, (n + 1) * P:(n + 2) * P], wqkv[:, n * D:(n + 1) * D], xt_q[:, :],
                                  start=True, stop=True)
                    pe.matmul(M[:, 384:512], xt_q[:, :], wqkv[:, 2 * D:3 * D], start=True, stop=True)\
                        .then_inc(*s("qkv"))

            def attend(part, t, after=None):
                s = att_t.step
                if part == "queries":
                    kr = (t // TB) % RING * PH + (t % TB) * TILE_ROWS
                    pe.wait_ge(*att_v.done("qbd", t))
                    pe.wait_ge(*qkv_v.done("k", after))
                    pe.wait_ge(*att_v.done("add", t - 1))
                    for j in range(NB):
                        ins = pe.matmul(N[j // 4][:, (j % 4) * P:(j % 4) * P + KK],
                                        qbd[:, j, :, :].rearrange("p h q -> p (h q)"),
                                        KT[:, bass.ds(kr, KW), j * BLK:j * BLK + KW], start=True, stop=True)
                        if j % 4 == 3:
                            ins.then_inc(*s(f"s{j // 4}"))
                if part == "turn":
                    pe.wait_ge(*att_v.done("norm", t))
                    for j in range(NB):
                        ins = pe.transpose(N[j // 4][0:KK, (j % 4) * P:(j % 4 + 1) * P], prob[:, j, :],
                                           ident[:, :])
                        if j % 4 == 3:
                            ins.then_inc(*s(f"p{j // 4}"))
                if part == "values":
                    pe.wait_ge(*att_s.done("p1", t))
                    pe.wait_ge(*v_in.through(t))
                    for k in range(2):
                        for j in range(NB):
                            o = N[k][:, :].rearrange("p (h a w) -> p h a w", h=4, a=BLK)
                            ins = pe.matmul(o[:, :, :, j * BLK:(j + 1) * BLK], vwin[0:KK, j, :],
                                            PT[0:KK, j, k * 64:(k + 1) * 64], start=True, stop=True)
                    ins.then_inc(*s("o"))
                if part == "project":
                    pe.wait_ge(*att_v.done("o1", t))
                    pe.wait_ge(*att_s.done("o0", t))
                    pe.matmul(N[0][:, 0:D], ones[0:1, :], rows[:, 1, :], start=True, stop=False)
                    for h in range(NH):
                        ins = pe.matmul(N[0][:, 0:D], OT[:, h, :], wp[:, h, :], start=False, stop=(h == NH - 1))
                    ins.then_inc(*s("proj"))

            slots(pe, conv, route, experts, close, qkv, attend, prepare)


def constants():
    p = np.arange(P)
    t = np.arange(NT)
    f = np.float32
    pos = np.zeros((P, NT, 2), f)
    pos[:, :, 0] = (p % W)[:, None]
    pos[:, :, 1] = (p // W)[:, None] + (t % TB)[None, :] * TILE_ROWS
    rows = ((t // TB)[:, None] * G + np.arange(G)[None, :]) * PATCHES + PADM
    base = np.broadcast_to(rows, (P, NT, G)).astype(f)
    q = p % (BLK * BLK)
    a = np.arange(KW)
    ok = []
    for at, blocks in ((q // BLK, (0, 1, TB - 1)), (q % BLK, (0, 1, NB - 1))):
        first = np.array([4 * k for k in blocks])
        key = first[None, :, None] - HALO + a[None, None, :]
        start = np.clip(first[None, :] + at[:, None] - HALO, 0, H - WIN)
        ok.append((key >= start[:, :, None]) & (key < start[:, :, None] + WIN))
    mask = ok[0][:, :, None, :, None] & ok[1][:, None, :, None, :]
    return {
        "c_ident": np.eye(P, dtype=f), "c_tri": np.triu(np.ones((P, P), f)), "c_pos": pos, "c_base": base,
        "c_heads": (p[:, None] // HD == np.arange(NH)[None, :]).astype(f),
        "c_dec": np.broadcast_to(np.arange(E, 0, -1).astype(f), (P, E)).copy(),
        "c_mask": np.where(mask, f(0), f(-1e30)).astype(f).reshape(P, 3, 3, KK),
    }


CONV = ["v_w", "v_b", "qd_w", "qd_b", "qs_w", "qw_w", "qw_b", "out_w", "out_b", "prior", "dscale"]
MOE = ["gate_w", "gate_b", "w1", "b1", "w2", "b2"]
ATT = ["Wqkv", "bqkv", "rpb", "Wproj", "bproj"]


def program(nc, aps, out):
    build(nc, aps["x"], *[aps[f"L0_conv_{n}"] for n in CONV],
          [[aps[f"L{k}_ffn_{n}"] for n in MOE] for k in range(2)],
          *[aps[f"L1_conv_{n}"] for n in ATT],
          *[aps[n] for n in ("c_ident", "c_tri", "c_pos", "c_base", "c_heads", "c_dec", "c_mask")], out)


def kernel(**inputs):
    import concourse.bacc as bacc
    from concourse.bass_utils import run_bass_kernel_spmd

    nc = bacc.Bacc("TRN2", target_bir_lowering=False, num_devices=1)
    arrays, aps = {}, {}
    for name, a in {**{k: np.asarray(v) for k, v in inputs.items()}, **constants()}.items():
        a = np.ascontiguousarray(a)
        arrays[f"in_{name}"] = a
        aps[name] = nc.dram_tensor(f"in_{name}", a.shape, mybir.dt.from_np(a.dtype), kind="ExternalInput").ap()
    out = nc.dram_tensor("out_0", (B, H, W, D), F32, kind="ExternalOutput").ap()
    program(nc, aps, out)
    r = run_bass_kernel_spmd(nc, [arrays], core_ids=[0])
    return r.results[0]["out_0"]
```

```python
from contextlib import ExitStack

import numpy as np

import concourse.bass as bass
from concourse import mybir

ALU = mybir.AluOpType
ACT = mybir.ActivationFunctionType
AX = mybir.AxisListType
F32 = mybir.dt.float32
I32 = mybir.dt.int32
U32 = mybir.dt.uint32

P = 128
B, H, W, D = 4, 32, 32, 128
TILE_ROWS = P // W
TB = H // TILE_ROWS
NT = B * TB
G, C, K = 8, 32, 9
GK = G * K
CORNERS = 4
DG = G - 1
NQ = DG
QJ = K
PATCH = CORNERS * C
PADM = W + 1
PATCHES = H * W + PADM
MAX_SCALE = 6.0
CORNER_AT = [0, 1, W, W + 1]
VW, OFFW = G * C, GK * 4
E, F = 8, 512
FC = F // P
CAPACITY = -(-5 * B * H * W // (4 * E))
BIGGEST = float(np.finfo(np.float32).max)
NH, HD, WIN = 8, 16, 7
BLK = 4
NB = W // BLK
KW = BLK + WIN - 1
KK = KW * KW
HALO = WIN // 2
PH = H + 2 * HALO
RING = 1
QRING = 4
LEAD = TB + 1
PLEAD = 2
SRING = 4
MADE = 3
SOON = 2 * TB


VALUES = ("norm", "turn", "values")
PLACES = ("norm", "turn", "offsets", "places", "corners")


class Steps:

    def __init__(self, sem, names):
        self.sem, self.names, self.at = sem, names.split(), 0

    def begin(self, eng):
        eng.sem_inc(self.sem, 2 * len(self.names))

    def step(self, name):
        assert self.names[self.at] == name, (self.names[self.at], name)
        self.at = (self.at + 1) % len(self.names)
        return self.sem, 1

    def done(self, name, turn):
        return self.sem, turn * len(self.names) + (2 * len(self.names) + self.names.index(name) + 1)

    def all(self, turn):
        return self.done(self.names[-1], turn)


class Landed:

    def __init__(self, sem, dmas=1, ahead=1):
        self.sem, self.dmas, self.ahead = sem, dmas, ahead

    def begin(self, eng):
        eng.sem_inc(self.sem, 16 * self.dmas * self.ahead)

    def one(self):
        return self.sem, 16

    def through(self, turn):
        return self.sem, turn * (16 * self.dmas) + (1 + self.ahead) * 16 * self.dmas


def build(nc, x, v_w, v_b, qd_w, qd_b, qs_w, qw_w, qw_b, out_w, out_b, prior, dscale,
          moe_weights, Wqkv, bqkv, rpb, Wproj, bproj,
          c_ident, c_tri, c_iota, c_pos, c_base, c_heads, c_dec, c_mask, out):
    ctx = ExitStack()
    with ctx:
        def sb(name, shape, dt=F32):
            return ctx.enter_context(nc.sbuf_tensor(name, shape, dt))

        def sem(name):
            return ctx.enter_context(nc.semaphore(name))

        def bank(name):
            return ctx.enter_context(nc.psum_tensor(name, [P, 512], F32))

        patches = nc.dram_tensor("patches", (B * G * PATCHES, PATCH), F32, kind="Internal").ap()
        vpad = nc.dram_tensor("vpad", (B * PH, PH, D), F32, kind="Internal").ap()

        X = sb("X", [P, NT, D])
        ident = sb("ident", [P, P])
        tri = sb("tri", [P, P])
        ones = sb("ones", [P, P])
        pos = sb("pos", [P, NT, 2])
        base = sb("base", [P, B, G])
        iota = sb("iota", [P, W])
        heads = sb("heads", [P, NH])
        dec = sb("dec", [P, E])

        wv = sb("wv", [D, VW])
        wo = sb("wo", [D, OFFW])
        vb = sb("vb", [P, VW])
        ob = sb("ob", [P, OFFW])
        pr = sb("pr", [P, K * 2])
        ow = sb("ow", [P, 2, D])
        rows = sb("rows", [1, 2, D])
        w1 = [sb(f"w1_{n}", [D, E, F]) for n in range(2)]
        w2 = [sb(f"w2_{n}", [P, E * FC, D]) for n in range(2)]
        b1 = [sb(f"b1_{n}", [P, E * FC]) for n in range(2)]
        b2 = [sb(f"b2_{n}", [E, D]) for n in range(2)]
        gw = [sb(f"gw_{n}", [D, E]) for n in range(2)]
        gb = [sb(f"gb_{n}", [P, E]) for n in range(2)]
        taken = [sb(f"taken_{n}", [P, E]) for n in range(2)]
        wqkv = sb("wqkv", [D, 3 * D])
        bq = sb("bq", [P, 2])
        bv = sb("bv", [P, D])
        wp = sb("wp", [P, NH, D])
        bias = sb("bias", [P, 3, 3, KK])

        rank = sb("rank", [P, SRING, GK], U32)
        wq = sb("wq", [P, SRING, GK * CORNERS])
        spot = sb("spot", [P, SRING, 3, K])
        st_p, mv_p = sb("st_p", [P, NT, 6]), sb("mv_p", [P, NT, 2])
        rs_p = sb("rs_p", [P, NT])
        got = sb("got", [P, NQ, QJ * PATCH])
        ranks = sb("ranks", [P, NQ, QJ], U32)
        tent = sb("tent", [P, 2, K, W])
        made = sb("made", [P, MADE, H * W])
        v_dense = sb("v_dense", [P, NT, C])
        summed = sb("summed", [P, VW])
        summed_T = sb("summed_T", [P, 2, P])
        st_m, mv_m, sd_m, rs_m = sb("st_m", [P, 6]), sb("mv_m", [P, 2]), sb("sd_m", [P, 2]), sb("rs_m", [P, 1])
        st_q, mv_q, sd_q, rs_q = sb("st_q", [P, 6]), sb("mv_q", [P, 2]), sb("sd_q", [P, 2]), sb("rs_q", [P, 1])
        xn_q, xt_q = sb("xn_q", [P, D]), sb("xt_q", [D, P])
        xn_m = [sb(f"xn_m{n}", [P, D]) for n in range(2)]
        xt_m = [sb(f"xt_m{n}", [D, P]) for n in range(2)]
        route_b = [sb(f"route{n}", [P, 7, E]) for n in range(2)]
        small = [sb(f"small{n}", [P, 6]) for n in range(2)]
        gate_T = [sb(f"gate_T{n}", [E, P]) for n in range(2)]
        share = [sb(f"share{n}", [P, D]) for n in range(2)]
        hid = sb("hid", [P, 2, FC, P])
        acc = sb("acc", [P, D])
        fin = sb("fin", [P, 3, D])
        QT = sb("QT", [P, QRING, NB, BLK * BLK])
        KT = sb("KT", [P, RING * PH, PH])
        vt = sb("vt", [P, D])
        soft = sb("soft", [P, 4, NB])
        turns = sb("turns", [P, 1024])
        qbd = turns[:, :].rearrange("p (j h q) -> p j h q", j=NB, h=NH)
        spread = turns[:, :].rearrange("p (c q) -> p c q", c=TB)
        PT = sb("PT", [P, NB, P])[:, :, :]
        OT = sb("OT", [P, NH, P])[:, :, :]
        vwin = sb("vwin", [P, NB, D])[:, :, :]
        prob = sb("prob", [P, NB, KK])[:, :, :]
        arena = sb("arena", [P, 4 * D + VW + OFFW + 17 * GK])
        cut = [0]

        def part(n):
            cut[0] += n
            return arena[:, cut[0] - n:cut[0]]

        xn_p, xt_p = part(D), part(P)
        xn_o, xt_o = part(D), part(P)
        vsb, osb = part(VW), part(OFFW)
        sg = part(GK)
        pp, fl, fr, fr0, tmp = (part(2 * GK) for _ in range(5))
        wlin = part(4 * GK)
        wyw = part(2 * GK)
        pint = wyw.bitcast(I32)

        zeros = got[:, 0, 0:PATCHES]

        Z = [bank("Z0"), bank("Z1")]
        Y = [bank("Y0"), bank("Y1")]
        M = bank("M")
        N = [bank("N0"), bank("N1")]
        CV = bank("CV")
        RB = [CV, M]

        x_in = [sem(f"x_in{part}") for part in range(2)]
        first_in = sem("first_in")
        const_in = sem("const_in")
        rpb_in = sem("rpb_in")
        zeros_out = sem("zeros_out")
        zeros_set = sem("zeros_set")
        values_out = Landed(sem("values_out"), CORNERS)
        v_out = Landed(sem("v_out"), TILE_ROWS)
        v_in = Landed(sem("v_in"), KW)
        y_out = Landed(sem("y_out"))
        got_q = [Landed(sem(f"got_{q}"), QJ, ahead=0) for q in range(NQ)]
        setup = sem("setup")

        val_v = Steps(sem("val_v"), "xn vals dense")
        val_s = Steps(sem("val_s"), "xT")
        val_t = Steps(sem("val_t"), "xT vals")
        place_v = Steps(sem("place_v"), "xn offs e1 sig off pos clamp spot spotw int flt "
                        "above floor frac frac0 a0 in0 w0 a1 in1 w1 wy wq flc lin rank")
        place_s = Steps(sem("place_s"), "xT exp")
        place_t = Steps(sem("place_t"), "xT offs")
        dense_v = Steps(sem("dense_v"), "apart weigh m0 m1 m2 m3 m4 m5 m6 m7 m8")
        dense_s = Steps(sem("dense_s"), "abs tent s0 s1 out")
        dense_t = Steps(sem("dense_t"), "k0 k1 k2 k3 k4 k5 k6 k7 k8 look")
        measured = sem("measured")
        gath_g = Steps(sem("gath_g"), "c0 c1")
        conv_v = Steps(sem("conv_v"), " ".join(f"m{q} r{q}" for q in range(NQ)) + " add")
        conv_t = Steps(sem("conv_t"), "T proj")
        conv_s = Steps(sem("conv_s"), "T")
        route_v = [Steps(sem(f"route{n}_v"), "stats aggr eps rstd xn lg max neg eqd first hot rsum pos taken "
                         "kept gate") for n in range(2)]
        route_s = [Steps(sem(f"route{n}_s"), "std xT exp gT b2") for n in range(2)]
        route_t = [Steps(sem(f"route{n}_t"), "xT lg cum gT b2") for n in range(2)]
        exp_v = Steps(sem("exp_v"), "a0 a1 a2 a3 a4 a5 a6 a7 fin clip fpart hi sign x1 x2")
        exp_s = Steps(sem("exp_s"), "h0 h1 h2 h3 h4 h5 h6 h7")
        exp_t = Steps(sem("exp_t"), "z0 z1 y0 z2 y1 z3 y2 z4 y3 z5 y4 z6 y5 z7 y6 y7")
        qkv_v = Steps(sem("qkv_v"), "stats aggr eps rstd xn q k v")
        qkv_s = Steps(sem("qkv_s"), "std xT")
        qkv_t = Steps(sem("qkv_t"), "xT qkv")
        att_v = Steps(sem("att_v"), "qbd s0 s1 max neg rsum norm o1 add")
        att_s = Steps(sem("att_s"), "exp p0 p1 o0")
        att_t = Steps(sem("att_t"), "s0 s1 p0 p1 o proj")

        passed = sem("passed")

        block = ctx.enter_context(nc.Block())

        def slots(eng, conv, route, experts, close, qkv, attend, values, places, dense):

            def slot(i, u1, u0, u0_before, ends, qk, att, e1, cv=True, val=True, place=True, apart=0):
                last = NT - 1
                placed = place if not isinstance(i, int) else 0 < i <= NT - PLEAD
                tents = cv and not (isinstance(i, int) and i == last)
                after = last if isinstance(i, int) and i - 2 > last else i - 2

                def beside_second(e):
                    if e == 0:
                        if qk:
                            close(u0_before, 0, i - 2)
                        if e1:
                            route("gate", 1, i - 4)
                        if ends:
                            conv("turn", i - 1, i - 1 + PLEAD if placed else last)
                    if e == 1:
                        if ends:
                            conv("project", i - 1)
                            route("stats", 0, i - 1)
                        if e1:
                            route("gate_T", 1, i - 4)
                        if cv:
                            dense("make", i, range(0, 2))
                    if e == 2:
                        if qk:
                            qkv("stats", i - 2, u0_before)
                        if ends:
                            route("norm", 0, i - 1)
                        if e1:
                            route("share", 1, i - 4)
                        if cv:
                            dense("sum", i, range(0, 2), i - 4 if att else None)
                            dense("make", i, range(2, 4))
                    if e == 3:
                        if ends:
                            route("turn", 0, i - 1, u0_before)
                        if qk:
                            qkv("norm", i - 2)
                        if cv:
                            dense("sum", i, range(2, 4))
                            dense("make", i, range(4, 5))
                        if placed:
                            places("places", i - 1 + PLEAD)
                    if e == 4:
                        if ends:
                            route("logits", 0, i - 1, u0_before)
                        if qk:
                            qkv("turn", i - 2)
                        if placed:
                            places("corners", i - 1 + PLEAD)
                        if val:
                            values("norm", i + LEAD)
                        if place:
                            places("norm", i + PLEAD)
                        if cv:
                            dense("sum", i, range(4, 5))
                            dense("make", i, range(5, 7))
                    if e == 5:
                        if ends:
                            route("gate", 0, i - 1)
                        if qk:
                            qkv("project", i - 2)
                        if cv:
                            dense("sum", i, range(5, 7))
                            dense("make", i, range(7, 9))
                    if e == 6:
                        if ends:
                            route("gate_T", 0, i - 1)
                        if cv:
                            conv(0, i)
                            dense("sum", i, range(7, 9))
                            dense("copy", i)
                    if e == 7:
                        if ends:
                            route("share", 0, i - 1)
                        if cv:
                            conv(1, i)
                            dense("look", i)

                def beside_first(e):
                    if e == 0:
                        if e1 and not apart:
                            close(u1, 1, i - 4)
                        if att:
                            attend("queries", i - 3, after, i if cv else last)
                        if val:
                            values("turn", i + LEAD, i - 1 if ends else None)
                        if cv:
                            conv(2, i)
                    if e == 1:
                        if att:
                            attend("scores", i - 3)
                        if val:
                            values("values", i + LEAD)
                        if cv:
                            conv(3, i)
                    if e == 2:
                        if att:
                            attend("weights", i - 3)
                        if place:
                            places("turn", i + PLEAD, (i + LEAD if val else last, i - 1))
                        if cv:
                            conv(4, i)
                    if e == 3:
                        if att:
                            attend("turn", i - 3)
                        if place:
                            places("offsets", i + PLEAD)
                        if cv:
                            conv(5, i)
                    if e == 4:
                        if att:
                            attend("values", i - 3)
                    if e == 5:
                        if att:
                            attend("project", i - 3)
                            route("stats", 1, i - 3)
                    if e == 6:
                        if att:
                            route("norm", 1, i - 3)
                            route("turn", 1, i - 3, u1, after)
                        if tents:
                            dense("apart", i + 1)
                    if e == 7:
                        if att:
                            route("logits", 1, i - 3, u1)
                        if cv:
                            conv(6, i)
                        if tents:
                            dense("weigh", i + 1)

                if apart:
                    def beside(e):
                        beside_second(e)
                        if e >= apart - 1:
                            beside_first(e - (apart - 1))

                    experts(u1, 1, i - 4, beside)
                    for e in range(E - (apart - 1), E):
                        beside_first(e)
                    close(u1, 1, i - 4)
                    return
                if e1:
                    experts(u1, 1, i - 4, beside_second)
                else:
                    for e in range(E):
                        beside_second(e)
                if ends:
                    experts(u0, 0, i - 1, beside_first)
                else:
                    for e in range(E):
                        beside_first(e)

            for i in range(4):
                slot(i, 1, i - 1, i - 2, ends=i > 0, qk=i > 1, att=i > 2, e1=False)
            with eng.Fori(4, NT - LEAD) as i:
                slot(i, i * 2 - 5, i * 2 - 4, i * 2 - 6, True, True, True, True)
            with eng.Fori(NT - LEAD, NT - PLEAD) as i:
                slot(i, i * 2 - 5, i * 2 - 4, i * 2 - 6, True, True, True, True, val=False)
            for i in range(NT - PLEAD, NT):
                slot(i, i * 2 - 5, i * 2 - 4, i * 2 - 6, True, True, True, True, val=False, place=False)
            u = 2 * NT - 5
            slot(NT, u, u + 1, u - 1, True, True, True, True, cv=False, val=False, place=False)
            slot(NT + 1, u + 2, None, u + 1, False, True, True, True, cv=False, val=False, place=False, apart=7)
            slot(NT + 2, u + 3, None, None, False, False, True, True, cv=False, val=False, place=False, apart=1)
            slot(NT + 3, u + 4, None, None, False, False, False, True, cv=False, val=False, place=False, apart=8)

        CONSTS = 0

        @block.sync
        def _(sp):
            nonlocal CONSTS
            for landed in (values_out, v_out, v_in, y_out):
                landed.begin(sp)
            xv = x.rearrange("b h w d -> (b h w) d").rearrange("(t p) d -> p t d", p=P)
            for part in range(2):
                sp.dma_start(X[:, part * SOON:(part + 1) * SOON, :], xv[:, part * SOON:(part + 1) * SOON, :])\
                    .then_inc(x_in[part], 16)
                if part == 0:
                    for dst, src in ((ident[:, :], c_ident), (wv[:, :], v_w),
                                     (vb[:, :], v_b.partition_broadcast(P))):
                        sp.dma_start(dst, src, allow_slow_non_contiguous=True).then_inc(first_in, 16)
            loads = [
                (wo[:, 0:2 * GK], qd_w), (wo[:, 2 * GK:3 * GK], qs_w), (wo[:, 3 * GK:], qw_w),
                (ob[:, 0:2 * GK], qd_b.partition_broadcast(P)),
                (ob[:, 3 * GK:], qw_b.partition_broadcast(P)),
                (sg[:, 0:G], dscale.rearrange("a b c g e f -> (a b c g e f)").partition_broadcast(P)),
                (pr[:, :], prior.rearrange("a b c e k t -> (a b c e k t)").partition_broadcast(P)),
                (pos[:, :, :], c_pos), (base[:, :, :], c_base), (iota[:, :], c_iota),
                (heads[:, :], c_heads), (dec[:, :], c_dec), (tri[:, :], c_tri),
                (ow[:, :, :], out_w.rearrange("(n p) d -> p n d", p=P)),
                (rows[:, 0, :], out_b.unsqueeze(0)), (rows[:, 1, :], bproj.unsqueeze(0)),
                (wqkv[:, :], Wqkv), (wp[:, 0, :], Wproj),
                (bq[:, :], bqkv[0:2 * D].rearrange("(n p) -> p n", p=P)),
                (bv[:, :], bqkv[2 * D:3 * D].partition_broadcast(P)),
                (bias[:, :, :, :], c_mask),
            ]
            for n, (gate_w, gate_b, m1, mb1, m2, mb2) in enumerate(moe_weights):
                loads += [
                    (gw[n][:, :], gate_w), (gb[n][:, :], gate_b.partition_broadcast(P)),
                    (w1[n][:, :, :], m1.rearrange("e d f -> d e f")),
                    (b1[n][:, :], mb1.rearrange("e (c p) -> p (e c)", p=P)),
                    (w2[n][:, :, :], m2.rearrange("e (c p) d -> p (e c) d", p=P)),
                    (b2[n][:, :], mb2),
                ]
            for dst, src in loads:
                sp.dma_start(dst, src, allow_slow_non_contiguous=True).then_inc(const_in, 16)
            CONSTS = 16 * len(loads)
            sp.wait_ge(zeros_set, 1)
            pv = patches.rearrange("(n m) f -> n m f", m=PATCHES)
            for q, at in enumerate(CORNER_AT):
                for m0, m1 in ((0, PADM - at), (PATCHES - at, PATCHES)):
                    if m1 > m0:
                        sp.dma_start(pv[:, m0:m1, q * C:(q + 1) * C],
                                     zeros[0:B * G, 0:(m1 - m0) * C].rearrange("n (m c) -> n m c", c=C))\
                            .then_inc(zeros_out, 16)
            for qi in range(BLK):
                for qj in range(BLK):
                    q = qi * BLK + qj
                    sp.dma_start(prob[q:P:BLK * BLK, 0, :].rearrange("h (a c) -> h a c", a=KW),
                                 rpb[:, HALO - qi:HALO - qi + KW, HALO - qj:HALO - qj + KW])\
                        .then_inc(rpb_in, 16)
            halo = HALO * PH * D // (B * G)
            for b in range(B):
                for r0 in (b * PH, (b + 1) * PH - HALO):
                    sp.dma_start(vpad[r0:r0 + HALO, :, :].rearrange("r w d -> (r w d)")
                                 .rearrange("(p f) -> p f", f=halo), zeros[0:B * G, 0:halo]).then_inc(zeros_out, 16)
                for w0 in (0, PH - HALO):
                    sp.dma_start(vpad[b * PH + HALO:b * PH + HALO + H, w0:w0 + HALO, :]
                                 .rearrange("r w d -> r (w d)"), zeros[0:H, 0:HALO * D]).then_inc(zeros_out, 16)

            def store_values(t):
                sp.wait_ge(*val_v.done("vals", t))
                b, m0 = t // TB, (t % TB) * P
                for q, at in enumerate(CORNER_AT):
                    dst = pv[bass.ds(b * G, G), bass.ds(m0 + (PADM - at), P), q * C:(q + 1) * C]
                    sp.dma_start(dst.rearrange("g m c -> m g c"),
                                 vsb.rearrange("p (g c) -> p g c", g=G)).then_inc(*values_out.one())

            def store_v(t):
                sp.wait_ge(*qkv_v.done("v", t))
                r = (t // TB) * PH + (t % TB) * TILE_ROWS + HALO
                for a in range(TILE_ROWS):
                    sp.dma_start(vpad[bass.ds(r + a, 1), HALO:HALO + W, :].rearrange("o w d -> (o w) d"),
                                 vt[a * W:(a + 1) * W, :]).then_inc(*v_out.one())

            windows = bass.AP(tensor=vpad.tensor, offset=0, ap=[
                [PH * D, B * PH], [D, KW], [BLK * D, NB], [1, D]])

            def load_window(t, stored):
                sp.wait_ge(*v_out.through(stored))
                sp.wait_ge(*att_t.done("o", t - 1))
                r = (t // TB) * PH + (t % TB) * TILE_ROWS
                for a in range(KW):
                    sp.dma_start(vwin[a * KW:(a + 1) * KW, :, :],
                                 windows[bass.ds(r + a, 1), :, :, :].rearrange("o c j d -> (o c) j d"))\
                        .then_inc(*v_in.one())

            yv = out.rearrange("b h w d -> (b h w) d")

            def store_out(t, u):
                sp.wait_ge(*exp_v.all(u))
                sp.dma_start(yv[bass.ds(t * P, P), :], X[:, bass.ds(t, 1), :].rearrange("p o d -> p (o d)"))\
                    .then_inc(*y_out.one())

            with sp.Fori(0, LEAD) as t:
                store_values(t)

            def slot(i, u1, qk, att, e1, val=True):
                if qk:
                    store_v(i - 2)
                if att:
                    load_window(i - 3, i - 2 if not isinstance(i, int) or i - 2 < NT else NT - 1)
                if e1:
                    store_out(i - 4, u1)
                if val:
                    store_values(i + LEAD)

            for i in range(4):
                slot(i, None, i > 1, i > 2, False)
            with sp.Fori(4, NT - LEAD) as i:
                slot(i, i * 2 - 5, True, True, True)
            with sp.Fori(NT - LEAD, NT + 1) as i:
                slot(i, i * 2 - 5, True, True, True, val=False)
            u = 2 * NT - 5
            store_v(NT - 1)
            load_window(NT - 2, NT - 1)
            store_out(NT - 3, u + 2)
            load_window(NT - 1, NT - 1)
            store_out(NT - 2, u + 3)
            store_out(NT - 1, u + 4)
            sp.wait_ge(*y_out.through(NT - 1))

        @block.gpsimd
        def _(pool):
            gath_g.begin(pool)
            pool.memset(zeros, 0.0).then_inc(zeros_set, 1)
            pool.wait_ge(zeros_out, 16 * (6 + 4 * B))
            parts = (range(0, NQ - 1), range(NQ - 1, NQ))
            for b in range(B):
                pool.wait_ge(*values_out.through(b * TB + TB - 1))
                table = patches[0:(b + 1) * G * PATCHES, :]
                with pool.Fori(b * TB, (b + 1) * TB) as t:
                    pool.wait_ge(*place_v.done("rank", t))
                    for k, groups in enumerate(parts):
                        if k == 1:
                            pool.wait_ge(*conv_v.done(f"r{NQ - 1}", t - 1))
                        j0, j1 = groups[0] * QJ, (groups[-1] + 1) * QJ
                        rt = rank[:, bass.ds(t % SRING, 1), j0:j1].rearrange("p o j -> p (o j)")
                        pool.tensor_copy(ranks[:, groups[0]:groups[-1] + 1, :].rearrange("p q j -> p (q j)"), rt)\
                            .then_inc(*gath_g.step(f"c{k}"))
                        pool.wait_ge(*gath_g.done(f"c{k}", t))
                        for q in groups:
                            pool.wait_ge(*conv_v.done(f"r{q}", t - 1))
                            pool.sem_inc(passed, 1)
                            for j in range(QJ):
                                pool.indirect_dma_start(
                                    out=got[:, q, j * PATCH:(j + 1) * PATCH], out_offset=None, in_=table,
                                    in_offset=bass.IndirectOffsetOnAxis(ap=ranks[:, q, j:j + 1], axis=0),
                                ).then_inc(*got_q[q].one())
                    for q in parts[0]:
                        pool.wait_ge(*got_q[q].through(t))

        @block.vector
        def _(v):
            for s in (val_v, place_v, dense_v, conv_v, *route_v, exp_v, qkv_v, att_v):
                s.begin(v)
            def values(part, t, before=None):
                d, s = val_v.done, val_v.step
                if part == "norm":
                    xt = X[:, bass.ds(t, 1), :].rearrange("p o d -> p (o d)")
                    v.wait_ge(*val_t.done("xT", t - 1))
                    v.tensor_scalar(xn_p, xt, mv_p[:, bass.ds(t, 1), 0:1].rearrange("p o a -> p (o a)"),
                                    rs_p[:, bass.ds(t, 1)], ALU.subtract, ALU.mult).then_inc(*s("xn"))
                if part == "values":
                    v.wait_ge(*val_t.done("vals", t))
                    v.wait_ge(*values_out.through(t - 1))
                    v.tensor_tensor(vsb, CV[:, P:P + VW],
                                    vb[:, :], ALU.add).then_inc(*s("vals"))
                    v.tensor_tensor(v_dense[:, bass.ds(t, 1), :].rearrange("p o f -> p (o f)"),
                                    CV[:, P + DG * C:P + VW], vb[:, DG * C:VW], ALU.add).then_inc(*s("dense"))

            def places(part, t, before=None):
                d, s = place_v.done, place_v.step
                if part == "norm":
                    xt = X[:, bass.ds(t, 1), :].rearrange("p o d -> p (o d)")
                    v.wait_ge(*place_t.done("xT", t - 1))
                    v.tensor_scalar(xn_o, xt, mv_p[:, bass.ds(t, 1), 0:1].rearrange("p o a -> p (o a)"),
                                    rs_p[:, bass.ds(t, 1)], ALU.subtract, ALU.mult).then_inc(*s("xn"))
                if part == "offsets":
                    v.wait_ge(*place_t.done("offs", t))
                    v.tensor_tensor(osb, CV[:, 0:OFFW], ob[:, :], ALU.add).then_inc(*s("offs"))
                if part == "places":
                    v.wait_ge(*place_s.done("exp", t))
                    v.tensor_scalar(sg, sg, 1.0, None, ALU.add).then_inc(*s("e1"))
                    v.wait_ge(*d("e1", t))
                    v.reciprocal(sg, sg).then_inc(*s("sig"))
                    v.wait_ge(*d("sig", t))
                    v.scalar_tensor_tensor(out=pp.rearrange("p (a j) -> p j a", a=2),
                                           in0=osb[:, 0:2 * GK].rearrange("p (j a) -> p j a", a=2),
                                           scalar=MAX_SCALE, in1=sg.unsqueeze(2).to_broadcast([P, GK, 2]),
                                           op0=ALU.mult, op1=ALU.mult).then_inc(*s("off"))
                    v.wait_ge(*d("off", t))
                    pt = pos[:, bass.ds(t, 1), :].rearrange("p o a -> p (o a)")
                    p2 = pp.rearrange("p (a j) -> p a j", a=2)
                    v.tensor_tensor(p2, p2, pt.unsqueeze(2).to_broadcast([P, 2, GK]), ALU.add).then_inc(*s("pos"))
                    v.wait_ge(*d("pos", t))
                    v.tensor_scalar(pp, pp, -2.0, float(W + 1), ALU.max, ALU.min).then_inc(*s("clamp"))
                    v.wait_ge(*d("clamp", t))
                    sp3 = spot[:, bass.ds(t % SRING, 1), :, :].rearrange("p o a k -> p (o a) k")
                    v.tensor_scalar(sp3[:, 0:2, :], p2[:, :, DG * K:GK], 1.0, None, ALU.mult).then_inc(*s("spot"))
                    v.tensor_scalar(sp3[:, 2:3, :], osb[:, 3 * GK + DG * K:4 * GK].unsqueeze(1), 1.0, None,
                                    ALU.mult).then_inc(*s("spotw"))
                    v.tensor_copy(pint, pp).then_inc(*s("int"))
                    v.wait_ge(*d("int", t))
                    v.tensor_copy(fl, pint).then_inc(*s("flt"))
                    v.wait_ge(*d("flt", t))
                    v.tensor_tensor(tmp, fl, pp, ALU.is_gt).then_inc(*s("above"))
                    v.wait_ge(*d("above", t))
                    v.tensor_tensor(fl, fl, tmp, ALU.subtract).then_inc(*s("floor"))
                    v.wait_ge(*d("floor", t))
                    v.tensor_tensor(fr, pp, fl, ALU.subtract).then_inc(*s("frac"))
                    v.wait_ge(*d("frac", t))
                    v.tensor_scalar(fr0, fr, -1.0, 1.0, ALU.mult, ALU.add).then_inc(*s("frac0"))
                if part == "corners":
                    w0, w1_ = wlin[:, 0:2 * GK], wlin[:, 2 * GK:4 * GK]
                    v.tensor_scalar(tmp, fl, float(W - 1), None, ALU.is_le).then_inc(*s("a0"))
                    v.wait_ge(*d("a0", t))
                    v.scalar_tensor_tensor(out=tmp, in0=fl, scalar=0.0, in1=tmp, op0=ALU.is_ge, op1=ALU.mult)\
                        .then_inc(*s("in0"))
                    v.wait_ge(*d("in0", t))
                    v.tensor_tensor(w0, tmp, fr0, ALU.mult).then_inc(*s("w0"))
                    v.wait_ge(*d("w0", t))
                    v.tensor_scalar(tmp, fl, float(W - 2), None, ALU.is_le).then_inc(*s("a1"))
                    v.wait_ge(*d("a1", t))
                    v.scalar_tensor_tensor(out=tmp, in0=fl, scalar=-1.0, in1=tmp, op0=ALU.is_ge, op1=ALU.mult)\
                        .then_inc(*s("in1"))
                    v.wait_ge(*d("in1", t))
                    v.tensor_tensor(w1_, tmp, fr, ALU.mult).then_inc(*s("w1"))
                    v.wait_ge(*d("w1", t))
                    wl = wlin.rearrange("p (s a j) -> p s a j", s=2, a=2)
                    wy3 = wyw.rearrange("p (s j) -> p s j", s=2)
                    v.tensor_tensor(wy3, wl[:, :, 1, :], osb[:, 3 * GK:4 * GK].unsqueeze(1).to_broadcast([P, 2, GK]),
                                    ALU.mult).then_inc(*s("wy"))
                    v.wait_ge(*d("wy", t))
                    w4 = wq[:, bass.ds(t % SRING, 1), :].rearrange("p o f -> p (o f)")
                    v.tensor_tensor(w4.rearrange("p (j y x) -> p j y x", y=2, x=2),
                                    wyw.rearrange("p (y j) -> p j y", y=2).unsqueeze(3)
                                    .to_broadcast([P, GK, 2, 2]),
                                    wl[:, :, 0, :].rearrange("p x j -> p j x").unsqueeze(2)
                                    .to_broadcast([P, GK, 2, 2]), ALU.mult).then_inc(*s("wq"))
                    v.tensor_scalar(tmp, fl, -1.0, float(W - 1), ALU.max, ALU.min).then_inc(*s("flc"))
                    v.wait_ge(*d("flc", t))
                    v.scalar_tensor_tensor(out=fr0[:, 0:GK], in0=tmp[:, GK:2 * GK], scalar=float(W),
                                           in1=tmp[:, 0:GK], op0=ALU.mult, op1=ALU.add).then_inc(*s("lin"))
                    v.wait_ge(*d("lin", t))
                    bs = base[:, bass.ds(t // TB, 1), :].rearrange("p o g -> p (o g)")
                    rt = rank[:, bass.ds(t % SRING, 1), :].rearrange("p o j -> p (o j)")
                    v.tensor_tensor(rt.rearrange("p (g k) -> p g k", g=G),
                                    fr0[:, 0:GK].rearrange("p (g k) -> p g k", g=G),
                                    bs.unsqueeze(2).to_broadcast([P, G, K]), ALU.add).then_inc(*s("rank"))


            def dense(part, t, ks=(), before=None):
                d, s = dense_v.done, dense_v.step
                if part == "apart":
                    sp3 = spot[:, bass.ds(t % SRING, 1), 0:2, :].rearrange("p o a k -> p (o a) k")
                    v.wait_ge(*d("m8", t - 1))
                    v.tensor_tensor(tent[:, :, :, :].rearrange("p a k w -> p (a k) w"),
                                    iota[:, :].unsqueeze(1).to_broadcast([P, 2 * K, W]),
                                    sp3.rearrange("p a k -> p (a k)").unsqueeze(2).to_broadcast([P, 2 * K, W]),
                                    ALU.subtract).then_inc(*s("apart"))
                if part == "weigh":
                    v.wait_ge(*dense_s.done("tent", t))
                    wt = spot[:, bass.ds(t % SRING, 1), 2:3, :].rearrange("p o a k -> p (o a k)")
                    v.tensor_tensor(tent[:, 1, :, :], tent[:, 1, :, :],
                                    wt.unsqueeze(2).to_broadcast([P, K, W]), ALU.mult).then_inc(*s("weigh"))
                if part == "make":
                    for k in ks:
                        v.wait_ge(*(dense_t.done(f"k{k - MADE}", t) if k >= MADE else
                                    dense_t.done(f"k{k - MADE + K}", t - 1)))
                        if k == 0:
                            v.wait_ge(*d("weigh", t))
                        v.tensor_tensor(made[:, k % MADE, :].rearrange("p (y x) -> p y x", y=H),
                                        tent[:, 1, k, :].unsqueeze(2).to_broadcast([P, H, W]),
                                        tent[:, 0, k, :].unsqueeze(1).to_broadcast([P, H, W]), ALU.mult)\
                            .then_inc(*s(f"m{k}"))

            def measure(t0, t1, first):
                v.wait_ge(x_in[t0 // SOON], 16)
                for t in range(t0, t1):
                    v.bn_stats(st_p[:, t, :], X[:, t, :]).then_inc(measured, 1)
                n = t1 - t0
                for t in range(t0, t1):
                    v.wait_ge(measured, first + t - t0 + 1)
                    v.bn_aggr(mv_p[:, t, :], st_p[:, t, :]).then_inc(measured, 1)
                v.wait_ge(measured, first + 2 * n)
                v.tensor_scalar(rs_p[:, t0:t1], mv_p[:, t0:t1, 1:2].rearrange("p t a -> p (t a)"), 1e-6, None,
                                ALU.add).then_inc(measured, 1)
                v.wait_ge(measured, first + 2 * n + 2)
                v.reciprocal(rs_p[:, t0:t1], rs_p[:, t0:t1]).then_inc(measured, 1)
                v.wait_ge(measured, first + 2 * n + 3)

            measure(0, SOON, 0)
            v.wait_ge(first_in, 16 * 3)
            with v.Fori(0, LEAD) as t:
                for part in VALUES:
                    values(part, t)
            v.memset(KT[:, :, :], 0.0).then_inc(setup, 1)
            v.memset(ones[:, :], 1.0).then_inc(setup, 1)
            for n in range(2):
                v.memset(taken[n][:, :], 0.0).then_inc(setup, 1)
            v.wait_ge(const_in, CONSTS)
            v.tensor_tensor(ob[:, 0:2 * GK].rearrange("p (g k) -> p g k", g=G),
                            ob[:, 0:2 * GK].rearrange("p (g k) -> p g k", g=G),
                            pr[:, :].unsqueeze(1).to_broadcast([P, G, 2 * K]), ALU.add).then_inc(setup, 1)
            v.tensor_scalar(ob[:, 2 * GK:3 * GK].rearrange("p (g k) -> p g k", g=G),
                            sg[:, 0:G].unsqueeze(2).to_broadcast([P, G, K]), 1.0, None, ALU.mult)\
                .then_inc(setup, 1)
            for h in range(NH - 1, -1, -1):
                v.wait_ge(setup, 6 + (NH - 1 - h))
                v.tensor_scalar(wp[:, h, :], wp[:, 0, :], heads[:, h:h + 1], None, ALU.mult).then_inc(setup, 1)
            v.wait_ge(rpb_in, 16 * BLK * BLK)
            bt = bias[:, :, :, :].rearrange("p t j k -> p (t j) k")
            v.tensor_tensor(bt, bt, prob[:, 0:1, :].to_broadcast([P, 9, KK]), ALU.add).then_inc(setup, 1)
            v.wait_ge(setup, 7 + NH)

            for t in range(PLEAD):
                for part in PLACES:
                    places(part, t)
            dense("apart", 0)
            dense("weigh", 0)
            measure(SOON, NT, 2 * SOON + 3)

            def conv(part, t, placed=None):
                d, s = conv_v.done, conv_v.step
                if isinstance(part, int):
                    q = part
                    if q == 0:
                        v.wait_ge(*place_v.done("wq", t))
                        v.wait_ge(*conv_t.done("T", t - 1))
                    g3 = got[:, q, :].rearrange("p (j c) -> p j c", c=C)
                    wj = wq[:, bass.ds(t % SRING, 1), q * QJ * CORNERS:(q + 1) * QJ * CORNERS]\
                        .rearrange("p o f -> p (o f)")
                    v.wait_ge(*got_q[q].through(t))
                    v.tensor_tensor(g3, g3, wj.unsqueeze(2).to_broadcast([P, QJ * CORNERS, C]), ALU.mult)\
                        .then_inc(*s(f"m{q}"))
                    v.wait_ge(*d(f"m{q}", t))
                    v.tensor_reduce(summed[:, q * C:(q + 1) * C],
                                    got[:, q, :].rearrange("p (j c) -> p c j", c=C), AX.X, ALU.add)\
                        .then_inc(*s(f"r{q}"))
                if part == "project":
                    xt = X[:, bass.ds(t, 1), :].rearrange("p o d -> p (o d)")
                    v.wait_ge(*conv_t.done("proj", t))
                    v.tensor_tensor(xt, CV[:, 256:384], xt, ALU.add).then_inc(*s("add"))

            def route(part, n, t, freed=None, after=None):
                d, s = route_v[n].done, route_v[n].step
                xt = X[:, bass.ds(t, 1), :].rearrange("p o d -> p (o d)")
                lg, eqd, hot, ps, kept, gate = (route_b[n][:, k, :] for k in range(6))
                if part == "stats":
                    v.wait_ge(*(conv_v, att_v)[n].all(t))
                    v.sem_inc(passed, 1)
                    v.bn_stats(st_m[:, :], xt).then_inc(*s("stats"))
                    v.wait_ge(*d("stats", t))
                    v.sem_inc(passed, 1)
                    v.bn_aggr(mv_m[:, :], st_m[:, :]).then_inc(*s("aggr"))
                    v.wait_ge(*d("aggr", t))
                    v.tensor_scalar(sd_m[:, 0:1], mv_m[:, 1:2], 1e-5, None, ALU.add).then_inc(*s("eps"))
                if part == "norm":
                    v.wait_ge(*route_s[n].done("std", t))
                    v.reciprocal(rs_m[:, :], sd_m[:, 1:2]).then_inc(*s("rstd"))
                    v.wait_ge(*d("rstd", t))
                    v.tensor_scalar(xn_m[n][:, :], xt, mv_m[:, 0:1], rs_m[:, 0:1], ALU.subtract, ALU.mult)\
                        .then_inc(*s("xn"))
                if part == "logits":
                    v.wait_ge(*route_t[n].done("lg", t))
                    v.tensor_tensor(lg, RB[n][:, 128:136], gb[n][:, :], ALU.add).then_inc(*s("lg"))
                    v.wait_ge(*d("lg", t))
                    v.tensor_reduce(small[n][:, 0:1], lg, AX.X, ALU.max).then_inc(*s("max"))
                    v.wait_ge(*d("max", t))
                    v.tensor_scalar(small[n][:, 1:2], small[n][:, 0:1], -1.0, None, ALU.mult).then_inc(*s("neg"))
                    v.scalar_tensor_tensor(out=eqd, in0=lg, scalar=small[n][:, 0:1], in1=dec[:, :],
                                           op0=ALU.is_equal, op1=ALU.mult).then_inc(*s("eqd"))
                    v.wait_ge(*d("eqd", t))
                    v.tensor_reduce(small[n][:, 2:3], eqd, AX.X, ALU.max).then_inc(*s("first"))
                    v.wait_ge(*d("first", t))
                    v.tensor_scalar(hot, eqd, small[n][:, 2:3], None, ALU.is_equal).then_inc(*s("hot"))
                if part == "gate":
                    v.wait_ge(*route_s[n].done("exp", t))
                    v.reciprocal(small[n][:, 4:5], small[n][:, 3:4]).then_inc(*s("rsum"))
                    v.wait_ge(*route_t[n].done("cum", t))
                    v.tensor_tensor(ps, RB[n][:, 136:144], taken[n][:, :], ALU.add).then_inc(*s("pos"))
                    v.wait_ge(*d("pos", t))
                    v.tensor_tensor(taken[n][:, :], RB[n][:, 144:152], taken[n][:, :], ALU.add)\
                        .then_inc(*s("taken"))
                    v.scalar_tensor_tensor(out=kept, in0=ps, scalar=float(CAPACITY), in1=hot,
                                           op0=ALU.is_le, op1=ALU.mult).then_inc(*s("kept"))
                    v.wait_ge(*d("kept", t))
                    v.tensor_scalar(gate, kept, small[n][:, 4:5], None, ALU.mult).then_inc(*s("gate"))

            def add_up(u, n, t, e0, e1):
                d, s = exp_v.done, exp_v.step
                gate = route_b[n][:, 5, :]
                v.wait_ge(*exp_t.done(f"y{e1 - 1}", u))
                for e in range(e0, e1):
                    so_far = acc
                    if e == 0:
                        v.wait_ge(*route_v[n].done("gate", t))
                        v.wait_ge(*route_s[n].done("b2", t))
                        v.wait_ge(*exp_v.all(u - 1))
                        so_far = share[n]
                    else:
                        v.wait_ge(*d(f"a{e - 1}", u))
                    v.scalar_tensor_tensor(out=acc[:, :], in0=Y[e // 4][:, (e % 4) * D:(e % 4 + 1) * D],
                                           scalar=gate[:, e:e + 1], in1=so_far[:, :],
                                           op0=ALU.mult, op1=ALU.add).then_inc(*s(f"a{e}"))

            def experts(u, n, t, beside):
                for e in range(E):
                    beside(e)
                    if e == 4:
                        add_up(u, n, t, 0, 4)

            def close(u, n, t):
                d, s = exp_v.done, exp_v.step
                xt = X[:, bass.ds(t, 1), :].rearrange("p o d -> p (o d)")
                add_up(u, n, t, 4, E)
                finite, clip, hi = (fin[:, k, :] for k in range(3))
                v.wait_ge(*d(f"a{E - 1}", u))
                v.tensor_scalar(finite, acc[:, :], 0.0, 0.0, ALU.mult, ALU.is_equal).then_inc(*s("fin"))
                v.tensor_scalar(clip, acc[:, :], -BIGGEST, BIGGEST, ALU.max, ALU.min).then_inc(*s("clip"))
                v.wait_ge(*d("clip", u))
                v.tensor_tensor(clip, clip, finite, ALU.mult).then_inc(*s("fpart"))
                v.tensor_scalar(hi, acc[:, :], BIGGEST, None, ALU.is_gt).then_inc(*s("hi"))
                v.wait_ge(*d("hi", u))
                v.scalar_tensor_tensor(out=hi, in0=acc[:, :], scalar=-BIGGEST, in1=hi,
                                       op0=ALU.is_lt, op1=ALU.subtract).then_inc(*s("sign"))
                v.tensor_tensor(xt, xt, clip, ALU.add).then_inc(*s("x1"))
                v.wait_ge(*d("x1", u))
                v.scalar_tensor_tensor(out=xt, in0=hi, scalar=-1e4, in1=xt,
                                       op0=ALU.mult, op1=ALU.add).then_inc(*s("x2"))

            def qkv(part, t, u=None):
                d, s = qkv_v.done, qkv_v.step
                xt = X[:, bass.ds(t, 1), :].rearrange("p o d -> p (o d)")
                if part == "stats":
                    v.wait_ge(*exp_v.all(u))
                    v.sem_inc(passed, 1)
                    v.bn_stats(st_q[:, :], xt).then_inc(*s("stats"))
                    v.wait_ge(*d("stats", t))
                    v.sem_inc(passed, 1)
                    v.bn_aggr(mv_q[:, :], st_q[:, :]).then_inc(*s("aggr"))
                    v.wait_ge(*d("aggr", t))
                    v.tensor_scalar(sd_q[:, 0:1], mv_q[:, 1:2], 1e-6, None, ALU.add).then_inc(*s("eps"))
                if part == "norm":
                    v.wait_ge(*qkv_s.done("std", t))
                    v.reciprocal(rs_q[:, :], sd_q[:, 1:2]).then_inc(*s("rstd"))
                    v.wait_ge(*d("rstd", t))
                    v.tensor_scalar(xn_q[:, :], xt, mv_q[:, 0:1], rs_q[:, 0:1], ALU.subtract, ALU.mult)\
                        .then_inc(*s("xn"))
                if part == "project":
                    r = t % QRING
                    v.wait_ge(*qkv_t.done("qkv", t))
                    v.tensor_scalar(QT[:, bass.ds(r, 1), :, :].rearrange("p o j (a c) -> p (o a) j c", a=BLK),
                                    M[:, 128:256].rearrange("p (a j c) -> p a j c", a=BLK, j=NB),
                                    bq[:, 0:1], HD ** -0.5, ALU.add, ALU.mult).then_inc(*s("q"))
                    kr = (t // TB) % RING * PH + (t % TB) * TILE_ROWS + HALO
                    v.tensor_scalar(KT[:, bass.ds(kr, TILE_ROWS), HALO:HALO + W],
                                    M[:, 256:384].rearrange("p (a w) -> p a w", a=TILE_ROWS),
                                    bq[:, 1:2], None, ALU.add).then_inc(*s("k"))
                    v.wait_ge(*v_out.through(t - 1))
                    v.tensor_tensor(vt[:, :], M[:, 384:512], bv[:, :], ALU.add).then_inc(*s("v"))

            def attend(part, t, after=None, looked=None):
                d, s = att_v.done, att_v.step
                if part == "queries":
                    v.wait_ge(*att_t.done("s1", t - 1))
                    v.wait_ge(*dense_t.done("look", looked))
                    v.tensor_tensor(qbd, QT[:, bass.ds(t % QRING, 1), :, :].rearrange("p o j q -> p (o j) q")
                                    .unsqueeze(2).to_broadcast([P, NB, NH, BLK * BLK]),
                                    heads[:, :].unsqueeze(1).unsqueeze(3).to_broadcast([P, NB, NH, BLK * BLK]),
                                    ALU.mult).then_inc(*s("qbd"))
                if part == "scores":
                    row = (t % TB + (TB - 1)) // TB + (t % TB + 1) // TB
                    bt = bias[:, bass.ds(row, 1), :, :].rearrange("p o j k -> p (o j) k")
                    for k, blocks in enumerate((((0, 1, 0), (1, 4, 1)), ((4, 7, 1), (7, 8, 2)))):
                        v.wait_ge(*att_t.done(f"s{k}", t))
                        for j0, j1, kind in blocks:
                            a, b = (j0 % 4) * P, (j0 % 4 + j1 - j0) * P
                            ins = v.tensor_tensor(
                                prob[:, j0:j1, :],
                                N[k][:, a:b].rearrange("p (j k) -> p j k", k=P)[:, :, 0:KK],
                                bt[:, kind:kind + 1, :].to_broadcast([P, j1 - j0, KK]), ALU.add)
                        ins.then_inc(*s(f"s{k}"))
                    v.wait_ge(*d("s1", t))
                    v.tensor_reduce(soft[:, 0, :], prob, AX.X, ALU.max).then_inc(*s("max"))
                    v.wait_ge(*d("max", t))
                    v.tensor_scalar(soft[:, 1, :], soft[:, 0, :], -1.0, None, ALU.mult).then_inc(*s("neg"))
                if part == "weights":
                    v.wait_ge(*att_s.done("exp", t))
                    v.reciprocal(soft[:, 3, :], soft[:, 2, :]).then_inc(*s("rsum"))
                    v.wait_ge(*d("rsum", t))
                    v.tensor_tensor(prob, prob, soft[:, 3, :].unsqueeze(2).to_broadcast([P, NB, KK]), ALU.mult)\
                        .then_inc(*s("norm"))
                if part == "values":
                    v.wait_ge(*att_t.done("o", t))
                    v.tensor_copy(OT[:, 4:8, :].rearrange("p h n -> p (h n)"), N[1][:, :]).then_inc(*s("o1"))
                if part == "project":
                    xt = X[:, bass.ds(t, 1), :].rearrange("p o d -> p (o d)")
                    v.wait_ge(*att_t.done("proj", t))
                    v.tensor_tensor(xt, N[0][:, 0:D], xt, ALU.add).then_inc(*s("add"))

            slots(v, conv, route, experts, close, qkv, attend, values, places, dense)

        @block.scalar
        def _(a):
            for s in (val_s, place_s, dense_s, conv_s, *route_s, exp_s, qkv_s, att_s):
                s.begin(a)

            def values(part, t, before=None):
                if part == "turn":
                    a.wait_ge(*val_t.done("xT", t))
                    a.activation(xt_p, CV[:, 0:P], ACT.Copy).then_inc(*val_s.step("xT"))

            def places(part, t, before=None):
                s = place_s.step
                if part == "turn":
                    a.wait_ge(*place_t.done("xT", t))
                    a.activation(xt_o, CV[:, 384:512], ACT.Copy).then_inc(*s("xT"))
                if part == "offsets":
                    a.wait_ge(*place_v.done("offs", t))
                    a.activation(sg, osb[:, 2 * GK:3 * GK], ACT.Exp, scale=-1.0).then_inc(*s("exp"))

            def dense(part, t, ks=(), before=None):
                s = dense_s.step
                if part == "apart":
                    a.wait_ge(*dense_v.done("apart", t))
                    flat = tent[:, :, :, :].rearrange("p a k w -> p (a k w)")
                    a.activation(flat, flat, ACT.Abs).then_inc(*s("abs"))
                    a.wait_ge(*dense_s.done("abs", t))
                    a.activation(flat, flat, ACT.Relu, scale=-1.0, bias=1.0).then_inc(*s("tent"))
                if part == "copy":
                    for k in range(2):
                        a.wait_ge(*dense_t.done("k8", t))
                        a.wait_ge(*dense_t.done("look", t - 1))
                        a.activation(spread[:, 4 * k:4 * k + 4, :].rearrange("p c q -> p (c q)"), N[k][:, :],
                                     ACT.Copy).then_inc(*s(f"s{k}"))
                if part == "look":
                    a.wait_ge(*dense_t.done("look", t))
                    a.wait_ge(*conv_t.done("T", t - 1))
                    a.activation(summed[:, DG * C:VW], N[0][:, 0:C], ACT.Copy).then_inc(*s("out"))

            def measure(t0, t1, first):
                a.wait_ge(measured, first + 2 * (t1 - t0) + 1)
                a.activation(rs_p[:, t0:t1], rs_p[:, t0:t1], ACT.Sqrt).then_inc(measured, 1)

            measure(0, SOON, 0)
            with a.Fori(0, LEAD) as t:
                for part in VALUES:
                    values(part, t)
            for t in range(PLEAD):
                for part in PLACES:
                    places(part, t)
            dense("apart", 0)
            measure(SOON, NT, 2 * SOON + 3)

            def conv(part, t, placed=None):
                if part == "turn":
                    a.wait_ge(*conv_t.done("T", t))
                    a.activation(summed_T[:, :, :].rearrange("p n q -> p (n q)"), CV[:, 0:256], ACT.Copy)\
                        .then_inc(*conv_s.step("T"))

            def route(part, n, t, freed=None, after=None):
                s = route_s[n].step
                if part == "stats":
                    a.wait_ge(*route_v[n].done("eps", t))
                    a.activation(sd_m[:, 1:2], sd_m[:, 0:1], ACT.Sqrt).then_inc(*s("std"))
                if part == "turn":
                    a.wait_ge(*route_t[n].done("xT", t))
                    a.wait_ge(*exp_t.done("z7", freed))
                    a.activation(xt_m[n][:, :], RB[n][:, 0:P], ACT.Copy).then_inc(*s("xT"))
                if part == "logits":
                    a.wait_ge(*route_v[n].done("neg", t))
                    a.activation(route_b[n][:, 6, :], route_b[n][:, 0, :], ACT.Exp, bias=small[n][:, 1:2],
                                 accum_out=small[n][:, 3:4]).then_inc(*s("exp"))
                if part == "gate_T":
                    a.wait_ge(*route_t[n].done("gT", t))
                    a.activation(gate_T[n][:, :], RB[n][0:E, 152:280], ACT.Copy).then_inc(*s("gT"))
                if part == "share":
                    a.wait_ge(*route_t[n].done("b2", t))
                    a.activation(share[n][:, :], RB[n][:, 280:408], ACT.Copy).then_inc(*s("b2"))

            def experts(u, n, t, beside):
                def relu(e):
                    a.wait_ge(*exp_t.done(f"z{e}", u))
                    a.wait_ge(*(exp_t.done(f"y{e - 2}", u) if e >= 2 else exp_t.done(f"y{e + 6}", u - 1)))
                    for c in range(FC):
                        ins = a.activation(hid[:, e % 2, c, :], Z[e % 2][:, c * P:(c + 1) * P], ACT.Relu,
                                           bias=b1[n][:, e * FC + c:e * FC + c + 1])
                    ins.then_inc(*exp_s.step(f"h{e}"))

                relu(0)
                for e in range(E):
                    if e + 1 < E:
                        relu(e + 1)
                    beside(e)

            def close(u, n, t):
                pass

            def qkv(part, t, u=None):
                s = qkv_s.step
                if part == "stats":
                    a.wait_ge(*qkv_v.done("eps", t))
                    a.activation(sd_q[:, 1:2], sd_q[:, 0:1], ACT.Sqrt).then_inc(*s("std"))
                if part == "turn":
                    a.wait_ge(*qkv_t.done("xT", t))
                    a.activation(xt_q[:, :], M[:, 0:P], ACT.Copy).then_inc(*s("xT"))

            def attend(part, t, after=None, looked=None):
                s = att_s.step
                if part == "scores":
                    a.wait_ge(*att_v.done("neg", t))
                    for j in range(NB):
                        ins = a.activation(prob[:, j, :], prob[:, j, :], ACT.Exp, bias=soft[:, 1, j:j + 1],
                                           accum_out=soft[:, 2, j:j + 1])
                    ins.then_inc(*s("exp"))
                if part == "turn":
                    for k in range(2):
                        a.wait_ge(*att_t.done(f"p{k}", t))
                        a.activation(PT[0:KK, 4 * k:4 * k + 4, :].rearrange("p j q -> p (j q)"), N[k][0:KK, :],
                                     ACT.Copy).then_inc(*s(f"p{k}"))
                if part == "values":
                    a.wait_ge(*att_t.done("o", t))
                    a.activation(OT[:, 0:4, :].rearrange("p h n -> p (h n)"), N[0][:, :], ACT.Copy)\
                        .then_inc(*s("o0"))

            slots(a, conv, route, experts, close, qkv, attend, values, places, dense)

        @block.tensor
        def _(pe):
            for s in (val_t, place_t, dense_t, conv_t, *route_t, exp_t, qkv_t, att_t):
                s.begin(pe)
            def values(part, t, before=None):
                s = val_t.step
                if part == "turn":
                    pe.wait_ge(*val_v.done("xn", t))
                    pe.wait_ge(*val_v.done("dense", t - 1))
                    if before is not None:
                        pe.wait_ge(*route_s[0].done("b2", before))
                    pe.transpose(CV[:, 0:P], xn_p, ident[:, :]).then_inc(*s("xT"))
                if part == "values":
                    pe.wait_ge(*val_s.done("xT", t))
                    pe.matmul(CV[:, P:P + VW], xt_p, wv[:, :], start=True, stop=True).then_inc(*s("vals"))

            def places(part, t, before=None):
                s = place_t.step
                if part == "turn":
                    pe.wait_ge(*place_v.done("xn", t))
                    pe.wait_ge(*val_v.done("dense", before[0]))
                    pe.wait_ge(*place_v.done("offs", t - 1))
                    pe.wait_ge(*route_s[0].done("b2", before[1]))
                    pe.transpose(CV[:, 384:512], xn_o, ident[:, :]).then_inc(*s("xT"))
                if part == "offsets":
                    pe.wait_ge(*place_s.done("xT", t))
                    pe.matmul(CV[:, 0:OFFW], xt_o, wo[:, :], start=True, stop=True).then_inc(*s("offs"))

            def dense(part, t, ks=(), before=None):
                s = dense_t.step
                if part == "sum":
                    for k in ks:
                        pe.wait_ge(*dense_v.done(f"m{k}", t))
                        if k == 0:
                            pe.wait_ge(*dense_s.done("out", t - 1))
                            if before is not None:
                                pe.wait_ge(*att_v.done("add", before))
                        for c in range(TB):
                            ins = pe.matmul(N[c // 4][:, (c % 4) * P:(c % 4 + 1) * P],
                                            made[:, k % MADE, c * P:(c + 1) * P], ident[:, :],
                                            start=(k == 0 and c % 4 == 0), stop=(k == K - 1 and c % 4 == 3))
                        ins.then_inc(*s(f"k{k}"))
                if part == "look":
                    pe.wait_ge(*dense_s.done("s1", t))
                    for c in range(TB):
                        ins = pe.matmul(N[0][:, 0:C], spread[:, c, :],
                                        v_dense[:, bass.ds(t // TB * TB + c, 1), :].rearrange("p o c -> p (o c)"),
                                        start=(c == 0), stop=(c == TB - 1))
                    ins.then_inc(*s("look"))

            pe.wait_ge(first_in, 16 * 3)
            with pe.Fori(0, LEAD) as t:
                for part in VALUES:
                    values(part, t)
            pe.wait_ge(setup, 7 + NH)
            for t in range(PLEAD):
                for part in PLACES:
                    places(part, t, (LEAD - 1, -1))

            def conv(part, t, placed=None):
                s = conv_t.step
                if part == "turn":
                    pe.wait_ge(*conv_v.done(f"r{NQ - 1}", t))
                    pe.wait_ge(*dense_s.done("out", t))
                    pe.wait_ge(*route_s[0].done("b2", t - 1))
                    pe.wait_ge(*place_v.done("offs", placed))
                    for n in range(2):
                        ins = pe.transpose(CV[:, n * P:(n + 1) * P], summed[:, n * P:(n + 1) * P], ident[:, :])
                    ins.then_inc(*s("T"))
                if part == "project":
                    pe.wait_ge(*conv_s.done("T", t))
                    pe.matmul(CV[:, 256:384], ones[0:1, :], rows[:, 0, :], start=True, stop=False)
                    pe.matmul(CV[:, 256:384], summed_T[:, 0, :], ow[:, 0, :], start=False, stop=False)
                    pe.matmul(CV[:, 256:384], summed_T[:, 1, :], ow[:, 1, :], start=False, stop=True)\
                        .then_inc(*s("proj"))

            def route(part, n, t, freed=None, after=None):
                s = route_t[n].step
                if part == "turn":
                    pe.wait_ge(*route_v[n].done("xn", t))
                    if n == 1:
                        pe.wait_ge(*route_s[n].done("b2", t - 1))
                        pe.wait_ge(*qkv_v.done("v", after))
                    pe.transpose(RB[n][:, 0:P], xn_m[n][:, :], ident[:, :]).then_inc(*s("xT"))
                if part == "logits":
                    pe.wait_ge(*route_s[n].done("xT", t))
                    pe.matmul(RB[n][:, 128:136], xt_m[n][:, :], gw[n][:, :], start=True, stop=True)\
                        .then_inc(*s("lg"))
                if part == "gate":
                    pe.wait_ge(*route_v[n].done("hot", t))
                    hot = route_b[n][:, 2, :]
                    pe.matmul(RB[n][:, 136:144], tri[:, :], hot, start=True, stop=True)
                    pe.matmul(RB[n][:, 144:152], ones[:, :], hot, start=True, stop=True).then_inc(*s("cum"))
                if part == "gate_T":
                    pe.wait_ge(*route_v[n].done("gate", t))
                    pe.matmul(RB[n][0:E, 152:280], route_b[n][:, 5, :], ident[:, :], start=True, stop=True)\
                        .then_inc(*s("gT"))
                if part == "share":
                    pe.wait_ge(*route_s[n].done("gT", t))
                    pe.matmul(RB[n][:, 280:408], gate_T[n][:, :], b2[n][:, :], start=True, stop=True)\
                        .then_inc(*s("b2"))

            def experts(u, n, t, beside):
                s = exp_t.step

                def up(e):
                    pe.wait_ge(*(exp_s.done(f"h{e - 2}", u) if e >= 2 else exp_s.done(f"h{e + 6}", u - 1)))
                    if e == 0:
                        pe.wait_ge(*route_s[n].done("xT", t))
                    for c in range(FC):
                        ins = pe.matmul(Z[e % 2][:, c * P:(c + 1) * P], w1[n][:, e, c * P:(c + 1) * P],
                                        xt_m[n][:, :], start=True, stop=True)
                    ins.then_inc(*s(f"z{e}"))

                def down(e):
                    pe.wait_ge(*exp_s.done(f"h{e}", u))
                    if e % 4 == 0:
                        pe.wait_ge(*exp_v.done(f"a{e + 3}", u - 1))
                    for c in range(FC):
                        ins = pe.matmul(Y[e // 4][:, (e % 4) * D:(e % 4 + 1) * D], hid[:, e % 2, c, :],
                                        w2[n][:, e * FC + c, :], start=(c == 0), stop=(c == FC - 1))
                    ins.then_inc(*s(f"y{e}"))

                up(0)
                for e in range(E):
                    if e + 1 < E:
                        up(e + 1)
                    down(e)
                    beside(e)

            def close(u, n, t):
                pass

            def qkv(part, t, u=None):
                s = qkv_t.step
                if part == "turn":
                    pe.wait_ge(*qkv_v.done("xn", t))
                    pe.wait_ge(*route_s[1].done("b2", t - 2))
                    pe.transpose(M[:, 0:P], xn_q[:, :], ident[:, :]).then_inc(*s("xT"))
                if part == "project":
                    pe.wait_ge(*qkv_s.done("xT", t))
                    for n in range(2):
                        pe.matmul(M[:, (n + 1) * P:(n + 2) * P], wqkv[:, n * D:(n + 1) * D], xt_q[:, :],
                                  start=True, stop=True)
                    pe.matmul(M[:, 384:512], xt_q[:, :], wqkv[:, 2 * D:3 * D], start=True, stop=True)\
                        .then_inc(*s("qkv"))

            def attend(part, t, after=None, looked=None):
                s = att_t.step
                if part == "queries":
                    kr = (t // TB) % RING * PH + (t % TB) * TILE_ROWS
                    pe.wait_ge(*att_v.done("qbd", t))
                    pe.wait_ge(*qkv_v.done("k", after))
                    pe.wait_ge(*att_v.done("add", t - 1))
                    pe.wait_ge(*dense_s.done("out", looked))
                    for j in range(NB):
                        ins = pe.matmul(N[j // 4][:, (j % 4) * P:(j % 4) * P + KK],
                                        qbd[:, j, :, :].rearrange("p h q -> p (h q)"),
                                        KT[:, bass.ds(kr, KW), j * BLK:j * BLK + KW], start=True, stop=True)
                        if j % 4 == 3:
                            ins.then_inc(*s(f"s{j // 4}"))
                if part == "turn":
                    pe.wait_ge(*att_v.done("norm", t))
                    for j in range(NB):
                        ins = pe.transpose(N[j // 4][0:KK, (j % 4) * P:(j % 4 + 1) * P], prob[:, j, :],
                                           ident[:, :])
                        if j % 4 == 3:
                            ins.then_inc(*s(f"p{j // 4}"))
                if part == "values":
                    pe.wait_ge(*att_s.done("p1", t))
                    pe.wait_ge(*v_in.through(t))
                    for k in range(2):
                        for j in range(NB):
                            o = N[k][:, :].rearrange("p (h a w) -> p h a w", h=4, a=BLK)
                            ins = pe.matmul(o[:, :, :, j * BLK:(j + 1) * BLK], vwin[0:KK, j, :],
                                            PT[0:KK, j, k * 64:(k + 1) * 64], start=True, stop=True)
                    ins.then_inc(*s("o"))
                if part == "project":
                    pe.wait_ge(*att_v.done("o1", t))
                    pe.wait_ge(*att_s.done("o0", t))
                    pe.matmul(N[0][:, 0:D], ones[0:1, :], rows[:, 1, :], start=True, stop=False)
                    for h in range(NH):
                        ins = pe.matmul(N[0][:, 0:D], OT[:, h, :], wp[:, h, :], start=False, stop=(h == NH - 1))
                    ins.then_inc(*s("proj"))

            slots(pe, conv, route, experts, close, qkv, attend, values, places, dense)


def constants():
    p = np.arange(P)
    t = np.arange(NT)
    f = np.float32
    pos = np.zeros((P, NT, 2), f)
    pos[:, :, 0] = (p % W)[:, None]
    pos[:, :, 1] = (p // W)[:, None] + (t % TB)[None, :] * TILE_ROWS
    base = np.broadcast_to(np.arange(B * G).reshape(B, G) * PATCHES + PADM, (P, B, G)).astype(f)
    q = p % (BLK * BLK)
    a = np.arange(KW)
    ok = []
    for at, blocks in ((q // BLK, (0, 1, TB - 1)), (q % BLK, (0, 1, NB - 1))):
        first = np.array([4 * k for k in blocks])
        key = first[None, :, None] - HALO + a[None, None, :]
        start = np.clip(first[None, :] + at[:, None] - HALO, 0, H - WIN)
        ok.append((key >= start[:, :, None]) & (key < start[:, :, None] + WIN))
    mask = ok[0][:, :, None, :, None] & ok[1][:, None, :, None, :]
    return {
        "c_ident": np.eye(P, dtype=f), "c_tri": np.triu(np.ones((P, P), f)), "c_pos": pos, "c_base": base,
        "c_iota": np.broadcast_to(np.arange(W), (P, W)).astype(f),
        "c_heads": (p[:, None] // HD == np.arange(NH)[None, :]).astype(f),
        "c_dec": np.broadcast_to(np.arange(E, 0, -1).astype(f), (P, E)).copy(),
        "c_mask": np.where(mask, f(0), f(-1e30)).astype(f).reshape(P, 3, 3, KK),
    }


CONV = ["v_w", "v_b", "qd_w", "qd_b", "qs_w", "qw_w", "qw_b", "out_w", "out_b", "prior", "dscale"]
MOE = ["gate_w", "gate_b", "w1", "b1", "w2", "b2"]
ATT = ["Wqkv", "bqkv", "rpb", "Wproj", "bproj"]


def program(nc, aps, out):
    build(nc, aps["x"], *[aps[f"L0_conv_{n}"] for n in CONV],
          [[aps[f"L{k}_ffn_{n}"] for n in MOE] for k in range(2)],
          *[aps[f"L1_conv_{n}"] for n in ATT],
          *[aps[n] for n in ("c_ident", "c_tri", "c_iota", "c_pos", "c_base", "c_heads", "c_dec", "c_mask")], out)


def kernel(**inputs):
    import concourse.bacc as bacc
    from concourse.bass_utils import run_bass_kernel_spmd

    nc = bacc.Bacc("TRN2", target_bir_lowering=False, num_devices=1)
    arrays, aps = {}, {}
    for name, a in {**{k: np.asarray(v) for k, v in inputs.items()}, **constants()}.items():
        a = np.ascontiguousarray(a)
        arrays[f"in_{name}"] = a
        aps[name] = nc.dram_tensor(f"in_{name}", a.shape, mybir.dt.from_np(a.dtype), kind="ExternalInput").ap()
    out = nc.dram_tensor("out_0", (B, H, W, D), F32, kind="ExternalOutput").ap()
    program(nc, aps, out)
    r = run_bass_kernel_spmd(nc, [arrays], core_ids=[0])
    return r.results[0]["out_0"]
```

```python
from contextlib import ExitStack

import numpy as np

import concourse.bass as bass
from concourse import mybir

ALU = mybir.AluOpType
ACT = mybir.ActivationFunctionType
AX = mybir.AxisListType
F32 = mybir.dt.float32
I32 = mybir.dt.int32
U32 = mybir.dt.uint32

P = 128
B, H, W, D = 4, 32, 32, 128
TILE_ROWS = P // W
TB = H // TILE_ROWS
NT = B * TB
G, C, K = 8, 32, 9
GK = G * K
CORNERS = 4
DG = G - 1
NQ = DG
QJ = K
PATCH = CORNERS * C
PADM = W + 1
PATCHES = H * W + PADM
MAX_SCALE = 6.0
CORNER_AT = [0, 1, W, W + 1]
VW, OFFW = G * C, GK * 4
E, F = 8, 512
FC = F // P
CAPACITY = -(-5 * B * H * W // (4 * E))
BIGGEST = float(np.finfo(np.float32).max)
NH, HD, WIN = 8, 16, 7
BLK = 4
NB = W // BLK
KW = BLK + WIN - 1
KK = KW * KW
HALO = WIN // 2
PH = H + 2 * HALO
QRING = 4
LEAD = TB + 1
PLEAD = 2
SRING = 4
MADE = 3


PLACES = ("norm", "turn", "offsets", "places", "corners")


class Steps:

    def __init__(self, sem, names):
        self.sem, self.names, self.at = sem, names.split(), 0

    def begin(self, eng, begun=0):
        eng.sem_inc(self.sem, (2 + begun) * len(self.names))

    def step(self, name):
        assert self.names[self.at] == name, (self.names[self.at], name)
        self.at = (self.at + 1) % len(self.names)
        return self.sem, 1

    def done(self, name, turn):
        return self.sem, turn * len(self.names) + (2 * len(self.names) + self.names.index(name) + 1)

    def all(self, turn):
        return self.done(self.names[-1], turn)


class Landed:

    def __init__(self, sem, dmas=1, ahead=1):
        self.sem, self.dmas, self.ahead = sem, dmas, ahead

    def begin(self, eng, begun=0):
        eng.sem_inc(self.sem, 16 * self.dmas * (self.ahead + begun))

    def one(self):
        return self.sem, 16

    def through(self, turn):
        return self.sem, turn * (16 * self.dmas) + (1 + self.ahead) * 16 * self.dmas


def build(nc, x, v_w, v_b, qd_w, qd_b, qs_w, qw_w, qw_b, out_w, out_b, prior, dscale,
          moe_weights, Wqkv, bqkv, rpb, Wproj, bproj,
          c_ident, c_tri, c_iota, c_pos, c_base, c_heads, c_dec, c_mask, out):
    ctx = ExitStack()
    with ctx:
        def sb(name, shape, dt=F32):
            return ctx.enter_context(nc.sbuf_tensor(name, shape, dt))

        def sem(name):
            return ctx.enter_context(nc.semaphore(name))

        def bank(name):
            return ctx.enter_context(nc.psum_tensor(name, [P, 512], F32))

        patches = nc.dram_tensor("patches", (B * G * PATCHES, PATCH), F32, kind="Internal").ap()
        vpad = nc.dram_tensor("vpad", (B * PH, PH, D), F32, kind="Internal").ap()

        X = sb("X", [P, NT, D])
        ident = sb("ident", [P, P])
        tri = sb("tri", [P, P])
        ones = sb("ones", [P, P])
        pos = sb("pos", [P, NT, 2])
        base = sb("base", [P, B, G])
        iota = sb("iota", [P, W])
        heads = sb("heads", [P, NH])
        dec = sb("dec", [P, E])

        wv = sb("wv", [D, VW])
        wo = sb("wo", [D, OFFW])
        vb = sb("vb", [P, VW])
        ob = sb("ob", [P, OFFW])
        pr = sb("pr", [P, K * 2])
        ow = sb("ow", [P, 2, D])
        rows = sb("rows", [1, 2, D])
        w1 = [sb(f"w1_{n}", [D, E, F]) for n in range(2)]
        w2 = [sb(f"w2_{n}", [P, E * FC, D]) for n in range(2)]
        b1 = [sb(f"b1_{n}", [P, E * FC]) for n in range(2)]
        b2 = [sb(f"b2_{n}", [E, D]) for n in range(2)]
        gw = [sb(f"gw_{n}", [D, E]) for n in range(2)]
        gb = [sb(f"gb_{n}", [P, E]) for n in range(2)]
        taken = [sb(f"taken_{n}", [P, E]) for n in range(2)]
        wqkv = sb("wqkv", [D, 3 * D])
        bq = sb("bq", [P, 2])
        bv = sb("bv", [P, D])
        wp = sb("wp", [P, NH, D])
        bias = sb("bias", [P, 3, 3, KK])

        rank = sb("rank", [P, SRING, GK], U32)
        wq = sb("wq", [P, SRING, GK * CORNERS])
        spot = sb("spot", [P, SRING, 3, K])
        st_p, mv_p = sb("st_p", [P, NT, 6]), sb("mv_p", [P, NT, 2])
        rs_p = sb("rs_p", [P, NT])
        got = sb("got", [P, NQ, QJ * PATCH])
        ranks = sb("ranks", [P, NQ, QJ], U32)
        tent = sb("tent", [P, 2, K, W])
        made = sb("made", [P, MADE, H * W])
        v_dense = sb("v_dense", [P, NT, C])
        summed = sb("summed", [P, VW])
        summed_T = sb("summed_T", [P, 2, P])
        st_m, mv_m, sd_m, rs_m = sb("st_m", [P, 6]), sb("mv_m", [P, 2]), sb("sd_m", [P, 2]), sb("rs_m", [P, 1])
        st_q, mv_q, sd_q, rs_q = sb("st_q", [P, 6]), sb("mv_q", [P, 2]), sb("sd_q", [P, 2]), sb("rs_q", [P, 1])
        xn_q, xt_q = sb("xn_q", [P, D]), sb("xt_q", [D, P])
        xn_m = [sb(f"xn_m{n}", [P, D]) for n in range(2)]
        xt_m = [sb(f"xt_m{n}", [D, P]) for n in range(2)]
        route_b = [sb(f"route{n}", [P, 7, E]) for n in range(2)]
        small = [sb(f"small{n}", [P, 6]) for n in range(2)]
        gate_T = [sb(f"gate_T{n}", [E, P]) for n in range(2)]
        share = [sb(f"share{n}", [P, D]) for n in range(2)]
        hid = sb("hid", [P, 2, FC, P])
        acc = sb("acc", [P, D])
        fin = sb("fin", [P, 3, D])
        QT = sb("QT", [P, QRING, NB, BLK * BLK])
        KT = sb("KT", [P, PH, PH])
        vt = sb("vt", [P, D])
        soft = sb("soft", [P, 4, NB])
        turns = sb("turns", [P, 1024])
        qbd = turns[:, :].rearrange("p (j h q) -> p j h q", j=NB, h=NH)
        spread = turns[:, :].rearrange("p (c q) -> p c q", c=TB)
        PT = sb("PT", [P, NB, P])[:, :, :]
        OT = sb("OT", [P, NH, P])[:, :, :]
        OT_of = OT.rearrange("p h (a k w) -> p (h a) k w", a=BLK, k=2)
        vwin = sb("vwin", [P, NB, D])[:, :, :]
        prob = sb("prob", [P, NB, KK])[:, :, :]
        arena = sb("arena", [P, 4 * D + VW + OFFW + 17 * GK])
        cut = [0]

        def part(n):
            cut[0] += n
            return arena[:, cut[0] - n:cut[0]]

        xn_p, xt_p = part(D), part(P)
        xn_o, xt_o = part(D), part(P)
        vsb, osb = part(VW), part(OFFW)
        sg = part(GK)
        pp, fl, fr, fr0, tmp = (part(2 * GK) for _ in range(5))
        wlin = part(4 * GK)
        wyw = part(2 * GK)
        pint = wyw.bitcast(I32)

        first_xn = got[:, 3, :].rearrange("p (t d) -> p t d", t=LEAD)
        first_xt = got[:, 4, :].rearrange("p (t d) -> p t d", t=LEAD)
        first_vs = got[:, 1:3, :].rearrange("p q f -> p (q f)").rearrange("p (t f) -> p t f", f=VW)
        zeros = got[:, 0, 0:PATCHES]

        Z = [bank("Z0"), bank("Z1")]
        Y = [bank("Y0"), bank("Y1")]
        M = bank("M")
        N = [bank("N0"), bank("N1")]
        CV = bank("CV")
        RB = [CV, M]
        ALL = [*Z, *Y, M, *N, CV]

        x_in = [sem(f"x_in{part}") for part in range(2)]
        first_in = sem("first_in")
        place_in = sem("place_in")
        first_out = sem("first_out")
        const_in = sem("const_in")
        rpb_in = sem("rpb_in")
        edges_out = sem("edges_out")
        zeros_out = sem("zeros_out")
        zeros_set = sem("zeros_set")
        values_out = Landed(sem("values_out"), CORNERS)
        v_out = Landed(sem("v_out"), TILE_ROWS)
        v_in = Landed(sem("v_in"), KW)
        y_out = Landed(sem("y_out"))
        got_q = [Landed(sem(f"got_{q}"), QJ, ahead=0) for q in range(NQ)]
        setup = sem("setup")

        val_v = Steps(sem("val_v"), "xn vals dense")
        val_s = Steps(sem("val_s"), "xT")
        val_t = Steps(sem("val_t"), "xT vals")
        place_v = Steps(sem("place_v"), "xn offs e1 sig off pos clamp spot spotw int flt "
                        "above floor frac frac0 in0 in1 w0 w1 wy wq flc lin rank")
        place_s = Steps(sem("place_s"), "xT exp")
        place_t = Steps(sem("place_t"), "xT offs")
        dense_v = Steps(sem("dense_v"), "apart weigh m0 m1 m2 m3 m4 m5 m6 m7 m8")
        dense_s = Steps(sem("dense_s"), "abs tent s0 s1 out")
        dense_t = Steps(sem("dense_t"), "k0 k1 k2 k3 k4 k5 k6 k7 k8 look")
        ts = range(LEAD)
        first_v = Steps(sem("first_v"), " ".join([f"xn{t}" for t in ts] + [f"vals{t} dense{t}" for t in ts]))
        first_s = Steps(sem("first_s"), " ".join(f"xT{t}" for t in ts))
        first_t = Steps(sem("first_t"), " ".join([f"xT{t}" for t in ts] + [f"vals{t}" for t in ts]))
        measured = sem("measured")
        gath_g = Steps(sem("gath_g"), "c0 c1")
        conv_v = Steps(sem("conv_v"), " ".join(f"m{q} r{q}" for q in range(NQ)) + " add")
        conv_t = Steps(sem("conv_t"), "T proj")
        conv_s = Steps(sem("conv_s"), "T")
        route_v = [Steps(sem(f"route{n}_v"), "stats aggr eps rstd xn lg max neg eqd first hot rsum pos taken "
                         "kept gate") for n in range(2)]
        route_s = [Steps(sem(f"route{n}_s"), "std xT exp gT b2") for n in range(2)]
        route_t = [Steps(sem(f"route{n}_t"), "xT lg cum gT b2") for n in range(2)]
        exp_v = Steps(sem("exp_v"), "a0 a1 a2 a3 a4 a5 a6 a7 fin clip fpart hi sign x1 x2")
        exp_s = Steps(sem("exp_s"), "h0 h1 h2 h3 h4 h5 h6 h7")
        exp_t = Steps(sem("exp_t"), "z0 z1 y0 z2 y1 z3 y2 z4 y3 z5 y4 z6 y5 z7 y6 y7")
        qkv_v = Steps(sem("qkv_v"), "stats aggr eps rstd xn q k v")
        qkv_s = Steps(sem("qkv_s"), "std xT")
        qkv_t = Steps(sem("qkv_t"), "xT qkv")
        att_v = Steps(sem("att_v"), "qbd s0 s1 max neg rsum norm o1 add")
        att_s = Steps(sem("att_s"), "exp p0 p1 o0")
        att_t = Steps(sem("att_t"), "s0 s1 p0 p1 o proj")

        passed = sem("passed")

        block = ctx.enter_context(nc.Block())

        def slots(eng, conv, route, experts, close, qkv, attend, values, places, dense):

            def slot(i, u1, u0, u0_before, ends, qk, att, e1, val=True, place=True, final=False):
                last = NT - 1
                placed = place if not isinstance(i, int) else 0 < i <= NT - PLEAD
                tents = not final

                def beside_second(e):
                    if e == 0:
                        if qk:
                            close(u0_before, 0, i - 2)
                        if e1:
                            route("gate", 1, i - 4)
                        if ends:
                            conv("turn", i - 1, i - 1 + PLEAD if placed else last)
                    if e == 1:
                        if ends:
                            conv("project", i - 1)
                            route("stats", 0, i - 1)
                        if e1:
                            route("gate_T", 1, i - 4)
                        dense("make", i, range(0, 2))
                    if e == 2:
                        if qk:
                            qkv("stats", i - 2, u0_before)
                        if ends:
                            route("norm", 0, i - 1)
                        if e1:
                            route("share", 1, i - 4)
                        dense("sum", i, range(0, 2), i - 4 if att else None)
                        dense("make", i, range(2, 4))
                    if e == 3:
                        if ends:
                            route("turn", 0, i - 1, u0_before)
                        if qk:
                            qkv("norm", i - 2)
                        dense("sum", i, range(2, 4))
                        dense("make", i, range(4, 5))
                        if placed:
                            places("places", i - 1 + PLEAD)
                    if e == 4:
                        if ends:
                            route("logits", 0, i - 1, u0_before)
                        if qk:
                            qkv("turn", i - 2)
                        if placed:
                            places("corners", i - 1 + PLEAD)
                        if val:
                            values("norm", i + LEAD)
                        if place:
                            places("norm", i + PLEAD)
                        dense("sum", i, range(4, 5))
                        dense("make", i, range(5, 7))
                    if e == 5:
                        if ends:
                            route("gate", 0, i - 1)
                        if qk:
                            qkv("project", i - 2)
                        dense("sum", i, range(5, 7))
                        dense("make", i, range(7, 9))
                    if e == 6:
                        if ends:
                            route("gate_T", 0, i - 1)
                        conv(0, i)
                        dense("sum", i, range(7, 9))
                        dense("copy", i)
                    if e == 7:
                        if ends:
                            route("share", 0, i - 1)
                        conv(1, i)
                        dense("look", i)

                def beside_first(e):
                    if e == 0:
                        if e1:
                            close(u1, 1, i - 4)
                        if att:
                            attend("queries", i - 3, i - 2, i)
                        if val:
                            values("turn", i + LEAD, i - 1 if ends else None)
                        conv(2, i)
                    if e == 1:
                        if att:
                            attend("scores", i - 3)
                        if val:
                            values("values", i + LEAD)
                        conv(3, i)
                    if e == 2:
                        if att:
                            attend("weights", i - 3)
                        if place:
                            places("turn", i + PLEAD, (i + LEAD if val else last, i - 1))
                        conv(4, i)
                    if e == 3:
                        if att:
                            attend("turn", i - 3)
                        if place:
                            places("offsets", i + PLEAD)
                        conv(5, i)
                    if e == 4:
                        if att:
                            attend("values", i - 3)
                        if final:
                            conv(6, i)
                    if e == 5:
                        if att:
                            attend("project", i - 3)
                            route("stats", 1, i - 3)
                        if final:
                            conv("turn", i, last)
                    if e == 6:
                        if att:
                            route("norm", 1, i - 3)
                            route("turn", 1, i - 3, u1, i - 2)
                        if tents:
                            dense("apart", i + 1)
                        if final:
                            conv("project", i)
                            route("stats", 0, i)
                    if e == 7:
                        if att:
                            route("logits", 1, i - 3, u1)
                        if not final:
                            conv(6, i)
                        if tents:
                            dense("weigh", i + 1)
                        if final:
                            route("norm", 0, i)
                            route("turn", 0, i, u0)

                if e1:
                    experts(u1, 1, i - 4, beside_second)
                else:
                    for e in range(E):
                        beside_second(e)
                if ends:
                    experts(u0, 0, i - 1, beside_first)
                else:
                    for e in range(E):
                        beside_first(e)

            for i in range(4):
                slot(i, 1, i - 1, i - 2, ends=i > 0, qk=i > 1, att=i > 2, e1=False)
            with eng.Fori(4, NT - LEAD) as i:
                slot(i, i * 2 - 5, i * 2 - 4, i * 2 - 6, True, True, True, True)
            with eng.Fori(NT - LEAD, NT - PLEAD) as i:
                slot(i, i * 2 - 5, i * 2 - 4, i * 2 - 6, True, True, True, True, val=False)
            for i in range(NT - PLEAD, NT):
                slot(i, i * 2 - 5, i * 2 - 4, i * 2 - 6, True, True, True, True, val=False, place=False,
                     final=i == NT - 1)

            last = NT - 1
            u = 2 * NT - 5

            def beside_0(e):
                if e == 0:
                    close(u - 1, 0, last - 1)
                    route("gate", 1, last - 3)
                    route("logits", 0, last, u - 1)
                if e == 1:
                    qkv("stats", last - 1, u - 1)
                    route("gate_T", 1, last - 3)
                    route("gate", 0, last)
                if e == 2:
                    qkv("norm", last - 1)
                    route("share", 1, last - 3)
                    route("gate_T", 0, last)
                if e == 3:
                    qkv("turn", last - 1)
                    route("share", 0, last)
                if e == 4:
                    qkv("project", last - 1)
                if e == 5:
                    attend("queries", last - 2, last - 1, last)
                if e == 6:
                    attend("scores", last - 2)
                if e == 7:
                    attend("weights", last - 2)

            def beside_1(e):
                if e == 0:
                    close(u, 0, last)
                    attend("turn", last - 2)
                if e == 1:
                    qkv("stats", last, u)
                    attend("values", last - 2)
                if e == 2:
                    qkv("norm", last)
                    attend("project", last - 2)
                if e == 3:
                    route("stats", 1, last - 2)
                    qkv("turn", last, None, last - 3)
                if e == 4:
                    route("norm", 1, last - 2)
                    qkv("project", last)
                if e == 5:
                    attend("queries", last - 1, last, last)
                if e == 6:
                    route("turn", 1, last - 2, u + 1, last)
                    attend("scores", last - 1)
                if e == 7:
                    route("logits", 1, last - 2, u + 1)
                    attend("weights", last - 1)

            def beside_2(e):
                if e == 0:
                    close(u + 1, 1, last - 3)
                    route("gate", 1, last - 2)
                    attend("turn", last - 1)
                if e == 1:
                    route("gate_T", 1, last - 2)
                    attend("values", last - 1)
                if e == 2:
                    route("share", 1, last - 2)
                    attend("project", last - 1)
                if e == 3:
                    route("stats", 1, last - 1)
                    attend("queries", last, last, last)
                if e == 4:
                    route("norm", 1, last - 1)
                    attend("scores", last)
                if e == 5:
                    attend("weights", last)
                if e == 6:
                    route("turn", 1, last - 1, u + 2, last)
                    attend("turn", last)
                if e == 7:
                    route("logits", 1, last - 1, u + 2)
                    attend("values", last)

            def beside_3(e):
                if e == 0:
                    close(u + 2, 1, last - 2)
                    route("gate", 1, last - 1)
                    attend("project", last)
                if e == 1:
                    route("gate_T", 1, last - 1)
                if e == 2:
                    route("share", 1, last - 1)
                    route("stats", 1, last)
                if e == 3:
                    route("norm", 1, last)
                if e == 6:
                    route("turn", 1, last, u + 3, last)
                if e == 7:
                    route("logits", 1, last, u + 3)

            def beside_4(e):
                if e == 0:
                    close(u + 3, 1, last - 1)
                    route("gate", 1, last)
                if e == 1:
                    route("gate_T", 1, last)
                if e == 2:
                    route("share", 1, last)

            experts(u, 0, last, beside_0)
            experts(u + 1, 1, last - 3, beside_1)
            experts(u + 2, 1, last - 2, beside_2)
            experts(u + 3, 1, last - 1, beside_3)
            experts(u + 4, 1, last, beside_4)
            close(u + 4, 1, last)

        CONSTS = PLACE_CONSTS = 0

        @block.sync
        def _(sp):
            nonlocal CONSTS, PLACE_CONSTS
            values_out.begin(sp, begun=LEAD)
            for landed in (v_out, v_in, y_out):
                landed.begin(sp)
            xv = x.rearrange("b h w d -> (b h w) d").rearrange("(t p) d -> p t d", p=P)
            sp.dma_start(X[:, 0:LEAD, :], xv[:, 0:LEAD, :]).then_inc(x_in[0], 16)
            first = [(ident[:, :], c_ident), (wv[:, :], v_w), (vb[:, :], v_b.partition_broadcast(P))]
            for dst, src in first:
                sp.dma_start(dst, src, allow_slow_non_contiguous=True).then_inc(first_in, 16)
            place_loads = [
                (ob[:, 0:2 * GK], qd_b.partition_broadcast(P)),
                (ob[:, 3 * GK:], qw_b.partition_broadcast(P)),
                (sg[:, 0:G], dscale.rearrange("a b c g e f -> (a b c g e f)").partition_broadcast(P)),
                (pr[:, :], prior.rearrange("a b c e k t -> (a b c e k t)").partition_broadcast(P)),
                (wo[:, 0:2 * GK], qd_w), (wo[:, 2 * GK:3 * GK], qs_w), (wo[:, 3 * GK:], qw_w),
                (pos[:, :, :], c_pos), (base[:, :, :], c_base), (iota[:, :], c_iota),
            ]
            for dst, src in place_loads:
                sp.dma_start(dst, src, allow_slow_non_contiguous=True).then_inc(place_in, 16)
            PLACE_CONSTS = 16 * len(place_loads)
            sp.wait_ge(zeros_set, 1)
            pv = patches.rearrange("(n m) f -> n m f", m=PATCHES)
            for q, at in enumerate(CORNER_AT):
                for m0, m1 in ((0, PADM - at), (PATCHES - at, PATCHES)):
                    if m1 > m0:
                        sp.dma_start(pv[:, m0:m1, q * C:(q + 1) * C],
                                     zeros[0:B * G, 0:(m1 - m0) * C].rearrange("n (m c) -> n m c", c=C))\
                            .then_inc(edges_out, 16)
            for t in range(LEAD):
                sp.wait_ge(*first_v.done(f"vals{t}", 0))
                n0, m0 = t // TB * G, (t % TB) * P
                for q, at in enumerate(CORNER_AT):
                    dst = pv[n0:n0 + G, m0 + PADM - at:m0 + PADM - at + P, q * C:(q + 1) * C]
                    sp.dma_start(dst.rearrange("g m c -> m g c"),
                                 first_vs[:, t, :].rearrange("p (g c) -> p g c", g=G)).then_inc(first_out, 16)
            sp.dma_start(X[:, LEAD:NT, :], xv[:, LEAD:NT, :]).then_inc(x_in[1], 16)
            loads = [
                (heads[:, :], c_heads), (dec[:, :], c_dec), (tri[:, :], c_tri),
                (ow[:, :, :], out_w.rearrange("(n p) d -> p n d", p=P)),
                (rows[:, 0, :], out_b.unsqueeze(0)), (rows[:, 1, :], bproj.unsqueeze(0)),
                (wqkv[:, :], Wqkv), (wp[:, 0, :], Wproj),
                (bq[:, :], bqkv[0:2 * D].rearrange("(n p) -> p n", p=P)),
                (bv[:, :], bqkv[2 * D:3 * D].partition_broadcast(P)),
                (bias[:, :, :, :], c_mask),
            ]
            for n, (gate_w, gate_b, m1, mb1, m2, mb2) in enumerate(moe_weights):
                loads += [
                    (gw[n][:, :], gate_w), (gb[n][:, :], gate_b.partition_broadcast(P)),
                    (w1[n][:, :, :], m1.rearrange("e d f -> d e f")),
                    (b1[n][:, :], mb1.rearrange("e (c p) -> p (e c)", p=P)),
                    (w2[n][:, :, :], m2.rearrange("e (c p) d -> p (e c) d", p=P)),
                    (b2[n][:, :], mb2),
                ]
            for dst, src in loads:
                sp.dma_start(dst, src, allow_slow_non_contiguous=True).then_inc(const_in, 16)
            CONSTS = 16 * len(loads)
            for qi in range(BLK):
                for qj in range(BLK):
                    q = qi * BLK + qj
                    sp.dma_start(prob[q:P:BLK * BLK, 0, :].rearrange("h (a c) -> h a c", a=KW),
                                 rpb[:, HALO - qi:HALO - qi + KW, HALO - qj:HALO - qj + KW])\
                        .then_inc(rpb_in, 16)
            sp.wait_ge(setup, 3)
            halo_zeros = KT[:, :, :].rearrange("p a w -> p (a w)")
            halo = HALO * PH * D // (B * G)
            for b in range(B):
                for r0 in (b * PH, (b + 1) * PH - HALO):
                    sp.dma_start(vpad[r0:r0 + HALO, :, :].rearrange("r w d -> (r w d)")
                                 .rearrange("(p f) -> p f", f=halo), halo_zeros[0:B * G, 0:halo]).then_inc(zeros_out, 16)
                for w0 in (0, PH - HALO):
                    sp.dma_start(vpad[b * PH + HALO:b * PH + HALO + H, w0:w0 + HALO, :]
                                 .rearrange("r w d -> r (w d)"), halo_zeros[0:H, 0:HALO * D]).then_inc(zeros_out, 16)

            def store_values(t):
                sp.wait_ge(*val_v.done("vals", t))
                b, m0 = t // TB, (t % TB) * P
                for q, at in enumerate(CORNER_AT):
                    dst = pv[bass.ds(b * G, G), bass.ds(m0 + (PADM - at), P), q * C:(q + 1) * C]
                    sp.dma_start(dst.rearrange("g m c -> m g c"),
                                 vsb.rearrange("p (g c) -> p g c", g=G)).then_inc(*values_out.one())

            def store_v(t):
                sp.wait_ge(*qkv_v.done("v", t))
                r = (t // TB) * PH + (t % TB) * TILE_ROWS + HALO
                for a in range(TILE_ROWS):
                    sp.dma_start(vpad[bass.ds(r + a, 1), HALO:HALO + W, :].rearrange("o w d -> (o w) d"),
                                 vt[a * W:(a + 1) * W, :]).then_inc(*v_out.one())

            windows = bass.AP(tensor=vpad.tensor, offset=0, ap=[
                [PH * D, B * PH], [D, KW], [BLK * D, NB], [1, D]])

            def load_window(t, stored):
                sp.wait_ge(*v_out.through(stored))
                sp.wait_ge(*att_t.done("o", t - 1))
                r = (t // TB) * PH + (t % TB) * TILE_ROWS
                for a in range(KW):
                    sp.dma_start(vwin[a * KW:(a + 1) * KW, :, :],
                                 windows[bass.ds(r + a, 1), :, :, :].rearrange("o c j d -> (o c) j d"))\
                        .then_inc(*v_in.one())

            yv = out.rearrange("b h w d -> (b h w) d")

            def store_out(t, u):
                sp.wait_ge(*exp_v.all(u))
                sp.dma_start(yv[bass.ds(t * P, P), :], X[:, bass.ds(t, 1), :].rearrange("p o d -> p (o d)"))\
                    .then_inc(*y_out.one())

            def slot(i, u1, qk, att, e1, val=True):
                if qk:
                    store_v(i - 2)
                if att:
                    load_window(i - 3, i - 2 if not isinstance(i, int) or i - 2 < NT else NT - 1)
                if e1:
                    store_out(i - 4, u1)
                if val:
                    store_values(i + LEAD)

            for i in range(4):
                slot(i, None, i > 1, i > 2, False)
            with sp.Fori(4, NT - LEAD) as i:
                slot(i, i * 2 - 5, True, True, True)
            with sp.Fori(NT - LEAD, NT) as i:
                slot(i, i * 2 - 5, True, True, True, val=False)
            u = 2 * NT - 5
            store_v(NT - 2)
            load_window(NT - 3, NT - 2)
            store_v(NT - 1)
            load_window(NT - 2, NT - 1)
            store_out(NT - 4, u + 1)
            load_window(NT - 1, NT - 1)
            for k in range(3):
                store_out(NT - 3 + k, u + 2 + k)
            sp.wait_ge(*y_out.through(NT - 1))

        @block.gpsimd
        def _(pool):
            gath_g.begin(pool)
            pool.memset(zeros, 0.0).then_inc(zeros_set, 1)
            pool.wait_ge(edges_out, 16 * 6)
            pool.wait_ge(first_out, 16 * CORNERS * LEAD)
            parts = (range(0, NQ - 2), range(NQ - 2, NQ))
            for b in range(B):
                if b > 0:
                    pool.wait_ge(*values_out.through(b * TB + TB - 1))
                table = patches[0:(b + 1) * G * PATCHES, :]
                with pool.Fori(b * TB, (b + 1) * TB) as t:
                    pool.wait_ge(*place_v.done("rank", t))
                    for k, groups in enumerate(parts):
                        if k == 1:
                            pool.wait_ge(*conv_v.done(f"r{NQ - 1}", t - 1))
                        j0, j1 = groups[0] * QJ, (groups[-1] + 1) * QJ
                        rt = rank[:, bass.ds(t % SRING, 1), j0:j1].rearrange("p o j -> p (o j)")
                        pool.tensor_copy(ranks[:, groups[0]:groups[-1] + 1, :].rearrange("p q j -> p (q j)"), rt)\
                            .then_inc(*gath_g.step(f"c{k}"))
                        pool.wait_ge(*gath_g.done(f"c{k}", t))
                        for q in groups:
                            pool.wait_ge(*conv_v.done(f"r{q}", t - 1))
                            pool.sem_inc(passed, 1)
                            for j in range(QJ):
                                pool.indirect_dma_start(
                                    out=got[:, q, j * PATCH:(j + 1) * PATCH], out_offset=None, in_=table,
                                    in_offset=bass.IndirectOffsetOnAxis(ap=ranks[:, q, j:j + 1], axis=0),
                                ).then_inc(*got_q[q].one())
                    for q in parts[0]:
                        pool.wait_ge(*got_q[q].through(t))

        @block.vector
        def _(v):
            for s in (val_v, val_s, val_t):
                s.begin(v, begun=LEAD)
            for s in (first_v, place_v, dense_v, conv_v, *route_v, exp_v, qkv_v, att_v):
                s.begin(v)
            def values(part, t, before=None):
                d, s = val_v.done, val_v.step
                if part == "norm":
                    xt = X[:, bass.ds(t, 1), :].rearrange("p o d -> p (o d)")
                    v.wait_ge(*val_t.done("xT", t - 1))
                    v.tensor_scalar(xn_p, xt, mv_p[:, bass.ds(t, 1), 0:1].rearrange("p o a -> p (o a)"),
                                    rs_p[:, bass.ds(t, 1)], ALU.subtract, ALU.mult).then_inc(*s("xn"))
                if part == "values":
                    v.wait_ge(*val_t.done("vals", t))
                    v.wait_ge(*values_out.through(t - 1))
                    v.tensor_tensor(vsb, CV[:, P:P + VW],
                                    vb[:, :], ALU.add).then_inc(*s("vals"))
                    v.tensor_tensor(v_dense[:, bass.ds(t, 1), :].rearrange("p o f -> p (o f)"),
                                    CV[:, P + DG * C:P + VW], vb[:, DG * C:VW], ALU.add).then_inc(*s("dense"))

            def places(part, t, before=None):
                d, s = place_v.done, place_v.step
                if part == "norm":
                    xt = X[:, bass.ds(t, 1), :].rearrange("p o d -> p (o d)")
                    v.wait_ge(*place_t.done("xT", t - 1))
                    v.tensor_scalar(xn_o, xt, mv_p[:, bass.ds(t, 1), 0:1].rearrange("p o a -> p (o a)"),
                                    rs_p[:, bass.ds(t, 1)], ALU.subtract, ALU.mult).then_inc(*s("xn"))
                if part == "offsets":
                    v.wait_ge(*place_t.done("offs", t))
                    v.tensor_tensor(osb, CV[:, 0:OFFW], ob[:, :], ALU.add).then_inc(*s("offs"))
                if part == "places":
                    v.wait_ge(*place_s.done("exp", t))
                    v.tensor_scalar(sg, sg, 1.0, None, ALU.add).then_inc(*s("e1"))
                    v.wait_ge(*d("e1", t))
                    v.reciprocal(sg, sg).then_inc(*s("sig"))
                    v.wait_ge(*d("sig", t))
                    v.scalar_tensor_tensor(out=pp.rearrange("p (a j) -> p j a", a=2),
                                           in0=osb[:, 0:2 * GK].rearrange("p (j a) -> p j a", a=2),
                                           scalar=MAX_SCALE, in1=sg.unsqueeze(2).to_broadcast([P, GK, 2]),
                                           op0=ALU.mult, op1=ALU.mult).then_inc(*s("off"))
                    v.wait_ge(*d("off", t))
                    pt = pos[:, bass.ds(t, 1), :].rearrange("p o a -> p (o a)")
                    p2 = pp.rearrange("p (a j) -> p a j", a=2)
                    v.tensor_tensor(p2, p2, pt.unsqueeze(2).to_broadcast([P, 2, GK]), ALU.add).then_inc(*s("pos"))
                    v.wait_ge(*d("pos", t))
                    v.tensor_scalar(pp, pp, -2.0, float(W + 1), ALU.max, ALU.min).then_inc(*s("clamp"))
                    v.wait_ge(*d("clamp", t))
                    sp3 = spot[:, bass.ds(t % SRING, 1), :, :].rearrange("p o a k -> p (o a) k")
                    v.tensor_scalar(sp3[:, 0:2, :], p2[:, :, DG * K:GK], 1.0, None, ALU.mult).then_inc(*s("spot"))
                    v.tensor_scalar(sp3[:, 2:3, :], osb[:, 3 * GK + DG * K:4 * GK].unsqueeze(1), 1.0, None,
                                    ALU.mult).then_inc(*s("spotw"))
                    v.tensor_copy(pint, pp).then_inc(*s("int"))
                    v.wait_ge(*d("int", t))
                    v.tensor_copy(fl, pint).then_inc(*s("flt"))
                    v.wait_ge(*d("flt", t))
                    v.tensor_tensor(tmp, fl, pp, ALU.is_gt).then_inc(*s("above"))
                    v.wait_ge(*d("above", t))
                    v.tensor_tensor(fl, fl, tmp, ALU.subtract).then_inc(*s("floor"))
                    v.wait_ge(*d("floor", t))
                    v.tensor_tensor(fr, pp, fl, ALU.subtract).then_inc(*s("frac"))
                    v.wait_ge(*d("frac", t))
                    v.tensor_scalar(fr0, fr, -1.0, 1.0, ALU.mult, ALU.add).then_inc(*s("frac0"))
                if part == "corners":
                    w0, w1_ = wlin[:, 0:2 * GK], wlin[:, 2 * GK:4 * GK]
                    v.wait_ge(*d("frac0", t))
                    v.scalar_tensor_tensor(out=w0, in0=fl, scalar=0.0, in1=fr0, op0=ALU.is_ge, op1=ALU.mult)\
                        .then_inc(*s("in0"))
                    v.scalar_tensor_tensor(out=w1_, in0=fl, scalar=-1.0, in1=fr, op0=ALU.is_ge, op1=ALU.mult)\
                        .then_inc(*s("in1"))
                    v.wait_ge(*d("in0", t))
                    v.scalar_tensor_tensor(out=w0, in0=fl, scalar=float(W - 1), in1=w0,
                                           op0=ALU.is_le, op1=ALU.mult).then_inc(*s("w0"))
                    v.wait_ge(*d("in1", t))
                    v.scalar_tensor_tensor(out=w1_, in0=fl, scalar=float(W - 2), in1=w1_,
                                           op0=ALU.is_le, op1=ALU.mult).then_inc(*s("w1"))
                    v.wait_ge(*d("w1", t))
                    wl = wlin.rearrange("p (s a j) -> p s a j", s=2, a=2)
                    wy3 = wyw.rearrange("p (s j) -> p s j", s=2)
                    v.tensor_tensor(wy3, wl[:, :, 1, :], osb[:, 3 * GK:4 * GK].unsqueeze(1).to_broadcast([P, 2, GK]),
                                    ALU.mult).then_inc(*s("wy"))
                    v.wait_ge(*d("wy", t))
                    w4 = wq[:, bass.ds(t % SRING, 1), :].rearrange("p o f -> p (o f)")
                    v.tensor_tensor(w4.rearrange("p (j y x) -> p j y x", y=2, x=2),
                                    wyw.rearrange("p (y j) -> p j y", y=2).unsqueeze(3)
                                    .to_broadcast([P, GK, 2, 2]),
                                    wl[:, :, 0, :].rearrange("p x j -> p j x").unsqueeze(2)
                                    .to_broadcast([P, GK, 2, 2]), ALU.mult).then_inc(*s("wq"))
                    v.tensor_scalar(tmp, fl, -1.0, float(W - 1), ALU.max, ALU.min).then_inc(*s("flc"))
                    v.wait_ge(*d("flc", t))
                    v.scalar_tensor_tensor(out=fr0[:, 0:GK], in0=tmp[:, GK:2 * GK], scalar=float(W),
                                           in1=tmp[:, 0:GK], op0=ALU.mult, op1=ALU.add).then_inc(*s("lin"))
                    v.wait_ge(*d("lin", t))
                    bs = base[:, bass.ds(t // TB, 1), :].rearrange("p o g -> p (o g)")
                    rt = rank[:, bass.ds(t % SRING, 1), :].rearrange("p o j -> p (o j)")
                    v.tensor_tensor(rt.rearrange("p (g k) -> p g k", g=G),
                                    fr0[:, 0:GK].rearrange("p (g k) -> p g k", g=G),
                                    bs.unsqueeze(2).to_broadcast([P, G, K]), ALU.add).then_inc(*s("rank"))


            def dense(part, t, ks=(), before=None):
                d, s = dense_v.done, dense_v.step
                if part == "apart":
                    sp3 = spot[:, bass.ds(t % SRING, 1), 0:2, :].rearrange("p o a k -> p (o a) k")
                    v.wait_ge(*d("m8", t - 1))
                    v.tensor_tensor(tent[:, :, :, :].rearrange("p a k w -> p (a k) w"),
                                    iota[:, :].unsqueeze(1).to_broadcast([P, 2 * K, W]),
                                    sp3.rearrange("p a k -> p (a k)").unsqueeze(2).to_broadcast([P, 2 * K, W]),
                                    ALU.subtract).then_inc(*s("apart"))
                if part == "weigh":
                    v.wait_ge(*dense_s.done("tent", t))
                    wt = spot[:, bass.ds(t % SRING, 1), 2:3, :].rearrange("p o a k -> p (o a k)")
                    v.tensor_tensor(tent[:, 1, :, :], tent[:, 1, :, :],
                                    wt.unsqueeze(2).to_broadcast([P, K, W]), ALU.mult).then_inc(*s("weigh"))
                if part == "make":
                    for k in ks:
                        v.wait_ge(*(dense_t.done(f"k{k - MADE}", t) if k >= MADE else
                                    dense_t.done(f"k{k - MADE + K}", t - 1)))
                        if k == 0:
                            v.wait_ge(*d("weigh", t))
                        v.tensor_tensor(made[:, k % MADE, :].rearrange("p (y x) -> p y x", y=H),
                                        tent[:, 1, k, :].unsqueeze(2).to_broadcast([P, H, W]),
                                        tent[:, 0, k, :].unsqueeze(1).to_broadcast([P, H, W]), ALU.mult)\
                            .then_inc(*s(f"m{k}"))

            def measure(t0, t1, first):
                v.wait_ge(x_in[t0 // LEAD], 16)
                for t in range(t0, t1):
                    v.bn_stats(st_p[:, t, :], X[:, t, :]).then_inc(measured, 1)
                n = t1 - t0
                for t in range(t0, t1):
                    v.wait_ge(measured, first + t - t0 + 1)
                    v.bn_aggr(mv_p[:, t, :], st_p[:, t, :]).then_inc(measured, 1)
                v.wait_ge(measured, first + 2 * n)
                v.tensor_scalar(rs_p[:, t0:t1], mv_p[:, t0:t1, 1:2].rearrange("p t a -> p (t a)"), 1e-6, None,
                                ALU.add).then_inc(measured, 1)
                v.wait_ge(measured, first + 2 * n + 2)
                v.reciprocal(rs_p[:, t0:t1], rs_p[:, t0:t1]).then_inc(measured, 1)
                v.wait_ge(measured, first + 2 * n + 3)

            measure(0, LEAD, 0)
            v.wait_ge(first_in, 16 * 3)
            for t in range(LEAD):
                v.tensor_scalar(first_xn[:, t, :], X[:, t, :], mv_p[:, t, 0:1], rs_p[:, t:t + 1],
                                ALU.subtract, ALU.mult).then_inc(*first_v.step(f"xn{t}"))
            for t in range(LEAD):
                v.wait_ge(*first_t.done(f"vals{t}", 0))
                bank = ALL[t % len(ALL)]
                v.tensor_tensor(first_vs[:, t, :], bank[:, 0:VW], vb[:, :], ALU.add)\
                    .then_inc(*first_v.step(f"vals{t}"))
                v.tensor_tensor(v_dense[:, t, :], bank[:, DG * C:VW], vb[:, DG * C:VW], ALU.add)\
                    .then_inc(*first_v.step(f"dense{t}"))
            v.wait_ge(place_in, PLACE_CONSTS)
            v.tensor_tensor(ob[:, 0:2 * GK].rearrange("p (g k) -> p g k", g=G),
                            ob[:, 0:2 * GK].rearrange("p (g k) -> p g k", g=G),
                            pr[:, :].unsqueeze(1).to_broadcast([P, G, 2 * K]), ALU.add).then_inc(setup, 1)
            v.tensor_scalar(ob[:, 2 * GK:3 * GK].rearrange("p (g k) -> p g k", g=G),
                            sg[:, 0:G].unsqueeze(2).to_broadcast([P, G, K]), 1.0, None, ALU.mult)\
                .then_inc(setup, 1)
            v.wait_ge(setup, 2)
            for part in PLACES:
                places(part, 0)
            v.memset(KT[:, :, :], 0.0).then_inc(setup, 1)
            v.memset(ones[:, :], 1.0).then_inc(setup, 1)
            for n in range(2):
                v.memset(taken[n][:, :], 0.0).then_inc(setup, 1)
            measure(LEAD, NT, 2 * LEAD + 3)
            for part in PLACES:
                places(part, 1)
            dense("apart", 0)
            dense("weigh", 0)
            v.wait_ge(const_in, CONSTS)
            for h in range(NH - 1, -1, -1):
                v.wait_ge(setup, 6 + (NH - 1 - h))
                v.tensor_scalar(wp[:, h, :], wp[:, 0, :], heads[:, h:h + 1], None, ALU.mult).then_inc(setup, 1)
            v.wait_ge(rpb_in, 16 * BLK * BLK)
            bt = bias[:, :, :, :].rearrange("p t j k -> p (t j) k")
            v.tensor_tensor(bt, bt, prob[:, 0:1, :].to_broadcast([P, 9, KK]), ALU.add).then_inc(setup, 1)
            v.wait_ge(setup, 7 + NH)

            def conv(part, t, placed=None):
                d, s = conv_v.done, conv_v.step
                if isinstance(part, int):
                    q = part
                    if q == 0:
                        v.wait_ge(*place_v.done("wq", t))
                        v.wait_ge(*conv_t.done("T", t - 1))
                    g3 = got[:, q, :].rearrange("p (j c) -> p j c", c=C)
                    wj = wq[:, bass.ds(t % SRING, 1), q * QJ * CORNERS:(q + 1) * QJ * CORNERS]\
                        .rearrange("p o f -> p (o f)")
                    v.wait_ge(*got_q[q].through(t))
                    v.tensor_tensor(g3, g3, wj.unsqueeze(2).to_broadcast([P, QJ * CORNERS, C]), ALU.mult)\
                        .then_inc(*s(f"m{q}"))
                    v.wait_ge(*d(f"m{q}", t))
                    v.tensor_reduce(summed[:, q * C:(q + 1) * C],
                                    got[:, q, :].rearrange("p (j c) -> p c j", c=C), AX.X, ALU.add)\
                        .then_inc(*s(f"r{q}"))
                if part == "project":
                    xt = X[:, bass.ds(t, 1), :].rearrange("p o d -> p (o d)")
                    v.wait_ge(*conv_t.done("proj", t))
                    v.tensor_tensor(xt, CV[:, 256:384], xt, ALU.add).then_inc(*s("add"))

            def route(part, n, t, freed=None, after=None):
                d, s = route_v[n].done, route_v[n].step
                xt = X[:, bass.ds(t, 1), :].rearrange("p o d -> p (o d)")
                lg, eqd, hot, ps, kept, gate = (route_b[n][:, k, :] for k in range(6))
                if part == "stats":
                    v.wait_ge(*(conv_v, att_v)[n].all(t))
                    v.sem_inc(passed, 1)
                    v.bn_stats(st_m[:, :], xt).then_inc(*s("stats"))
                    v.wait_ge(*d("stats", t))
                    v.sem_inc(passed, 1)
                    v.bn_aggr(mv_m[:, :], st_m[:, :]).then_inc(*s("aggr"))
                    v.wait_ge(*d("aggr", t))
                    v.tensor_scalar(sd_m[:, 0:1], mv_m[:, 1:2], 1e-5, None, ALU.add).then_inc(*s("eps"))
                if part == "norm":
                    v.wait_ge(*route_s[n].done("std", t))
                    v.reciprocal(rs_m[:, :], sd_m[:, 1:2]).then_inc(*s("rstd"))
                    v.wait_ge(*d("rstd", t))
                    v.tensor_scalar(xn_m[n][:, :], xt, mv_m[:, 0:1], rs_m[:, 0:1], ALU.subtract, ALU.mult)\
                        .then_inc(*s("xn"))
                if part == "logits":
                    v.wait_ge(*route_t[n].done("lg", t))
                    v.tensor_tensor(lg, RB[n][:, 128:136], gb[n][:, :], ALU.add).then_inc(*s("lg"))
                    v.wait_ge(*d("lg", t))
                    v.tensor_reduce(small[n][:, 0:1], lg, AX.X, ALU.max).then_inc(*s("max"))
                    v.wait_ge(*d("max", t))
                    v.tensor_scalar(small[n][:, 1:2], small[n][:, 0:1], -1.0, None, ALU.mult).then_inc(*s("neg"))
                    v.scalar_tensor_tensor(out=eqd, in0=lg, scalar=small[n][:, 0:1], in1=dec[:, :],
                                           op0=ALU.is_equal, op1=ALU.mult).then_inc(*s("eqd"))
                    v.wait_ge(*d("eqd", t))
                    v.tensor_reduce(small[n][:, 2:3], eqd, AX.X, ALU.max).then_inc(*s("first"))
                    v.wait_ge(*d("first", t))
                    v.tensor_scalar(hot, eqd, small[n][:, 2:3], None, ALU.is_equal).then_inc(*s("hot"))
                if part == "gate":
                    v.wait_ge(*route_s[n].done("exp", t))
                    v.reciprocal(small[n][:, 4:5], small[n][:, 3:4]).then_inc(*s("rsum"))
                    v.wait_ge(*route_t[n].done("cum", t))
                    v.tensor_tensor(ps, RB[n][:, 136:144], taken[n][:, :], ALU.add).then_inc(*s("pos"))
                    v.wait_ge(*d("pos", t))
                    v.tensor_tensor(taken[n][:, :], RB[n][:, 144:152], taken[n][:, :], ALU.add)\
                        .then_inc(*s("taken"))
                    v.scalar_tensor_tensor(out=kept, in0=ps, scalar=float(CAPACITY), in1=hot,
                                           op0=ALU.is_le, op1=ALU.mult).then_inc(*s("kept"))
                    v.wait_ge(*d("kept", t))
                    v.tensor_scalar(gate, kept, small[n][:, 4:5], None, ALU.mult).then_inc(*s("gate"))

            def add_up(u, n, t, e0, e1):
                d, s = exp_v.done, exp_v.step
                gate = route_b[n][:, 5, :]
                v.wait_ge(*exp_t.done(f"y{e1 - 1}", u))
                for e in range(e0, e1):
                    so_far = acc
                    if e == 0:
                        v.wait_ge(*route_v[n].done("gate", t))
                        v.wait_ge(*route_s[n].done("b2", t))
                        v.wait_ge(*exp_v.all(u - 1))
                        so_far = share[n]
                    else:
                        v.wait_ge(*d(f"a{e - 1}", u))
                    v.scalar_tensor_tensor(out=acc[:, :], in0=Y[e // 4][:, (e % 4) * D:(e % 4 + 1) * D],
                                           scalar=gate[:, e:e + 1], in1=so_far[:, :],
                                           op0=ALU.mult, op1=ALU.add).then_inc(*s(f"a{e}"))

            def experts(u, n, t, beside):
                for e in range(E):
                    beside(e)
                    if e == 4:
                        add_up(u, n, t, 0, 4)

            def close(u, n, t):
                d, s = exp_v.done, exp_v.step
                xt = X[:, bass.ds(t, 1), :].rearrange("p o d -> p (o d)")
                add_up(u, n, t, 4, E)
                finite, clip, hi = (fin[:, k, :] for k in range(3))
                v.wait_ge(*d(f"a{E - 1}", u))
                v.tensor_scalar(finite, acc[:, :], 0.0, 0.0, ALU.mult, ALU.is_equal).then_inc(*s("fin"))
                v.tensor_scalar(clip, acc[:, :], -BIGGEST, BIGGEST, ALU.max, ALU.min).then_inc(*s("clip"))
                v.wait_ge(*d("clip", u))
                v.tensor_tensor(clip, clip, finite, ALU.mult).then_inc(*s("fpart"))
                v.tensor_scalar(hi, acc[:, :], BIGGEST, None, ALU.is_gt).then_inc(*s("hi"))
                v.wait_ge(*d("hi", u))
                v.scalar_tensor_tensor(out=hi, in0=acc[:, :], scalar=-BIGGEST, in1=hi,
                                       op0=ALU.is_lt, op1=ALU.subtract).then_inc(*s("sign"))
                v.tensor_tensor(xt, xt, clip, ALU.add).then_inc(*s("x1"))
                v.wait_ge(*d("x1", u))
                v.scalar_tensor_tensor(out=xt, in0=hi, scalar=-1e4, in1=xt,
                                       op0=ALU.mult, op1=ALU.add).then_inc(*s("x2"))

            def qkv(part, t, u=None, before=None):
                d, s = qkv_v.done, qkv_v.step
                xt = X[:, bass.ds(t, 1), :].rearrange("p o d -> p (o d)")
                if part == "stats":
                    v.wait_ge(*exp_v.all(u))
                    v.sem_inc(passed, 1)
                    v.bn_stats(st_q[:, :], xt).then_inc(*s("stats"))
                    v.wait_ge(*d("stats", t))
                    v.sem_inc(passed, 1)
                    v.bn_aggr(mv_q[:, :], st_q[:, :]).then_inc(*s("aggr"))
                    v.wait_ge(*d("aggr", t))
                    v.tensor_scalar(sd_q[:, 0:1], mv_q[:, 1:2], 1e-6, None, ALU.add).then_inc(*s("eps"))
                if part == "norm":
                    v.wait_ge(*qkv_s.done("std", t))
                    v.reciprocal(rs_q[:, :], sd_q[:, 1:2]).then_inc(*s("rstd"))
                    v.wait_ge(*d("rstd", t))
                    v.tensor_scalar(xn_q[:, :], xt, mv_q[:, 0:1], rs_q[:, 0:1], ALU.subtract, ALU.mult)\
                        .then_inc(*s("xn"))
                if part == "project":
                    r = t % QRING
                    v.wait_ge(*qkv_t.done("qkv", t))
                    v.tensor_scalar(QT[:, bass.ds(r, 1), :, :].rearrange("p o j (a c) -> p (o a) j c", a=BLK),
                                    M[:, 128:256].rearrange("p (a j c) -> p a j c", a=BLK, j=NB),
                                    bq[:, 0:1], HD ** -0.5, ALU.add, ALU.mult).then_inc(*s("q"))
                    kr = (t % TB) * TILE_ROWS + HALO
                    v.tensor_scalar(KT[:, bass.ds(kr, TILE_ROWS), HALO:HALO + W],
                                    M[:, 256:384].rearrange("p (a w) -> p a w", a=TILE_ROWS),
                                    bq[:, 1:2], None, ALU.add).then_inc(*s("k"))
                    v.wait_ge(*v_out.through(t - 1))
                    v.tensor_tensor(vt[:, :], M[:, 384:512], bv[:, :], ALU.add).then_inc(*s("v"))

            def attend(part, t, after=None, looked=None):
                d, s = att_v.done, att_v.step
                if part == "queries":
                    v.wait_ge(*att_t.done("s1", t - 1))
                    v.wait_ge(*dense_t.done("look", looked))
                    v.tensor_tensor(qbd, QT[:, bass.ds(t % QRING, 1), :, :].rearrange("p o j q -> p (o j) q")
                                    .unsqueeze(2).to_broadcast([P, NB, NH, BLK * BLK]),
                                    heads[:, :].unsqueeze(1).unsqueeze(3).to_broadcast([P, NB, NH, BLK * BLK]),
                                    ALU.mult).then_inc(*s("qbd"))
                if part == "scores":
                    row = (t % TB + (TB - 1)) // TB + (t % TB + 1) // TB
                    bt = bias[:, bass.ds(row, 1), :, :].rearrange("p o j k -> p (o j) k")
                    for k, blocks in enumerate((((0, 1, 0), (1, 4, 1)), ((4, 7, 1), (7, 8, 2)))):
                        v.wait_ge(*att_t.done(f"s{k}", t))
                        for j0, j1, kind in blocks:
                            a, b = (j0 % 4) * P, (j0 % 4 + j1 - j0) * P
                            ins = v.tensor_tensor(
                                prob[:, j0:j1, :],
                                N[k][:, a:b].rearrange("p (j k) -> p j k", k=P)[:, :, 0:KK],
                                bt[:, kind:kind + 1, :].to_broadcast([P, j1 - j0, KK]), ALU.add)
                        ins.then_inc(*s(f"s{k}"))
                    v.wait_ge(*d("s1", t))
                    v.tensor_reduce(soft[:, 0, :], prob, AX.X, ALU.max).then_inc(*s("max"))
                    v.wait_ge(*d("max", t))
                    v.tensor_scalar(soft[:, 1, :], soft[:, 0, :], -1.0, None, ALU.mult).then_inc(*s("neg"))
                if part == "weights":
                    v.wait_ge(*att_s.done("exp", t))
                    v.reciprocal(soft[:, 3, :], soft[:, 2, :]).then_inc(*s("rsum"))
                    v.wait_ge(*d("rsum", t))
                    v.tensor_tensor(prob, prob, soft[:, 3, :].unsqueeze(2).to_broadcast([P, NB, KK]), ALU.mult)\
                        .then_inc(*s("norm"))
                if part == "values":
                    v.wait_ge(*att_t.done("o", t))
                    v.tensor_copy(OT_of[:, :, 1, :], N[1][:, :].rearrange("p (g w) -> p g w", g=NH * BLK)).then_inc(*s("o1"))
                if part == "project":
                    xt = X[:, bass.ds(t, 1), :].rearrange("p o d -> p (o d)")
                    v.wait_ge(*att_t.done("proj", t))
                    v.tensor_tensor(xt, N[0][:, 0:D], xt, ALU.add).then_inc(*s("add"))

            slots(v, conv, route, experts, close, qkv, attend, values, places, dense)

        @block.scalar
        def _(a):
            for s in (first_s, place_s, dense_s, conv_s, *route_s, exp_s, qkv_s, att_s):
                s.begin(a)

            def values(part, t, before=None):
                if part == "turn":
                    a.wait_ge(*val_t.done("xT", t))
                    a.activation(xt_p, CV[:, 0:P], ACT.Copy).then_inc(*val_s.step("xT"))

            def places(part, t, before=None):
                s = place_s.step
                if part == "turn":
                    a.wait_ge(*place_t.done("xT", t))
                    a.activation(xt_o, CV[:, 384:512], ACT.Copy).then_inc(*s("xT"))
                if part == "offsets":
                    a.wait_ge(*place_v.done("offs", t))
                    a.activation(sg, osb[:, 2 * GK:3 * GK], ACT.Exp, scale=-1.0).then_inc(*s("exp"))

            def dense(part, t, ks=(), before=None):
                s = dense_s.step
                if part == "apart":
                    a.wait_ge(*dense_v.done("apart", t))
                    flat = tent[:, :, :, :].rearrange("p a k w -> p (a k w)")
                    a.activation(flat, flat, ACT.Abs).then_inc(*s("abs"))
                    a.wait_ge(*dense_s.done("abs", t))
                    a.activation(flat, flat, ACT.Relu, scale=-1.0, bias=1.0).then_inc(*s("tent"))
                if part == "copy":
                    for k in range(2):
                        a.wait_ge(*dense_t.done("k8", t))
                        a.wait_ge(*dense_t.done("look", t - 1))
                        a.activation(spread[:, 4 * k:4 * k + 4, :].rearrange("p c q -> p (c q)"), N[k][:, :],
                                     ACT.Copy).then_inc(*s(f"s{k}"))
                if part == "look":
                    a.wait_ge(*dense_t.done("look", t))
                    a.wait_ge(*conv_t.done("T", t - 1))
                    a.activation(summed[:, DG * C:VW], N[0][:, 0:C], ACT.Copy).then_inc(*s("out"))

            def measure(t0, t1, first):
                a.wait_ge(measured, first + 2 * (t1 - t0) + 1)
                a.activation(rs_p[:, t0:t1], rs_p[:, t0:t1], ACT.Sqrt).then_inc(measured, 1)

            measure(0, LEAD, 0)
            for t in range(LEAD):
                a.wait_ge(*first_t.done(f"xT{t}", 0))
                a.activation(first_xt[:, t, :], ALL[t % len(ALL)][:, 384:512], ACT.Copy)\
                    .then_inc(*first_s.step(f"xT{t}"))
            for part in PLACES:
                places(part, 0)
            measure(LEAD, NT, 2 * LEAD + 3)
            for part in PLACES:
                places(part, 1)
            dense("apart", 0)

            def conv(part, t, placed=None):
                if part == "turn":
                    a.wait_ge(*conv_t.done("T", t))
                    a.activation(summed_T[:, :, :].rearrange("p n q -> p (n q)"), CV[:, 0:256], ACT.Copy)\
                        .then_inc(*conv_s.step("T"))

            def route(part, n, t, freed=None, after=None):
                s = route_s[n].step
                if part == "stats":
                    a.wait_ge(*route_v[n].done("eps", t))
                    a.activation(sd_m[:, 1:2], sd_m[:, 0:1], ACT.Sqrt).then_inc(*s("std"))
                if part == "turn":
                    a.wait_ge(*route_t[n].done("xT", t))
                    a.wait_ge(*exp_t.done("z7", freed))
                    a.activation(xt_m[n][:, :], RB[n][:, 0:P], ACT.Copy).then_inc(*s("xT"))
                if part == "logits":
                    a.wait_ge(*route_v[n].done("neg", t))
                    a.activation(route_b[n][:, 6, :], route_b[n][:, 0, :], ACT.Exp, bias=small[n][:, 1:2],
                                 accum_out=small[n][:, 3:4]).then_inc(*s("exp"))
                if part == "gate_T":
                    a.wait_ge(*route_t[n].done("gT", t))
                    a.activation(gate_T[n][:, :], RB[n][0:E, 152:280], ACT.Copy).then_inc(*s("gT"))
                if part == "share":
                    a.wait_ge(*route_t[n].done("b2", t))
                    a.activation(share[n][:, :], RB[n][:, 280:408], ACT.Copy).then_inc(*s("b2"))

            def experts(u, n, t, beside):
                def relu(e):
                    a.wait_ge(*exp_t.done(f"z{e}", u))
                    a.wait_ge(*(exp_t.done(f"y{e - 2}", u) if e >= 2 else exp_t.done(f"y{e + 6}", u - 1)))
                    for c in range(FC):
                        ins = a.activation(hid[:, e % 2, c, :], Z[e % 2][:, c * P:(c + 1) * P], ACT.Relu,
                                           bias=b1[n][:, e * FC + c:e * FC + c + 1])
                    ins.then_inc(*exp_s.step(f"h{e}"))

                relu(0)
                for e in range(E):
                    if e + 1 < E:
                        relu(e + 1)
                    beside(e)

            def close(u, n, t):
                pass

            def qkv(part, t, u=None, before=None):
                s = qkv_s.step
                if part == "stats":
                    a.wait_ge(*qkv_v.done("eps", t))
                    a.activation(sd_q[:, 1:2], sd_q[:, 0:1], ACT.Sqrt).then_inc(*s("std"))
                if part == "turn":
                    a.wait_ge(*qkv_t.done("xT", t))
                    a.activation(xt_q[:, :], M[:, 0:P], ACT.Copy).then_inc(*s("xT"))

            def attend(part, t, after=None, looked=None):
                s = att_s.step
                if part == "scores":
                    a.wait_ge(*att_v.done("neg", t))
                    for j in range(NB):
                        ins = a.activation(prob[:, j, :], prob[:, j, :], ACT.Exp, bias=soft[:, 1, j:j + 1],
                                           accum_out=soft[:, 2, j:j + 1])
                    ins.then_inc(*s("exp"))
                if part == "turn":
                    for k in range(2):
                        a.wait_ge(*att_t.done(f"p{k}", t))
                        a.activation(PT[0:KK, 4 * k:4 * k + 4, :].rearrange("p j q -> p (j q)"), N[k][0:KK, :],
                                     ACT.Copy).then_inc(*s(f"p{k}"))
                if part == "values":
                    a.wait_ge(*att_t.done("o", t))
                    a.activation(OT_of[:, :, 0, :], N[0][:, :].rearrange("p (g w) -> p g w", g=NH * BLK), ACT.Copy)\
                        .then_inc(*s("o0"))

            slots(a, conv, route, experts, close, qkv, attend, values, places, dense)

        @block.tensor
        def _(pe):
            for s in (first_t, place_t, dense_t, conv_t, *route_t, exp_t, qkv_t, att_t):
                s.begin(pe)
            def values(part, t, before=None):
                s = val_t.step
                if part == "turn":
                    pe.wait_ge(*val_v.done("xn", t))
                    pe.wait_ge(*val_v.done("dense", t - 1))
                    if before is not None:
                        pe.wait_ge(*route_s[0].done("b2", before))
                    pe.transpose(CV[:, 0:P], xn_p, ident[:, :]).then_inc(*s("xT"))
                if part == "values":
                    pe.wait_ge(*val_s.done("xT", t))
                    pe.matmul(CV[:, P:P + VW], xt_p, wv[:, :], start=True, stop=True).then_inc(*s("vals"))

            def places(part, t, before=None):
                s = place_t.step
                if part == "turn":
                    pe.wait_ge(*place_v.done("xn", t))
                    pe.wait_ge(*val_v.done("dense", before[0]))
                    pe.wait_ge(*place_v.done("offs", t - 1))
                    pe.wait_ge(*route_s[0].done("b2", before[1]))
                    pe.transpose(CV[:, 384:512], xn_o, ident[:, :]).then_inc(*s("xT"))
                if part == "offsets":
                    pe.wait_ge(*place_s.done("xT", t))
                    pe.matmul(CV[:, 0:OFFW], xt_o, wo[:, :], start=True, stop=True).then_inc(*s("offs"))

            def dense(part, t, ks=(), before=None):
                s = dense_t.step
                if part == "sum":
                    for k in ks:
                        pe.wait_ge(*dense_v.done(f"m{k}", t))
                        if k == 0:
                            pe.wait_ge(*dense_s.done("out", t - 1))
                            if before is not None:
                                pe.wait_ge(*att_v.done("add", before))
                        for c in range(TB):
                            ins = pe.matmul(N[c // 4][:, (c % 4) * P:(c % 4 + 1) * P],
                                            made[:, k % MADE, c * P:(c + 1) * P], ident[:, :],
                                            start=(k == 0 and c % 4 == 0), stop=(k == K - 1 and c % 4 == 3))
                        ins.then_inc(*s(f"k{k}"))
                if part == "look":
                    pe.wait_ge(*dense_s.done("s1", t))
                    for c in range(TB):
                        ins = pe.matmul(N[0][:, 0:C], spread[:, c, :],
                                        v_dense[:, bass.ds(t // TB * TB + c, 1), :].rearrange("p o c -> p (o c)"),
                                        start=(c == 0), stop=(c == TB - 1))
                    ins.then_inc(*s("look"))

            pe.wait_ge(first_in, 16 * 3)
            for t in range(LEAD):
                pe.wait_ge(*first_v.done(f"xn{t}", 0))
                if t >= len(ALL):
                    pe.wait_ge(*first_s.done(f"xT{t - len(ALL)}", 0))
                pe.transpose(ALL[t % len(ALL)][:, 384:512], first_xn[:, t, :], ident[:, :])\
                    .then_inc(*first_t.step(f"xT{t}"))
            for t in range(LEAD):
                pe.wait_ge(*first_s.done(f"xT{t + len(ALL) if t + len(ALL) < LEAD else t}", 0))
                if t >= len(ALL):
                    pe.wait_ge(*first_v.done(f"dense{t - len(ALL)}", 0))
                pe.matmul(ALL[t % len(ALL)][:, 0:VW], first_xt[:, t, :], wv[:, :], start=True, stop=True)\
                    .then_inc(*first_t.step(f"vals{t}"))
            pe.wait_ge(place_in, PLACE_CONSTS)
            pe.wait_ge(*first_v.all(0))
            for t in range(PLEAD):
                for part in PLACES:
                    places(part, t, (LEAD - 1, -1))
            pe.wait_ge(setup, 7 + NH)

            def conv(part, t, placed=None):
                s = conv_t.step
                if part == "turn":
                    pe.wait_ge(*conv_v.done(f"r{NQ - 1}", t))
                    pe.wait_ge(*dense_s.done("out", t))
                    pe.wait_ge(*route_s[0].done("b2", t - 1))
                    pe.wait_ge(*place_v.done("offs", placed))
                    for n in range(2):
                        ins = pe.transpose(CV[:, n * P:(n + 1) * P], summed[:, n * P:(n + 1) * P], ident[:, :])
                    ins.then_inc(*s("T"))
                if part == "project":
                    pe.wait_ge(*conv_s.done("T", t))
                    pe.matmul(CV[:, 256:384], ones[0:1, :], rows[:, 0, :], start=True, stop=False)
                    pe.matmul(CV[:, 256:384], summed_T[:, 0, :], ow[:, 0, :], start=False, stop=False)
                    pe.matmul(CV[:, 256:384], summed_T[:, 1, :], ow[:, 1, :], start=False, stop=True)\
                        .then_inc(*s("proj"))

            def route(part, n, t, freed=None, after=None):
                s = route_t[n].step
                if part == "turn":
                    pe.wait_ge(*route_v[n].done("xn", t))
                    if n == 1:
                        pe.wait_ge(*route_s[n].done("b2", t - 1))
                        pe.wait_ge(*qkv_v.done("v", after))
                    pe.transpose(RB[n][:, 0:P], xn_m[n][:, :], ident[:, :]).then_inc(*s("xT"))
                if part == "logits":
                    pe.wait_ge(*route_s[n].done("xT", t))
                    pe.matmul(RB[n][:, 128:136], xt_m[n][:, :], gw[n][:, :], start=True, stop=True)\
                        .then_inc(*s("lg"))
                if part == "gate":
                    pe.wait_ge(*route_v[n].done("hot", t))
                    hot = route_b[n][:, 2, :]
                    pe.matmul(RB[n][:, 136:144], tri[:, :], hot, start=True, stop=True)
                    pe.matmul(RB[n][:, 144:152], ones[:, :], hot, start=True, stop=True).then_inc(*s("cum"))
                if part == "gate_T":
                    pe.wait_ge(*route_v[n].done("gate", t))
                    pe.matmul(RB[n][0:E, 152:280], route_b[n][:, 5, :], ident[:, :], start=True, stop=True)\
                        .then_inc(*s("gT"))
                if part == "share":
                    pe.wait_ge(*route_s[n].done("gT", t))
                    pe.matmul(RB[n][:, 280:408], gate_T[n][:, :], b2[n][:, :], start=True, stop=True)\
                        .then_inc(*s("b2"))

            def experts(u, n, t, beside):
                s = exp_t.step

                def up(e):
                    pe.wait_ge(*(exp_s.done(f"h{e - 2}", u) if e >= 2 else exp_s.done(f"h{e + 6}", u - 1)))
                    if e == 0:
                        pe.wait_ge(*route_s[n].done("xT", t))
                    for c in range(FC):
                        ins = pe.matmul(Z[e % 2][:, c * P:(c + 1) * P], w1[n][:, e, c * P:(c + 1) * P],
                                        xt_m[n][:, :], start=True, stop=True)
                    ins.then_inc(*s(f"z{e}"))

                def down(e):
                    pe.wait_ge(*exp_s.done(f"h{e}", u))
                    if e % 4 == 0:
                        pe.wait_ge(*exp_v.done(f"a{e + 3}", u - 1))
                    for c in range(FC):
                        ins = pe.matmul(Y[e // 4][:, (e % 4) * D:(e % 4 + 1) * D], hid[:, e % 2, c, :],
                                        w2[n][:, e * FC + c, :], start=(c == 0), stop=(c == FC - 1))
                    ins.then_inc(*s(f"y{e}"))

                up(0)
                for e in range(E):
                    if e + 1 < E:
                        up(e + 1)
                    down(e)
                    beside(e)

            def close(u, n, t):
                pass

            def qkv(part, t, u=None, before=None):
                s = qkv_t.step
                if part == "turn":
                    pe.wait_ge(*qkv_v.done("xn", t))
                    pe.wait_ge(*route_s[1].done("b2", t - 2 if before is None else before))
                    pe.transpose(M[:, 0:P], xn_q[:, :], ident[:, :]).then_inc(*s("xT"))
                if part == "project":
                    pe.wait_ge(*qkv_s.done("xT", t))
                    for n in range(2):
                        pe.matmul(M[:, (n + 1) * P:(n + 2) * P], wqkv[:, n * D:(n + 1) * D], xt_q[:, :],
                                  start=True, stop=True)
                    pe.matmul(M[:, 384:512], xt_q[:, :], wqkv[:, 2 * D:3 * D], start=True, stop=True)\
                        .then_inc(*s("qkv"))

            def attend(part, t, after=None, looked=None):
                s = att_t.step
                if part == "queries":
                    kr = (t % TB) * TILE_ROWS
                    pe.wait_ge(*att_v.done("qbd", t))
                    pe.wait_ge(*qkv_v.done("k", after))
                    pe.wait_ge(*att_v.done("add", t - 1))
                    pe.wait_ge(*dense_s.done("out", looked))
                    for j in range(NB):
                        ins = pe.matmul(N[j // 4][:, (j % 4) * P:(j % 4) * P + KK],
                                        qbd[:, j, :, :].rearrange("p h q -> p (h q)"),
                                        KT[:, bass.ds(kr, KW), j * BLK:j * BLK + KW], start=True, stop=True)
                        if j % 4 == 3:
                            ins.then_inc(*s(f"s{j // 4}"))
                if part == "turn":
                    pe.wait_ge(*att_v.done("norm", t))
                    for j in range(NB):
                        ins = pe.transpose(N[j // 4][0:KK, (j % 4) * P:(j % 4 + 1) * P], prob[:, j, :],
                                           ident[:, :])
                        if j % 4 == 3:
                            ins.then_inc(*s(f"p{j // 4}"))
                if part == "values":
                    pe.wait_ge(*att_s.done("p1", t))
                    pe.wait_ge(*v_in.through(t))
                    for j in range(NB):
                        o = N[j // 4][:, :].rearrange("p (h a w) -> p h a w", h=NH, a=BLK)
                        ins = pe.matmul(o[:, :, :, (j % 4) * BLK:(j % 4 + 1) * BLK], vwin[0:KK, j, :],
                                        PT[0:KK, j, :], start=True, stop=True)
                    ins.then_inc(*s("o"))
                if part == "project":
                    pe.wait_ge(*att_v.done("o1", t))
                    pe.wait_ge(*att_s.done("o0", t))
                    pe.matmul(N[0][:, 0:D], ones[0:1, :], rows[:, 1, :], start=True, stop=False)
                    for h in range(NH):
                        ins = pe.matmul(N[0][:, 0:D], OT[:, h, :], wp[:, h, :], start=False, stop=(h == NH - 1))
                    ins.then_inc(*s("proj"))

            slots(pe, conv, route, experts, close, qkv, attend, values, places, dense)


def constants():
    p = np.arange(P)
    t = np.arange(NT)
    f = np.float32
    pos = np.zeros((P, NT, 2), f)
    pos[:, :, 0] = (p % W)[:, None]
    pos[:, :, 1] = (p // W)[:, None] + (t % TB)[None, :] * TILE_ROWS
    base = np.broadcast_to(np.arange(B * G).reshape(B, G) * PATCHES + PADM, (P, B, G)).astype(f)
    q = p % (BLK * BLK)
    a = np.arange(KW)
    ok = []
    for at, blocks in ((q // BLK, (0, 1, TB - 1)), (q % BLK, (0, 1, NB - 1))):
        first = np.array([4 * k for k in blocks])
        key = first[None, :, None] - HALO + a[None, None, :]
        start = np.clip(first[None, :] + at[:, None] - HALO, 0, H - WIN)
        ok.append((key >= start[:, :, None]) & (key < start[:, :, None] + WIN))
    mask = ok[0][:, :, None, :, None] & ok[1][:, None, :, None, :]
    return {
        "c_ident": np.eye(P, dtype=f), "c_tri": np.triu(np.ones((P, P), f)), "c_pos": pos, "c_base": base,
        "c_iota": np.broadcast_to(np.arange(W), (P, W)).astype(f),
        "c_heads": (p[:, None] // HD == np.arange(NH)[None, :]).astype(f),
        "c_dec": np.broadcast_to(np.arange(E, 0, -1).astype(f), (P, E)).copy(),
        "c_mask": np.where(mask, f(0), f(-1e30)).astype(f).reshape(P, 3, 3, KK),
    }


CONV = ["v_w", "v_b", "qd_w", "qd_b", "qs_w", "qw_w", "qw_b", "out_w", "out_b", "prior", "dscale"]
MOE = ["gate_w", "gate_b", "w1", "b1", "w2", "b2"]
ATT = ["Wqkv", "bqkv", "rpb", "Wproj", "bproj"]


def program(nc, aps, out):
    build(nc, aps["x"], *[aps[f"L0_conv_{n}"] for n in CONV],
          [[aps[f"L{k}_ffn_{n}"] for n in MOE] for k in range(2)],
          *[aps[f"L1_conv_{n}"] for n in ATT],
          *[aps[n] for n in ("c_ident", "c_tri", "c_iota", "c_pos", "c_base", "c_heads", "c_dec", "c_mask")], out)


def kernel(**inputs):
    import concourse.bacc as bacc
    from concourse.bass_utils import run_bass_kernel_spmd

    nc = bacc.Bacc("TRN2", target_bir_lowering=False, num_devices=1)
    arrays, aps = {}, {}
    for name, a in {**{k: np.asarray(v) for k, v in inputs.items()}, **constants()}.items():
        a = np.ascontiguousarray(a)
        arrays[f"in_{name}"] = a
        aps[name] = nc.dram_tensor(f"in_{name}", a.shape, mybir.dt.from_np(a.dtype), kind="ExternalInput").ap()
    out = nc.dram_tensor("out_0", (B, H, W, D), F32, kind="ExternalOutput").ap()
    program(nc, aps, out)
    r = run_bass_kernel_spmd(nc, [arrays], core_ids=[0])
    return r.results[0]["out_0"]
```
